# Optimizing a Trainium2 kernel written in Bass

```python
import numpy as np
import jax
import jax.numpy as jnp

def _softmax(x, axis=-1):
    return jax.nn.softmax(x, axis=axis)

def _gelu(x):
    return jax.nn.gelu(x, approximate=True)

def _silu(x):
    return jax.nn.silu(x)

def _sigmoid(x):
    return jax.nn.sigmoid(x)

def _layernorm(x, axis=-1, eps=1e-05):
    m = jnp.mean(x, axis=axis, keepdims=True)
    v = jnp.var(x, axis=axis, keepdims=True)
    return (x - m) / jnp.sqrt(v + eps)

def _scatter_add(tgt, idx, src, axis=0):
    return tgt.at[idx].add(src)

def _segment_sum(src, seg, n):
    return jax.ops.segment_sum(src, seg, n)
kernel_name = 'mk_gnn_resnorm_d2_gnn_r32_81ebd7'

def setup_inputs(seed: int=0):
    np.random.seed(seed)
    _w = jnp.asarray

    def _rec_inputs():
        import jax
        import jax.numpy as jnp
        _gk = jax.random.key(seed)
        x = -0.0002117 + 1 * jax.random.normal(jax.random.fold_in(_gk, 1), (3125, 256), jnp.float32)
        _s = jax.random.randint(jax.random.fold_in(_gk, 2), (25000,), 0, 3125, jnp.int32)
        _d = jax.random.randint(jax.random.fold_in(_gk, 3), (25000,), 0, 3125, jnp.int32)
        _loop = jnp.arange(3125, dtype=jnp.int32)
        src = jnp.concatenate([_s, _d, _loop])
        dst = jnp.concatenate([_d, _s, _loop])
        _o = jnp.argsort(dst, stable=True)
        src = src[_o]
        dst = dst[_o]
        edge_attr_64 = 0.000279952 + 1.00013 * jax.random.normal(jax.random.fold_in(_gk, 12), (53125, 64), jnp.float32)
        edge_weight = jax.random.uniform(jax.random.fold_in(_gk, 14), (53125,), jnp.float32, 0.0, 0.03125)
        return (x, src, dst, edge_attr_64, edge_weight)
    x, src, dst, edge_attr_64, edge_weight = _rec_inputs()

    def _L0_gnn_setup():
        import jax, jax.numpy as jnp
        import numpy as np
        N_NODES = 3125
        N_EDGES = 100000
        DIM = 256
        LEAKY_SLOPE = 0.2
        EPS = 1e-12
        key = jax.random.key(seed)
        ks = jax.random.split(key, 8)
        embeddings = jax.random.normal(ks[0], (N_NODES, DIM), dtype=jnp.float32)
        edge_src = jax.random.randint(ks[1], (N_EDGES,), 0, N_NODES, dtype=jnp.int32)
        edge_dst = jax.random.randint(ks[2], (N_EDGES,), 0, N_NODES, dtype=jnp.int32)
        edge_val = jax.random.uniform(ks[3], (N_EDGES,), dtype=jnp.float32) / 32.0
        scale = 1.0 / np.sqrt(DIM)
        W1 = jax.random.normal(ks[4], (DIM, DIM), dtype=jnp.float32) * scale
        b1 = jax.random.normal(ks[5], (DIM,), dtype=jnp.float32) * 0.01
        W2 = jax.random.normal(ks[6], (DIM, DIM), dtype=jnp.float32) * scale
        b2 = jax.random.normal(ks[7], (DIM,), dtype=jnp.float32) * 0.01
        return {'embeddings': embeddings, 'edge_src': edge_src, 'edge_dst': edge_dst, 'edge_val': edge_val, 'W1': W1, 'b1': b1, 'W2': W2, 'b2': b2}
    _L0_gnn_all = _L0_gnn_setup()
    _L0_gnn_in = {k: v for k, v in _L0_gnn_all.items() if k in ('W1', 'b1', 'W2', 'b2')}
    del _L0_gnn_all

    def _L1_gnn_setup():
        import jax, jax.numpy as jnp
        import numpy as np
        N = 3125
        E = 10000
        CIN = 256
        EDIM = 64
        EEMB = 256
        H = 1024
        LN_EPS = 1e-05

        def _ln(x, g, b):
            m = jnp.mean(x, axis=-1, keepdims=True)
            v = jnp.var(x, axis=-1, keepdims=True)
            return (x - m) * jax.lax.rsqrt(v + LN_EPS) * g + b
        key = jax.random.key(seed)
        ks = jax.random.split(key, 16)

        def w(k, i, o):
            return (jax.random.normal(k, (i, o), jnp.float32) / np.sqrt(i)).astype(jnp.float32)
        return {'x': jax.random.normal(ks[0], (N, CIN), jnp.float32), 'edge_index': jax.random.randint(ks[1], (2, E), 0, N, dtype=jnp.int64), 'edge_attr': jax.random.normal(ks[2], (E, EDIM), jnp.float32), 'eps': jnp.float32(0.0), 'ee_w1': w(ks[3], EDIM, EEMB), 'ee_b1': jnp.zeros((EEMB,), jnp.float32), 'ee_w2': w(ks[4], EEMB, CIN), 'ee_b2': jnp.zeros((CIN,), jnp.float32), 'w1': w(ks[5], CIN, H), 'b1': jnp.zeros((H,), jnp.float32), 'g1': jnp.ones((H,), jnp.float32), 'be1': jnp.zeros((H,), jnp.float32), 'w2': w(ks[6], H, H), 'b2': jnp.zeros((H,), jnp.float32), 'g2': jnp.ones((H,), jnp.float32), 'be2': jnp.zeros((H,), jnp.float32), 'w3': w(ks[7], H, CIN), 'b3': jnp.zeros((CIN,), jnp.float32), 'bn_g': jnp.ones((CIN,), jnp.float32), 'bn_b': jnp.zeros((CIN,), jnp.float32)}
    _L1_gnn_all = _L1_gnn_setup()
    _L1_gnn_in = {k: v for k, v in _L1_gnn_all.items() if k in ('eps', 'ee_w1', 'ee_b1', 'ee_w2', 'ee_b2', 'w1', 'b1', 'g1', 'be1', 'w2', 'b2', 'g2', 'be2', 'w3', 'b3', 'bn_g', 'bn_b')}
    del _L1_gnn_all
    return {'x': x, 'src': src, 'dst': dst, 'edge_attr_64': edge_attr_64, 'edge_weight': edge_weight, 'L0_gnn_W1': _L0_gnn_in['W1'], 'L0_gnn_b1': _L0_gnn_in['b1'], 'L0_gnn_W2': _L0_gnn_in['W2'], 'L0_gnn_b2': _L0_gnn_in['b2'], 'L1_gnn_eps': _L1_gnn_in['eps'], 'L1_gnn_ee_w1': _L1_gnn_in['ee_w1'], 'L1_gnn_ee_b1': _L1_gnn_in['ee_b1'], 'L1_gnn_ee_w2': _L1_gnn_in['ee_w2'], 'L1_gnn_ee_b2': _L1_gnn_in['ee_b2'], 'L1_gnn_w1': _L1_gnn_in['w1'], 'L1_gnn_b1': _L1_gnn_in['b1'], 'L1_gnn_g1': _L1_gnn_in['g1'], 'L1_gnn_be1': _L1_gnn_in['be1'], 'L1_gnn_w2': _L1_gnn_in['w2'], 'L1_gnn_b2': _L1_gnn_in['b2'], 'L1_gnn_g2': _L1_gnn_in['g2'], 'L1_gnn_be2': _L1_gnn_in['be2'], 'L1_gnn_w3': _L1_gnn_in['w3'], 'L1_gnn_b3': _L1_gnn_in['b3'], 'L1_gnn_bn_g': _L1_gnn_in['bn_g'], 'L1_gnn_bn_b': _L1_gnn_in['bn_b']}

def reference(x, src, dst, edge_attr_64, edge_weight, L0_gnn_W1, L0_gnn_b1, L0_gnn_W2, L0_gnn_b2, L1_gnn_eps, L1_gnn_ee_w1, L1_gnn_ee_b1, L1_gnn_ee_w2, L1_gnn_ee_b2, L1_gnn_w1, L1_gnn_b1, L1_gnn_g1, L1_gnn_be1, L1_gnn_w2, L1_gnn_b2, L1_gnn_g2, L1_gnn_be2, L1_gnn_w3, L1_gnn_b3, L1_gnn_bn_g, L1_gnn_bn_b):
    import jax
    import jax.numpy as jnp

    def _L0_gnn_ref(embeddings, edge_src, edge_dst, edge_val, W1, b1, W2, b2):
        import jax, jax.numpy as jnp
        import numpy as np
        N_NODES = 3125
        N_EDGES = 100000
        DIM = 256
        LEAKY_SLOPE = 0.2
        EPS = 1e-12
        ego_emb = embeddings @ W1.T + b1
        messages = edge_val[:, None] * embeddings[edge_src]
        neighbor_emb = jax.ops.segment_sum(messages, edge_dst, num_segments=embeddings.shape[0])
        interaction_emb = neighbor_emb * embeddings
        side_emb = (neighbor_emb + interaction_emb) @ W2.T + b2
        out = ego_emb + side_emb
        out = jnp.where(out >= 0, out, LEAKY_SLOPE * out)
        norm = jnp.sqrt(jnp.sum(out * out, axis=1, keepdims=True))
        return out / jnp.maximum(norm, EPS)

    def _L1_gnn_ref(x, edge_index, edge_attr, eps, ee_w1, ee_b1, ee_w2, ee_b2, w1, b1, g1, be1, w2, b2, g2, be2, w3, b3, bn_g, bn_b):
        import jax, jax.numpy as jnp
        import numpy as np
        N = 3125
        E = 10000
        CIN = 256
        EDIM = 64
        EEMB = 256
        H = 1024
        LN_EPS = 1e-05

        def _ln(x, g, b):
            m = jnp.mean(x, axis=-1, keepdims=True)
            v = jnp.var(x, axis=-1, keepdims=True)
            return (x - m) * jax.lax.rsqrt(v + LN_EPS) * g + b
        n = x.shape[0]
        sl = jnp.arange(n, dtype=edge_index.dtype)
        ei = jnp.concatenate([edge_index, jnp.stack([sl, sl], axis=0)], axis=1)
        ea = jnp.concatenate([edge_attr, jnp.zeros((n, edge_attr.shape[1]), edge_attr.dtype)], axis=0)
        src, dst = (ei[0], ei[1])
        e = jax.nn.relu(ea @ ee_w1 + ee_b1) @ ee_w2 + ee_b2
        msg = x[src] + e
        agg = jax.ops.segment_sum(msg, dst, num_segments=n)
        h = (1.0 + eps) * x + agg
        h = jax.nn.relu(_ln(h @ w1 + b1, g1, be1))
        h = jax.nn.relu(_ln(h @ w2 + b2, g2, be2))
        y = h @ w3 + b3
        out = x + y
        out = _ln(out, bn_g, bn_b)
        return jax.nn.relu(out)
    edge_index = jnp.stack([src, dst])
    x = _layernorm(x + _L0_gnn_ref(x, src, dst, edge_weight, L0_gnn_W1, L0_gnn_b1, L0_gnn_W2, L0_gnn_b2), axis=-1)
    x = _layernorm(x + _L1_gnn_ref(x, edge_index, edge_attr_64, L1_gnn_eps, L1_gnn_ee_w1, L1_gnn_ee_b1, L1_gnn_ee_w2, L1_gnn_ee_b2, L1_gnn_w1, L1_gnn_b1, L1_gnn_g1, L1_gnn_be1, L1_gnn_w2, L1_gnn_b2, L1_gnn_g2, L1_gnn_be2, L1_gnn_w3, L1_gnn_b3, L1_gnn_bn_g, L1_gnn_bn_b), axis=-1)
    return x

_drawn_inputs = setup_inputs


def setup_inputs(seed=0):
    import zlib

    import numpy as np

    out = dict(_drawn_inputs(seed))
    spreads = {'L1_gnn_ee_b1': (0.0, 0.281),
     'L1_gnn_ee_b2': (0.0, 0.1),
     'L1_gnn_b1': (0.0, 2.0),
     'L1_gnn_g1': (1.0, 0.2),
     'L1_gnn_be1': (0.0, 0.332),
     'L1_gnn_b2': (0.0, 0.1),
     'L1_gnn_g2': (1.0, 0.2),
     'L1_gnn_be2': (0.0, 0.301),
     'L1_gnn_b3': (0.0, 0.1),
     'L1_gnn_bn_g': (1.0, 0.2),
     'L1_gnn_bn_b': (0.0, 0.1)}
    factors = {'edge_weight': 8.0,
     'L0_gnn_b1': 64.0,
     'L0_gnn_W2': 8.0,
     'L0_gnn_b2': 64.0,
     'L0_gnn_W1': 5.928}
    for name, (base, spread) in spreads.items():
        noise = np.random.default_rng([zlib.crc32(name.encode()), seed]).standard_normal(out[name].shape)
        drawn = base * np.exp(spread * noise) if base else spread * noise
        out[name] = jnp.asarray(drawn.astype(out[name].dtype))
    for name, factor in factors.items():
        out[name] = (out[name] * factor).astype(out[name].dtype)
    return out
```

```python
from contextlib import ExitStack

import concourse.bass as bass
from concourse import mybir

F32 = mybir.dt.float32
F32R = mybir.dt.float32r
I32 = mybir.dt.int32
ALU = mybir.AluOpType
ACT = mybir.ActivationFunctionType
AX_X = mybir.AxisListType.X

N, E, D, ED, H = 3125, 53125, 256, 64, 1024
P = 125
BLOCKS = N // P
TILES = E // P // BLOCKS
EDGE = 4
PAIRS = [(0, 2), (2, 2), (4, 2), (6, 2), (8, 2), (10, 2), (12, 2), (14, 2), (16, 1)]
NP = len(PAIRS)
LEAD = 3
CHUNKS = [(0, 6), (6, 6), (12, 5)]
KD = D // 128
KH = H // 128
LN_EPS = 1e-5
NORM_EPS = 1e-12
SLOPE = 0.2
SUMS = 10

NEAR_STEPS = [(-1, TILES - EDGE, EDGE), (0, 0, EDGE)] + [(0, j, m) for j, m in PAIRS[2:]] + [(1, 0, EDGE)]
OH_AT = [0]
for _, _, _m in NEAR_STEPS:
    OH_AT.append(OH_AT[-1] + _m)
OH_SLOTS = OH_AT[-1]


def wait(eng, sem, value):
    if isinstance(value, int) and value <= 0:
        return
    eng.wait_ge(sem, value)


class Near:

    @staticmethod
    def slot_free(q, k):
        if isinstance(q, int) and q == 0:
            return 0
        if k < 2:
            return SUMS * (q - 1) + 2
        if k < 6:
            return SUMS * (q - 1) + k + 1
        return SUMS * q + 1

    @staticmethod
    def t2_before_t1(b):
        return b - 1

    @staticmethod
    def t1_before_t2(b):
        return min(b + 2, BLOCKS) if isinstance(b, int) else b + 2


class General:

    @staticmethod
    def slot_free(q, k):
        return NP * q + k + 1

    @staticmethod
    def t2_before_t1(b):
        return b

    @staticmethod
    def t1_before_t2(b):
        return b + 1


def near_sum_steps(b):
    first = 1 if isinstance(b, int) and b == 0 else 0
    last = SUMS - 1 if isinstance(b, int) and b == BLOCKS - 1 else SUMS
    return [c for c in range(first, last)]


def near_inc(b, c):
    if isinstance(b, int) and b == 0 and c == 1:
        return 2
    if isinstance(b, int) and b == BLOCKS - 1 and c == SUMS - 2:
        return 2
    return 1


def gnn_program(nc, x, xT, src, dst, weight, attrT, w1T, w2T, bias01, bias02, eps_in, ee_w1, ee_b1row, ee_b1,
                ee_w2, ee_b2, m_w1, m_b1, m_g1, m_be1, m_w2, m_b2, m_g2, m_be2, m_w3, m_b3, bn_g, bn_b,
                ident_in, out):
    x1_dram = nc.dram_tensor("x1_dram", (N, D), F32).ap()
    hbase_dram = nc.dram_tensor("hbase_dram", (N, D), F32).ap()
    table_dram = nc.dram_tensor("table_dram", (N, 2 * D), F32).ap()

    with ExitStack() as keep:
        def sb(name, shape, dt, ctx=keep):
            return ctx.enter_context(nc.sbuf_tensor(name, shape, dt))

        def psum(name, shape, ctx):
            return ctx.enter_context(nc.psum_tensor(name, shape, F32))

        def sem(name, ctx=keep):
            return ctx.enter_context(nc.semaphore(name))

        dst_f = sb("dst_f", [P, BLOCKS, TILES], F32)
        rel = sb("rel", [P, BLOCKS, TILES], F32)
        lane = sb("lane", [P, 3 * P], F32)
        flag = sb("flag", [1, 1], I32)
        ident = sb("ident", [P, P], F32)

        eps_t = sb("eps_t", [P, 1], F32)
        ln_eps = sb("ln_eps", [P, 1], F32)

        with ExitStack() as ca:
            def sa(name, shape, dt):
                return sb(name, shape, dt, ca)

            def ma(name):
                return sem(name, ca)

            dst_i = sa("dst_i", [P, BLOCKS, TILES], I32)
            w_sb = sa("w_sb", [P, BLOCKS * TILES], F32)
            idx = sa("idx", [P, TILES], I32)
            attr = sa("attr", [ED + 1, TILES * P], F32)
            raw = sa("raw", [P, TILES, D], F32)
            msg = sa("msg", [P, TILES, 2, 2 * D], F32R)
            oh = sa("oh", [P, OH_SLOTS, P], F32R)
            bad = sa("bad", [P, BLOCKS, TILES], F32)
            bad_sum = sa("bad_sum", [P, 1], F32)
            ones_c = sa("ones_c", [P, 1], F32)
            zero_oh = sa("zero_oh", [P, P], F32)
            w1T_sb = sa("w1T_sb", [128, KD, D], F32)
            w2T_sb = sa("w2T_sb", [128, KD, D], F32)
            we1 = sa("we1", [ED + 1, D], F32)
            we2 = sa("we2", [128, KD, D], F32)
            b01 = sa("b01", [P, D], F32)
            b02 = sa("b02", [P, D], F32)
            b12 = sa("b12", [P, D], F32)
            eb1 = sa("eb1", [P, D], F32)
            r0 = sa("r0", [P, D], F32)
            eb2 = sa("eb2", [P, D], F32)
            eps_raw = sa("eps_raw", [P, 1], F32)
            xs = sa("xs", [P, D], F32)
            xr = sa("xr", [P, D], F32)
            xTb = sa("xTb", [128, KD, P], F32)
            s_r = sa("s_r", [P, 2 * D], F32)
            sT = sa("sT", [128, 4 * P], F32)
            o = sa("o", [P, D], F32)
            o2 = sa("o2", [P, D], F32)
            sq = sa("sq", [P, D], F32)
            st = sa("st", [P, 8], F32)
            bn6 = sa("bn6", [P, 6], F32)
            y = sa("y", [P, D], F32)
            x1 = sa("x1", [P, D], F32)
            tb = sa("tb", [P, D], F32)
            table = sa("table", [P, 2, D], F32R)
            hb = sa("hb", [P, D], F32)

            ps_sum = psum("ps_sum", [P, 512], ca)
            ps_e = [psum(f"ps_e{n}", [P, 512], ca) for n in range(3)]
            ps_t = psum("ps_t", [128, 512], ca)
            ps_d = psum("ps_d", [P, 512], ca)

            consts = ma("consts")
            edges_in = ma("edges_in")
            idx_in = [ma(f"idx_in{c}") for c in range(3)]
            attr_in = [ma(f"attr_in{c}") for c in range(3)]
            gathered = [ma(f"gathered{j}") for j in range(TILES)]
            xs_in, xr_in, xT_in = ma("xs_in"), ma("xr_in"), ma("xT_in")

            pool_ready = ma("pool_ready")
            prep = ma("prep")
            bad_ready, bad_total, flag_ready = ma("bad_ready"), ma("bad_total"), ma("flag_ready")
            rel_ready = ma("rel_ready")
            edge_net = ma("edge_net")
            high = ma("high")
            message = ma("message")
            oh_ready = ma("oh_ready")
            summed = ma("summed")

            s_ready = ma("s_ready")
            s_turned = ma("s_turned")
            sT_ready = ma("sT_ready")
            dense = ma("dense")
            dd = ma("dd")
            da = ma("da")
            stored = ma("stored")

            DD = 14
            DA = 3

            N_CONST = 16 * 14

            def tile_cols(n, j, m=1):
                return bass.ds(n * TILES + j, m)

            def rows(ap, b):
                return ap[bass.ds(b * P, P), :]

            block = ca.enter_context(nc.Block())

            @block.sync
            def _(sp):
                sp.dma_start(dst_i[:, :, :].rearrange("p b j -> p (b j)"), dst).then_inc(edges_in, 16)
                sp.dma_start(w_sb[:, :], weight).then_inc(edges_in, 16)
                sp.dma_start(we1[0:ED, :], ee_w1).then_inc(consts, 16)
                sp.dma_start(we1[ED:ED + 1, :], ee_b1row).then_inc(consts, 16)
                sp.dma_start(ident[:, :], ident_in).then_inc(consts, 16)
                sp.dma_start(b01[:, :], bias01).then_inc(consts, 16)
                sp.dma_start(b02[:, :], bias02).then_inc(consts, 16)
                sp.dma_start(eb1[:, :], ee_b1).then_inc(consts, 16)
                sp.dma_start(eb2[:, :], ee_b2).then_inc(consts, 16)
                sp.dma_start(eps_raw[:, :], eps_in).then_inc(consts, 16)
                for k in range(KD):
                    sp.dma_start(w1T_sb[:, k, :], w1T[k * 128:(k + 1) * 128, :]).then_inc(consts, 16)
                    sp.dma_start(w2T_sb[:, k, :], w2T[k * 128:(k + 1) * 128, :]).then_inc(consts, 16)
                    sp.dma_start(we2[:, k, :], ee_w2[k * 128:(k + 1) * 128, :]).then_inc(consts, 16)

                def load_span(q, n, start=0):
                    for c, (j, m) in enumerate(CHUNKS):
                        wait(sp, message, start + NP * (q - 1) + 3 * c + 3)
                        sp.nop(nofuse=True)
                        sp.dma_start(idx[:, j:j + m], src[:, tile_cols(n, j, m)]).then_inc(idx_in[c], 16)
                        sp.dma_start(attr[0:ED, j * P:(j + m) * P],
                                     attrT[:, bass.ds((n * TILES + j) * P, m * P)]).then_inc(attr_in[c], 16)

                def load_xs(b):
                    wait(sp, s_ready, b)
                    sp.nop(nofuse=True)
                    sp.dma_start(xs[:, :], rows(x, b)).then_inc(xs_in, 16)

                def load_x(b):
                    wait(sp, dd, DD * b)
                    sp.nop(nofuse=True)
                    sp.dma_start(xr[:, :], rows(x, b)).then_inc(xr_in, 16)
                    wait(sp, dense, b)
                    sp.nop(nofuse=True)
                    sp.dma_start(xTb[:, :, :], xT[:, :, bass.ds(b * P, P)]).then_inc(xT_in, 16)

                def store(b):
                    sp.wait_ge(dd, DD * (b + 1))
                    sp.nop(nofuse=True)
                    sp.dma_start(rows(x1_dram, b), x1[:, :]).then_inc(stored, 16)
                    sp.dma_start(rows(table_dram, b), table[:, :, :].rearrange("p a d -> p (a d)").bitcast(F32))\
                      .then_inc(stored, 16)
                    sp.dma_start(rows(hbase_dram, b), hb[:, :]).then_inc(stored, 16)

                sp.wait_ge(flag_ready, 1)
                near = sp.value_load(flag[0:1, 0:1])
                with sp.If(near == 1):
                    load_span(0, 0)
                    load_xs(0)
                    load_span(1, 1)
                    load_x(0)
                    with sp.Fori(2, BLOCKS) as q:
                        load_xs(q - 1)
                        load_span(q, q)
                        store(q - 2)
                        load_x(q - 1)
                    load_xs(BLOCKS - 1)
                    store(BLOCKS - 2)
                    load_x(BLOCKS - 1)
                    store(BLOCKS - 1)
                with sp.Else():
                    with sp.Fori(0, BLOCKS) as b:
                        load_xs(b)
                        load_x(b)
                        with sp.Fori(0, BLOCKS) as n:
                            load_span(b * BLOCKS + n, n, NP)
                        store(b)
                sp.wait_ge(stored, 48 * BLOCKS)

            @block.gpsimd
            def _(pool):
                pool.iota(lane[:, :], [[1, 3 * P]], base=-P, channel_multiplier=0,
                          allow_small_or_imprecise_dtypes=True).then_inc(pool_ready, 1)
                pool.wait_ge(flag_ready, 1)
                near = pool.value_load(flag[0:1, 0:1])

                def gather_span(q, start=0):
                    for c, (j0, m) in enumerate(CHUNKS):
                        pool.wait_ge(idx_in[c], 16 * (q + 1))
                        pool.nop(nofuse=True)
                        for j in range(j0, j0 + m):
                            if j % 2 == 0:
                                wait(pool, message, start + NP * (q - 1) + j // 2 + 1)
                                pool.nop(nofuse=True)
                            pool.indirect_dma_start(
                                out=raw[:, j, :], out_offset=None, in_=x,
                                in_offset=bass.IndirectOffsetOnAxis(ap=idx[:, j:j + 1], axis=0),
                            ).then_inc(gathered[j], 16)

                with pool.If(near == 1):
                    gather_span(0)
                    with pool.Fori(1, BLOCKS) as q:
                        gather_span(q)
                with pool.Else():
                    gather_span(0)
                    with pool.Fori(1, BLOCKS * BLOCKS) as q:
                        gather_span(q, NP)

            @block.tensor
            def _(pe):
                pe.wait_ge(bad_ready, 1)
                pe.matmul(ps_d[0:1, 0:1], bad_sum[:, :], ones_c[:, :], start=True, stop=True)\
                  .then_inc(bad_total, 1)
                pe.wait_ge(flag_ready, 1)
                near = pe.value_load(flag[0:1, 0:1])
                pe.wait_ge(consts, N_CONST)

                def edge_layer(q, k, start=0):
                    j0, m = PAIRS[k]
                    pe.wait_ge(attr_in[k // 3], 16 * (q + 1))
                    wait(pe, message, start + NP * q + k - 2)
                    for j in range(j0, j0 + m):
                        mm = pe.matmul(ps_e[k % 3][:, (j - j0) * D:(j - j0 + 1) * D],
                                       attr[:, j * P:(j + 1) * P], we1[:, :], start=True, stop=True)
                    mm.then_inc(edge_net, 1)

                def add_tile(j, slot, start, stop):
                    pe.matmul(ps_sum[:, :], oh[:, slot, :], msg[:, j, 0, :], start=start, stop=False,
                              skip_group_check=True)
                    return pe.matmul(ps_sum[:, :], oh[:, slot, :], msg[:, j, 1, :], start=False, stop=stop,
                                     skip_group_check=True)

                def near_step(b, c):
                    _, j0, m = NEAR_STEPS[c]
                    first, last = near_sum_steps(b)[0], near_sum_steps(b)[-1]
                    if c == first:
                        wait(pe, s_ready, b)
                    pe.wait_ge(oh_ready, SUMS * b + c + 1)
                    if 2 <= c <= NP - 1:
                        pe.wait_ge(message, NP * b + c + 1)
                    elif c == 1 and first == 1:
                        pe.wait_ge(message, 2)
                    elif c == SUMS - 1:
                        pe.wait_ge(message, NP * (b + 1) + 2)
                    for j in range(j0, j0 + m):
                        mm = add_tile(j, OH_AT[c] + j - j0, c == first and j == j0, c == last and j == j0 + m - 1)
                    mm.then_inc(summed, near_inc(b, c))

                def turn(b):
                    pe.wait_ge(s_ready, b + 1)
                    wait(pe, sT_ready, b)
                    for n in range(4):
                        mm = pe.transpose(ps_t[:, n * P:(n + 1) * P], s_r[:, n * 128:(n + 1) * 128], ident[:, :])
                    mm.then_inc(s_turned, 1)

                def products(b):
                    pe.wait_ge(xT_in, 16 * (b + 1))
                    pe.wait_ge(sT_ready, b + 1)
                    wait(pe, dd, DD * b)
                    for k in range(KD):
                        pe.matmul(ps_d[:, 0:D], xTb[:, k, :], w1T_sb[:, k, :], start=(k == 0), stop=False)
                    for k in range(KD):
                        pe.matmul(ps_d[:, 0:D], sT[:, k * P:(k + 1) * P], w2T_sb[:, k, :], start=False,
                                  stop=(k == KD - 1))
                    for k in range(KD):
                        mm = pe.matmul(ps_d[:, D:2 * D], sT[:, (KD + k) * P:(KD + k + 1) * P], we2[:, k, :],
                                       start=(k == 0), stop=(k == KD - 1))
                    mm.then_inc(dense, 1)

                def near_block(b, tail=True):
                    for s in range(NP):
                        k = s + LEAD
                        if k < NP:
                            edge_layer(b, k)
                        elif not (isinstance(b, int) and b == BLOCKS - 1):
                            edge_layer(b + 1, k - NP)
                        if s in near_sum_steps(b):
                            near_step(b, s)
                        if tail and s == 1:
                            turn(b - 1)
                        if tail and s == 4:
                            products(b - 1)
                    if SUMS - 1 in near_sum_steps(b):
                        near_step(b, SUMS - 1)

                with pe.If(near == 1):
                    for k in range(LEAD):
                        edge_layer(0, k)
                    near_block(0, tail=False)
                    with pe.Fori(1, BLOCKS - 1) as b:
                        near_block(b)
                    near_block(BLOCKS - 1)
                    turn(BLOCKS - 1)
                    products(BLOCKS - 1)
                with pe.Else():
                    pe.wait_ge(prep, 3)
                    pe.matmul(ps_sum[:, 0:D], zero_oh[:, :], eb1[:, :], start=True, stop=True,
                              skip_group_check=True).then_inc(summed, NP)
                    with pe.Fori(0, BLOCKS) as b:
                        pe.wait_ge(s_ready, b)
                        pe.matmul(ps_sum[:, 0:D], zero_oh[:, :], eb1[:, :], start=True, stop=False,
                                  skip_group_check=True)
                        pe.matmul(ps_sum[:, D:2 * D], zero_oh[:, :], eb1[:, :], start=False, stop=False,
                                  skip_group_check=True)
                        with pe.Fori(0, BLOCKS) as n:
                            q = b * BLOCKS + n
                            for k, (j0, m) in enumerate(PAIRS):
                                edge_layer(q, k, NP)
                                pe.wait_ge(oh_ready, NP * q + k + 1)
                                pe.wait_ge(message, NP * (q + 1) + k + 1)
                                for j in range(j0, j0 + m):
                                    mm = add_tile(j, j, False, False)
                                mm.then_inc(summed, 1)
                        turn(b)
                        products(b)

            @block.scalar
            def _(act):
                act.wait_ge(flag_ready, 1)
                near = act.value_load(flag[0:1, 0:1])

                def highs(path, q, n, k):
                    j0, m = PAIRS[k]
                    wait(act, summed, path.slot_free(q, k))
                    for j in range(j0, j0 + m):
                        act.wait_ge(gathered[j], 16 * (q + 1))
                        act.activation(msg[:, j, 0, 0:D], raw[:, j, :], ACT.Copy,
                                       scale=w_sb[:, tile_cols(n, j)])
                    act.wait_ge(edge_net, NP * q + k + 1)
                    act.activation(msg[:, j0:j0 + m, 0, D:2 * D],
                                   ps_e[k % 3][:, 0:m * D].rearrange("p (j d) -> p j d", d=D),
                                   ACT.Relu).then_inc(high, 1)

                def turned(b):
                    act.wait_ge(s_turned, b + 1)
                    wait(act, dense, b)
                    act.activation(sT[:, :], ps_t[:, 0:4 * P], ACT.Copy).then_inc(sT_ready, 1)

                def norm(b):
                    act.wait_ge(dd, DD * b + 2)
                    act.activation(sq[:, :], o2[:, :], ACT.Square, accum_out=st[:, 0:1]).then_inc(da, 1)
                    act.wait_ge(da, DA * b + 1)
                    act.activation(st[:, 1:2], st[:, 0:1], ACT.Sqrt).then_inc(da, 1)

                def deviation(b):
                    act.wait_ge(dd, DD * b + 7)
                    act.activation(st[:, 5:6], st[:, 4:5], ACT.Sqrt, bias=ln_eps[:, :]).then_inc(da, 1)

                def near_block(b, tail=True):
                    for s in range(NP):
                        k = s + LEAD
                        if k < NP:
                            highs(Near, b, b, k)
                        elif not (isinstance(b, int) and b == BLOCKS - 1):
                            highs(Near, b + 1, b + 1, k - NP)
                        if tail and s == 2:
                            turned(b - 1)
                        if tail and s == 6:
                            norm(b - 1)
                        if tail and s == 7:
                            deviation(b - 1)

                with act.If(near == 1):
                    for k in range(LEAD):
                        highs(Near, 0, 0, k)
                    near_block(0, tail=False)
                    with act.Fori(1, BLOCKS - 1) as b:
                        near_block(b)
                    near_block(BLOCKS - 1)
                    turned(BLOCKS - 1)
                    norm(BLOCKS - 1)
                    deviation(BLOCKS - 1)
                with act.Else():
                    with act.Fori(0, BLOCKS) as b:
                        with act.Fori(0, BLOCKS) as n:
                            for k in range(NP):
                                highs(General, b * BLOCKS + n, n, k)
                        turned(b)
                        norm(b)
                        deviation(b)

            @block.vector
            def _(dve):
                dve.memset(ones_c[:, :], 1.0).then_inc(prep, 1)
                dve.memset(ln_eps[:, :], LN_EPS).then_inc(prep, 1)
                dve.memset(zero_oh[:, :], 0.0).then_inc(prep, 1)
                dve.memset(attr[ED:ED + 1, :], 1.0).then_inc(prep, 1)
                dve.wait_ge(edges_in, 32)
                dve.tensor_copy(dst_f[:, :, :], dst_i[:, :, :]).then_inc(prep, 1)
                dve.wait_ge(prep, 5)
                for b in range(BLOCKS):
                    dve.tensor_scalar(rel[:, b, :], dst_f[:, b, :], float(-P * b), None, ALU.add).then_inc(prep, 1)
                dve.wait_ge(prep, 5 + BLOCKS)
                dve.tensor_scalar(bad[:, :, 0:EDGE], rel[:, :, 0:EDGE], float(-P), None, ALU.is_lt).then_inc(prep, 1)
                dve.tensor_scalar(bad[:, :, EDGE:TILES], rel[:, :, EDGE:TILES], 0.0, None, ALU.is_lt).then_inc(prep, 1)
                dve.wait_ge(prep, 7 + BLOCKS)
                lim = TILES - EDGE
                dve.scalar_tensor_tensor(bad[:, :, 0:lim], rel[:, :, 0:lim], float(P), bad[:, :, 0:lim],
                                         ALU.is_ge, ALU.add).then_inc(prep, 1)
                dve.scalar_tensor_tensor(bad[:, :, lim:TILES], rel[:, :, lim:TILES], float(2 * P),
                                         bad[:, :, lim:TILES], ALU.is_ge, ALU.add).then_inc(prep, 1)
                dve.wait_ge(prep, 9 + BLOCKS)
                dve.reduce_sum(bad_sum[:, :], bad[:, :, :].rearrange("p b j -> p (b j)"), AX_X).then_inc(bad_ready, 1)
                dve.wait_ge(bad_total, 1)
                dve.tensor_scalar(flag[:, :], ps_d[0:1, 0:1], 0.0, None, ALU.is_equal).then_inc(flag_ready, 1)
                dve.wait_ge(consts, N_CONST)
                dve.tensor_tensor(b12[:, :], b01[:, :], b02[:, :], ALU.add).then_inc(prep, 1)
                dve.tensor_scalar(r0[:, :], eb1[:, :], 0.0, None, ALU.max).then_inc(prep, 1)
                dve.tensor_scalar(eps_t[:, :], eps_raw[:, :], 1.0, None, ALU.add).then_inc(prep, 1)
                dve.wait_ge(prep, 12 + BLOCKS)
                dve.wait_ge(pool_ready, 1)
                dve.wait_ge(flag_ready, 1)
                near = dve.value_load(flag[0:1, 0:1])

                def near_oh(b, c):
                    span, j0, m = NEAR_STEPS[c]
                    wait(dve, summed, SUMS * (b - 1) + c + 1)
                    for j in range(j0, j0 + m):
                        ins = dve.tensor_scalar(oh[:, OH_AT[c] + j - j0, :],
                                                lane[:, (1 - span) * P:(2 - span) * P],
                                                rel2[:, tile_cols(b + span, j)], None, ALU.is_equal)
                    ins.then_inc(oh_ready, near_inc(b, c))

                rel2 = rel[:, :, :].rearrange("p b j -> p (b j)")
                dst2 = dst_f[:, :, :].rearrange("p b j -> p (b j)")

                def lows(q, n, k):
                    j0, m = PAIRS[k]
                    dve.wait_ge(high, NP * q + k + 1)
                    for j in range(j0, j0 + m):
                        dve.scalar_tensor_tensor(msg[:, j, 1, 0:D], raw[:, j, :], w_sb[:, tile_cols(n, j)],
                                                 msg[:, j, 0, 0:D].bitcast(F32), ALU.mult, ALU.subtract)
                    dve.scalar_tensor_tensor(msg[:, j0:j0 + m, 1, D:2 * D],
                                             ps_e[k % 3][:, 0:m * D].rearrange("p (j d) -> p j d", d=D), 0.0,
                                             msg[:, j0:j0 + m, 0, D:2 * D].bitcast(F32), ALU.max, ALU.subtract)\
                       .then_inc(message, 1)

                def take_sums(b, steps):
                    dve.wait_ge(summed, steps)
                    dve.wait_ge(xs_in, 16 * (b + 1))
                    wait(dve, s_turned, b)
                    dve.scalar_tensor_tensor(s_r[:, 0:D], xs[:, :], 1.0, ps_sum[:, 0:D], ALU.add, ALU.mult)
                    dve.tensor_tensor(s_r[:, D:2 * D], ps_sum[:, D:2 * D], r0[:, :], ALU.add).then_inc(s_ready, 1)

                def step(b, n, ins):
                    ins.then_inc(dd, 1)
                    dve.wait_ge(dd, DD * b + n)

                def tail1(b):
                    dve.wait_ge(dense, b + 1)
                    step(b, 1, dve.tensor_tensor(o[:, :], ps_d[:, 0:D], b12[:, :], ALU.add))
                    wait(dve, da, DA * b)
                    step(b, 2, dve.scalar_tensor_tensor(o2[:, :], o[:, :], SLOPE, o[:, :], ALU.mult, ALU.max))

                def tail2(b):
                    dve.wait_ge(da, DA * b + 2)
                    step(b, 3, dve.tensor_scalar(st[:, 2:3], st[:, 1:2], NORM_EPS, None, ALU.max))
                    step(b, 4, dve.reciprocal(st[:, 3:4], st[:, 2:3]))
                    dve.wait_ge(xr_in, 16 * (b + 1))
                    step(b, 5, dve.scalar_tensor_tensor(y[:, :], o2[:, :], st[:, 3:4], xr[:, :], ALU.mult, ALU.add))
                    step(b, 6, dve.bn_stats(bn6[:, :], y[:, :]))
                    dve.nop(nofuse=True)
                    step(b, 7, dve.bn_aggr(st[:, 3:5], bn6[:, :]))

                def tail3(b):
                    dve.wait_ge(da, DA * (b + 1))
                    step(b, 8, dve.reciprocal(st[:, 6:7], st[:, 5:6]))
                    wait(dve, stored, 48 * b)
                    step(b, 9, dve.tensor_scalar(x1[:, :], y[:, :], st[:, 3:4], st[:, 6:7], ALU.subtract, ALU.mult))
                    step(b, 10, dve.tensor_tensor(tb[:, :], x1[:, :], eb2[:, :], ALU.add))
                    step(b, 11, dve.tensor_copy(table[:, 0, :], tb[:, :]))
                    dve.tensor_tensor(table[:, 1, :], tb[:, :], table[:, 0, :].bitcast(F32), ALU.subtract)\
                       .then_inc(dd, 1)
                    dve.scalar_tensor_tensor(y[:, :], x1[:, :], eps_t[:, :], tb[:, :], ALU.mult, ALU.add)\
                       .then_inc(dd, 1)
                    dve.wait_ge(dd, DD * b + 13)
                    dve.tensor_tensor(hb[:, :], ps_d[:, D:2 * D], y[:, :], ALU.add).then_inc(dd, 1)

                def near_block(b, tail=True):
                    if tail:
                        take_sums(b - 1, SUMS * b)
                    for s in range(NP):
                        if s + 1 in near_sum_steps(b):
                            near_oh(b, s + 1)
                        k = s + LEAD
                        if k < NP:
                            lows(b, b, k)
                        elif not (isinstance(b, int) and b == BLOCKS - 1):
                            lows(b + 1, b + 1, k - NP)
                        if tail and s == 5:
                            tail1(b - 1)
                        if tail and s == 6:
                            tail2(b - 1)
                        if tail and s == 8:
                            tail3(b - 1)
                    if not (isinstance(b, int) and b == BLOCKS - 1):
                        near_oh(b + 1, 0)

                with dve.If(near == 1):
                    for k in range(LEAD):
                        lows(0, 0, k)
                    near_block(0, tail=False)
                    with dve.Fori(1, BLOCKS - 1) as b:
                        near_block(b)
                    near_block(BLOCKS - 1)
                    take_sums(BLOCKS - 1, SUMS * BLOCKS)
                    tail1(BLOCKS - 1)
                    tail2(BLOCKS - 1)
                    tail3(BLOCKS - 1)
                with dve.Else():
                    dve.memset(bad[0:1, 0:1, 0:1], 0.0).then_inc(message, NP)
                    with dve.Fori(0, BLOCKS) as b:
                        with dve.Fori(0, BLOCKS) as n:
                            q = b * BLOCKS + n
                            for k, (j0, m) in enumerate(PAIRS):
                                wait(dve, summed, NP * q + k + 1)
                                for j in range(j0, j0 + m):
                                    ins = dve.tensor_scalar(oh[:, j, :], lane[:, P:2 * P], dst2[:, tile_cols(n, j)],
                                                            None, ALU.is_equal)
                                ins.then_inc(oh_ready, 1)
                                lows(q, n, k)
                        dve.tensor_scalar(dst_f[:, :, :], dst_f[:, :, :], float(-P), None, ALU.add)\
                           .then_inc(rel_ready, 1)
                        dve.wait_ge(rel_ready, b + 1)
                        take_sums(b, NP * BLOCKS * (b + 1) + NP)
                        tail1(b)
                        tail2(b)
                        tail3(b)
        with ExitStack() as cb:
            def s2(name, shape, dt):
                return sb(name, shape, dt, cb)

            def m2(name):
                return sem(name, cb)

            w1m = s2("w1m", [128, 2, KD, H], F32R)
            w2m = s2("w2m", [128, 2, KH, H], F32R)
            w3m = s2("w3m", [128, 2, KH, D], F32R)
            STAGE = 3
            stage = [s2(f"stage{n}", [128, H], F32) for n in range(STAGE)]
            b1m = s2("b1m", [128, H], F32R)
            b2m = s2("b2m", [128, H], F32R)
            b3m = s2("b3m", [128, D], F32R)
            ones_f = s2("ones_f", [128, P], F32)
            ones_r = s2("ones_r", [128, P], F32R)
            g1, be1 = s2("g1", [128, KH], F32), s2("be1", [128, KH], F32)
            g2, be2 = s2("g2", [128, KH], F32), s2("be2", [128, KH], F32)
            bng, bnb = s2("bng", [P, D], F32), s2("bnb", [P, D], F32)
            idx2 = s2("idx2", [P, TILES], I32)
            grow = s2("grow", [P, TILES, 2 * D], F32R)
            oh2 = s2("oh2", [P, OH_SLOTS, P], F32R)
            zero2 = s2("zero2", [P, P], F32)
            zrow = s2("zrow", [P, D], F32)
            hbx = s2("hbx", [P, D], F32)
            x1f = s2("x1f", [P, D], F32)
            h = s2("h", [P, D], F32)
            hT = s2("hT", [128, 2, KD * P], F32R)
            zn = s2("zn", [P, H], F32)
            aF = s2("aF", [128, KH, P], F32)
            a1 = s2("a1", [128, 2, KH, P], F32R)
            a2 = s2("a2", [128, 2, KH, P], F32R)
            bs = [s2(f"bs{n}", [P, 2, 6], F32) for n in range(2)]
            mv = [s2(f"mv{n}", [P, 8], F32) for n in range(2)]
            fs = s2("fs", [P, 6], F32)
            fm = s2("fm", [P, 8], F32)
            t = s2("t", [P, D], F32)
            v = s2("v", [P, D], F32)
            res = s2("res", [P, D], F32)

            ps_s = psum("ps_s", [P, 512], cb)
            ps_z = [psum(f"ps_z{n}", [P, 2, 512], cb) for n in range(2)]
            ps_tr = psum("ps_tr", [128, 2, 512], cb)
            ps_y = psum("ps_y", [P, 512], cb)

            consts2 = m2("consts2")
            w_in = [m2(f"w_in{n}") for n in range(STAGE)]
            w_high, w_ready = m2("w_high"), m2("w_ready")
            prep2, prep_ones = m2("prep2"), m2("prep_ones")
            rebased = m2("rebased")
            split_high = [m2(f"split_high{n}") for n in range(2)]
            idx2_in = [m2(f"idx2_in{c}") for c in range(3)]
            got = [m2(f"got{j}") for j in range(TILES)]
            hb_in, x1_in = m2("hb_in"), m2("x1_in")
            oh2_ready = m2("oh2_ready")
            sum_done = m2("sum_done")
            h_ready = m2("h_ready")
            h_turned = m2("h_turned")
            hT_high, hT_ready = m2("hT_high"), m2("hT_ready")
            z_done = [m2(f"z_done{n}") for n in range(2)]
            ln = [m2(f"ln{n}") for n in range(2)]
            std = [m2(f"std{n}") for n in range(2)]
            zn_ready = [m2(f"zn_ready{n}") for n in range(2)]
            turned2 = [m2(f"turned2_{n}") for n in range(2)]
            relu_out = [m2(f"relu_out{n}") for n in range(2)]
            a_ready = [m2(f"a_ready{n}") for n in range(2)]
            y_done = m2("y_done")
            fin = m2("fin")
            fstd = m2("fstd")
            out_stored = m2("out_stored")
            LN = 5
            FIN = 12

            pieces = [(m_w1[k * 128:(k + 1) * 128, :], w1m[:, :, k, :]) for k in range(KD)]
            pieces += [(m_w2[k * 128:(k + 1) * 128, :], w2m[:, :, k, :]) for k in range(KH)]
            pieces += [(m_w3[k * 512:(k + 1) * 512, :].rearrange("(k p) d -> p k d", p=128), w3m[:, :, 4 * k:4 * k + 4, :])
                       for k in range(KH // 4)]
            biases = [(m_b1, b1m, H), (m_b2, b2m, H), (m_b3, b3m, D)]
            N_SPLIT = len(pieces) + len(biases)

            def pick(dest, part):
                return dest[:, part]

            def as_piece(tile, dest):
                return tile if len(dest.shape) == 3 else tile.rearrange("p (k d) -> p k d", d=D)

            block2 = cb.enter_context(nc.Block())

            @block2.sync
            def _(sp):
                near = sp.value_load(flag[0:1, 0:1])

                def load_idx(q, n):
                    for c, (j0, m) in enumerate(CHUNKS):
                        for j in range(j0, j0 + m):
                            wait(sp, got[j], 16 * q)
                        sp.nop(nofuse=True)
                        sp.dma_start(idx2[:, j0:j0 + m], src[:, tile_cols(n, j0, m)]).then_inc(idx2_in[c], 16)

                def load_hb(b):
                    wait(sp, h_ready, b)
                    sp.nop(nofuse=True)
                    sp.dma_start(hbx[:, :], rows(hbase_dram, b)).then_inc(hb_in, 16)

                def load_x1(b):
                    wait(sp, fin, FIN * b)
                    sp.nop(nofuse=True)
                    sp.dma_start(x1f[:, :], rows(x1_dram, b)).then_inc(x1_in, 16)

                def store(b):
                    sp.wait_ge(fin, FIN * (b + 1))
                    sp.nop(nofuse=True)
                    sp.dma_start(rows(out, b), res[:, :]).then_inc(out_stored, 16)

                def load_weights():
                    for tile, source in ((g1, m_g1), (be1, m_be1), (g2, m_g2), (be2, m_be2), (bng, bn_g), (bnb, bn_b)):
                        sp.dma_start(tile[:, :], source).then_inc(consts2, 16)
                    for n, (source, dest) in enumerate(pieces):
                        wait(sp, w_ready, n - STAGE + 1)
                        sp.dma_start(as_piece(stage[n % STAGE][:, :], dest), source).then_inc(w_in[n % STAGE], 16)
                    for n, (source, dest, width) in enumerate(biases, len(pieces)):
                        wait(sp, w_ready, n - STAGE + 1)
                        for row in (0, 32):
                            sp.dma_start(stage[n % STAGE][row:row + 1, 0:width], source).then_inc(w_in[n % STAGE], 16)

                def iteration(q):
                    if not (isinstance(q, int) and q >= BLOCKS):
                        load_idx(q, q)
                    if not (isinstance(q, int) and not 0 <= q - 1 < BLOCKS):
                        load_hb(q - 1)
                    if not (isinstance(q, int) and not 0 <= q - 4 < BLOCKS):
                        store(q - 4)
                    if not (isinstance(q, int) and not 0 <= q - 3 < BLOCKS):
                        load_x1(q - 3)

                with sp.If(near == 1):
                    load_idx(0, 0)
                    load_weights()
                    for q in range(1, 5):
                        iteration(q)
                    with sp.Fori(5, BLOCKS) as q:
                        iteration(q)
                    for q in range(BLOCKS, BLOCKS + 4):
                        iteration(q)
                with sp.Else():
                    load_weights()
                    with sp.Fori(0, BLOCKS) as b:
                        load_hb(b)
                        load_x1(b)
                        with sp.Fori(0, BLOCKS) as n:
                            load_idx(b * BLOCKS + n, n)
                        store(b)
                sp.wait_ge(out_stored, 16 * BLOCKS)

            @block2.gpsimd
            def _(pool):
                near = pool.value_load(flag[0:1, 0:1])

                def gather_span(path, q):
                    for c, (j0, m) in enumerate(CHUNKS):
                        pool.wait_ge(idx2_in[c], 16 * (q + 1))
                        pool.nop(nofuse=True)
                        for j in range(j0, j0 + m):
                            if j % 2 == 0:
                                wait(pool, sum_done, path.slot_free(q, j // 2))
                                pool.nop(nofuse=True)
                            pool.indirect_dma_start(
                                out=grow[:, j, :].bitcast(F32), out_offset=None, in_=table_dram,
                                in_offset=bass.IndirectOffsetOnAxis(ap=idx2[:, j:j + 1], axis=0),
                            ).then_inc(got[j], 16)

                with pool.If(near == 1):
                    gather_span(Near, 0)
                    with pool.Fori(1, BLOCKS) as q:
                        gather_span(Near, q)
                with pool.Else():
                    gather_span(Near, 0)
                    with pool.Fori(1, BLOCKS * BLOCKS) as q:
                        gather_span(General, q)

            @block2.tensor
            def _(pe):
                near = pe.value_load(flag[0:1, 0:1])
                pe.wait_ge(prep2, 3)

                def add_tile(j, slot, start, stop):
                    pe.matmul(ps_s[:, 0:D], oh2[:, slot, :], grow[:, j, 0:D], start=start, stop=False,
                              skip_group_check=True)
                    return pe.matmul(ps_s[:, 0:D], oh2[:, slot, :], grow[:, j, D:2 * D], start=False, stop=stop,
                                     skip_group_check=True)

                def near_step(b, c):
                    span, j0, m = NEAR_STEPS[c]
                    first, last = near_sum_steps(b)[0], near_sum_steps(b)[-1]
                    if c == first:
                        wait(pe, h_ready, b)
                    pe.wait_ge(oh2_ready, SUMS * b + c + 1)
                    for j in range(j0, j0 + m):
                        pe.wait_ge(got[j], 16 * (b + span + 1))
                        mm = add_tile(j, OH_AT[c] + j - j0, c == first and j == j0, c == last and j == j0 + m - 1)
                    mm.then_inc(sum_done, near_inc(b, c))

                def turn_h(path, b):
                    pe.wait_ge(h_ready, b + 1)
                    wait(pe, relu_out[1], 2 * path.t2_before_t1(b))
                    for k in range(KD):
                        mm = pe.transpose(ps_tr[:, 0, k * P:(k + 1) * P], h[:, k * 128:(k + 1) * 128], ident[:, :])
                    mm.then_inc(h_turned, 1)

                def three(acc, left, right, start, stop):
                    for n, (a, b) in enumerate(((0, 0), (0, 1), (1, 0))):
                        mm = pe.matmul(acc, left(a), right(b), start=start and n == 0, stop=stop and n == 2,
                                       skip_group_check=True)
                    return mm

                def layer1(b):
                    pe.wait_ge(hT_ready, b + 1)
                    wait(pe, zn_ready[0], 2 * b)
                    for n in range(2):
                        cols = slice(n * 512, (n + 1) * 512)
                        pe.matmul(ps_z[0][:, n, :], ones_r[:, :], b1m[:, cols], start=True, stop=False,
                                  skip_group_check=True)
                        for k in range(KD):
                            mm = three(ps_z[0][:, n, :], lambda a: hT[:, a, k * P:(k + 1) * P],
                                       lambda a: w1m[:, a, k, cols], False, k == KD - 1)
                        mm.then_inc(z_done[0], 1)

                def layer2(b, n):
                    if n == 0:
                        pe.wait_ge(a_ready[0], 2 * (b + 1))
                        wait(pe, zn_ready[1], 2 * b)
                    cols = slice(n * 512, (n + 1) * 512)
                    pe.matmul(ps_z[1][:, n, :], ones_r[:, :], b2m[:, cols], start=True, stop=False,
                              skip_group_check=True)
                    for k in range(KH):
                        mm = three(ps_z[1][:, n, :], lambda a: a1[:, a, k, :], lambda a: w2m[:, a, k, cols],
                                   False, k == KH - 1)
                    mm.then_inc(z_done[1], 1)

                def layer3(b, part):
                    if part == 0:
                        wait(pe, fin, FIN * b)
                        pe.wait_ge(a_ready[1], 2 * b + 1)
                        pe.matmul(ps_y[:, 0:D], ones_r[:, :], b3m[:, :], start=True, stop=False,
                                  skip_group_check=True)
                    else:
                        pe.wait_ge(a_ready[1], 2 * b + 2)
                    for k in range(4 * part, 4 * part + 4):
                        mm = three(ps_y[:, 0:D], lambda a: a2[:, a, k, :], lambda a: w3m[:, a, k, :],
                                   False, k == KH - 1)
                    if part == 1:
                        mm.then_inc(y_done, 1)

                def turn_z(path, layer, b):
                    if layer == 0:
                        pe.wait_ge(hT_ready, b + 1)
                    else:
                        pe.wait_ge(relu_out[0], 2 * path.t1_before_t2(b))
                    for half in range(2):
                        pe.wait_ge(zn_ready[layer], 2 * b + half + 1)
                        for c in range(4):
                            k = 4 * half + c
                            mm = pe.transpose(ps_tr[:, half, c * P:(c + 1) * P], zn[:, k * 128:(k + 1) * 128],
                                              ident[:, :])
                        mm.then_inc(turned2[layer], 1)

                def has(b):
                    return not isinstance(b, int) or 0 <= b < BLOCKS

                def iteration(i):
                    if has(i - 1):
                        layer1(i - 1)
                    if has(i - 2):
                        layer2(i - 2, 0)
                    if has(i - 1):
                        turn_z(Near, 0, i - 1)
                    if has(i - 2):
                        layer2(i - 2, 1)
                    if has(i):
                        steps = near_sum_steps(i)
                        for c in steps:
                            if c < 5:
                                near_step(i, c)
                    if has(i - 2):
                        turn_z(Near, 1, i - 2)
                    if has(i):
                        for c in steps:
                            if c >= 5:
                                near_step(i, c)
                    if has(i - 2):
                        layer3(i - 2, 0)
                    if has(i):
                        turn_h(Near, i)
                    if has(i - 2):
                        layer3(i - 2, 1)

                with pe.If(near == 1):
                    iteration(0)
                    pe.wait_ge(w_ready, N_SPLIT)
                    for i in range(1, 3):
                        iteration(i)
                    with pe.Fori(3, BLOCKS - 1) as i:
                        iteration(i)
                    for i in range(BLOCKS - 1, BLOCKS + 2):
                        iteration(i)
                with pe.Else():
                    pe.wait_ge(w_ready, N_SPLIT)
                    pe.matmul(ps_s[:, 0:D], zero2[:, :], zrow[:, :], start=True, stop=True,
                              skip_group_check=True).then_inc(sum_done, NP)
                    with pe.Fori(0, BLOCKS) as b:
                        pe.wait_ge(h_ready, b)
                        pe.matmul(ps_s[:, 0:D], zero2[:, :], zrow[:, :], start=True, stop=False,
                                  skip_group_check=True)
                        with pe.Fori(0, BLOCKS) as n:
                            q = b * BLOCKS + n
                            for k, (j0, m) in enumerate(PAIRS):
                                pe.wait_ge(oh2_ready, NP * q + k + 1)
                                for j in range(j0, j0 + m):
                                    pe.wait_ge(got[j], 16 * (q + 1))
                                    mm = add_tile(j, j, False, False)
                                mm.then_inc(sum_done, 1)
                        turn_h(General, b)
                        layer1(b)
                        turn_z(General, 0, b)
                        layer2(b, 0)
                        layer2(b, 1)
                        turn_z(General, 1, b)
                        layer3(b, 0)
                        layer3(b, 1)

            @block2.scalar
            def _(act):
                near = act.value_load(flag[0:1, 0:1])
                for n, (source, dest) in enumerate(pieces):
                    act.wait_ge(w_in[n % STAGE], 16 * (n // STAGE + 1))
                    act.activation(pick(dest, 0), as_piece(stage[n % STAGE][:, :], dest), ACT.Copy)\
                       .then_inc(w_high, 1)
                act.wait_ge(prep2, 5)
                for n, (source, dest, width) in enumerate(biases, len(pieces)):
                    act.wait_ge(w_in[n % STAGE], 16 * (n // STAGE + 2))
                    act.activation(dest[0:1, :], stage[n % STAGE][0:1, 0:width], ACT.Copy)
                    act.activation(dest[32:33, :], stage[n % STAGE][32:33, 0:width], ACT.Copy).then_inc(w_high, 1)
                act.wait_ge(consts2, 96)

                def h_high(b):
                    act.wait_ge(h_turned, b + 1)
                    wait(act, z_done[0], 2 * b)
                    act.activation(hT[:, 0, :], ps_tr[:, 0, 0:KD * P], ACT.Copy).then_inc(hT_high, 1)

                def deviation(layer, b):
                    act.wait_ge(ln[layer], LN * b + 3)
                    act.activation(mv[layer][:, 2:3], mv[layer][:, 1:2], ACT.Sqrt, bias=ln_eps[:, :])\
                       .then_inc(std[layer], 1)

                def normalize(path, layer, b):
                    act.wait_ge(ln[layer], LN * (b + 1))
                    if layer == 0:
                        wait(act, turned2[1], 2 * path.t2_before_t1(b))
                    else:
                        act.wait_ge(turned2[0], 2 * path.t1_before_t2(b))
                    for n in range(2):
                        act.activation(zn[:, n * 512:(n + 1) * 512], ps_z[layer][:, n, :], ACT.Identity,
                                       bias=mv[layer][:, 4:5], scale=mv[layer][:, 3:4]).then_inc(zn_ready[layer], 1)

                def relu(path, layer, b):
                    gg, bb = ((g1, be1), (g2, be2))[layer]
                    if layer == 0:
                        wait(act, a_ready[1], 2 * path.t2_before_t1(b))
                    else:
                        act.wait_ge(a_ready[0], 2 * path.t1_before_t2(b))
                    for half in range(2):
                        act.wait_ge(turned2[layer], 2 * b + half + 1)
                        for c in range(4):
                            k = 4 * half + c
                            ins = act.activation(aF[:, k, :], ps_tr[:, half, c * P:(c + 1) * P], ACT.Relu,
                                                 bias=bb[:, k:k + 1], scale=gg[:, k:k + 1])
                        ins.then_inc(relu_out[layer], 1)

                def finish_std(b, n):
                    act.wait_ge(fin, FIN * b + (3, 10)[n])
                    act.activation(fm[:, 2 + n:3 + n], fm[:, 1:2] if n == 0 else fm[:, 5:6], ACT.Sqrt,
                                   bias=ln_eps[:, :]).then_inc(fstd, 1)

                def has(b):
                    return not isinstance(b, int) or 0 <= b < BLOCKS

                def iteration(i):
                    if has(i - 3):
                        finish_std(i - 3, 0)
                    if has(i - 1):
                        deviation(0, i - 1)
                        normalize(Near, 0, i - 1)
                    if has(i - 3):
                        finish_std(i - 3, 1)
                    if has(i - 1):
                        relu(Near, 0, i - 1)
                    if has(i - 2):
                        deviation(1, i - 2)
                        normalize(Near, 1, i - 2)
                        relu(Near, 1, i - 2)
                    if has(i):
                        h_high(i)

                with act.If(near == 1):
                    for i in range(3):
                        iteration(i)
                    with act.Fori(3, BLOCKS) as i:
                        iteration(i)
                    for i in range(BLOCKS, BLOCKS + 3):
                        iteration(i)
                with act.Else():
                    with act.Fori(0, BLOCKS) as b:
                        h_high(b)
                        for layer in range(2):
                            deviation(layer, b)
                            normalize(General, layer, b)
                            relu(General, layer, b)
                        finish_std(b, 0)
                        finish_std(b, 1)

            @block2.vector
            def _(dve):
                dve.memset(zero2[:, :], 0.0).then_inc(prep2, 1)
                dve.memset(zrow[:, :], 0.0).then_inc(prep2, 1)
                dve.memset(ones_f[:, :], 1.0).then_inc(prep_ones, 1)
                dve.wait_ge(prep_ones, 1)
                dve.tensor_copy(ones_r[:, :], ones_f[:, :]).then_inc(prep2, 1)
                dve.memset(b1m[:, :].bitcast(F32), 0.0)
                dve.memset(b2m[:, :].bitcast(F32), 0.0).then_inc(prep2, 1)
                dve.memset(b3m[:, :].bitcast(F32), 0.0).then_inc(prep2, 1)
                near = dve.value_load(flag[0:1, 0:1])
                for n, (source, dest) in enumerate(pieces):
                    dve.wait_ge(w_high, n + 1)
                    dve.tensor_tensor(pick(dest, 1), as_piece(stage[n % STAGE][:, :], dest),
                                      pick(dest, 0).bitcast(F32), ALU.subtract).then_inc(w_ready, 1)
                for n, (source, dest, width) in enumerate(biases, len(pieces)):
                    dve.wait_ge(w_high, n + 1)
                    dve.tensor_tensor(dest[32:33, :], stage[n % STAGE][32:33, 0:width],
                                      dest[32:33, :].bitcast(F32), ALU.subtract).then_inc(w_ready, 1)
                dve.wait_ge(consts2, 96)
                rel2 = rel[:, :, :].rearrange("p b j -> p (b j)")
                dst2 = dst_f[:, :, :].rearrange("p b j -> p (b j)")

                def near_oh(b, c):
                    span, j0, m = NEAR_STEPS[c]
                    wait(dve, sum_done, SUMS * (b - 1) + c + 1)
                    for j in range(j0, j0 + m):
                        ins = dve.tensor_scalar(oh2[:, OH_AT[c] + j - j0, :],
                                                lane[:, (1 - span) * P:(2 - span) * P],
                                                rel2[:, tile_cols(b + span, j)], None, ALU.is_equal)
                    ins.then_inc(oh2_ready, near_inc(b, c))

                def take_h(b, steps):
                    dve.wait_ge(sum_done, steps)
                    dve.wait_ge(hb_in, 16 * (b + 1))
                    wait(dve, h_turned, b)
                    dve.tensor_tensor(h[:, :], ps_s[:, 0:D], hbx[:, :], ALU.add).then_inc(h_ready, 1)

                def h_low(b):
                    dve.wait_ge(hT_high, b + 1)
                    dve.tensor_tensor(hT[:, 1, :], ps_tr[:, 0, 0:KD * P], hT[:, 0, :].bitcast(F32), ALU.subtract)\
                       .then_inc(hT_ready, 1)

                def stats(layer, b, n):
                    dve.wait_ge(z_done[layer], 2 * b + n + 1)
                    dve.bn_stats(bs[layer][:, n, :], ps_z[layer][:, n, :]).then_inc(ln[layer], 1)

                def aggregate(out_, in_, s, value):
                    dve.wait_ge(s, value)
                    dve.nop(nofuse=True)
                    dve.bn_aggr(out_, in_).then_inc(s, 1)

                def norm_scalars(layer, b):
                    m = mv[layer]
                    dve.wait_ge(std[layer], b + 1)
                    dve.reciprocal(m[:, 3:4], m[:, 2:3]).then_inc(ln[layer], 1)
                    dve.wait_ge(ln[layer], LN * b + 4)
                    dve.scalar_tensor_tensor(m[:, 4:5], m[:, 0:1], -1.0, m[:, 3:4], ALU.mult, ALU.mult)\
                       .then_inc(ln[layer], 1)

                def split(layer, b):
                    a = (a1, a2)[layer]
                    if layer == 0:
                        wait(dve, z_done[1], 2 * b)
                    else:
                        wait(dve, y_done, b)
                    for half in range(2):
                        ks = slice(4 * half, 4 * half + 4)
                        dve.wait_ge(relu_out[layer], 2 * b + half + 1)
                        dve.tensor_copy(a[:, 0, ks, :], aF[:, ks, :]).then_inc(split_high[layer], 1)
                        dve.wait_ge(split_high[layer], 2 * b + half + 1)
                        dve.tensor_tensor(a[:, 1, ks, :], aF[:, ks, :], a[:, 0, ks, :].bitcast(F32), ALU.subtract)\
                           .then_inc(a_ready[layer], 1)

                def step(b, n, ins):
                    ins.then_inc(fin, 1)
                    dve.wait_ge(fin, FIN * b + n)

                def finish1(b):
                    dve.wait_ge(y_done, b + 1)
                    dve.wait_ge(x1_in, 16 * (b + 1))
                    step(b, 1, dve.tensor_tensor(t[:, :], ps_y[:, 0:D], x1f[:, :], ALU.add))
                    step(b, 2, dve.bn_stats(fs[:, :], t[:, :]))
                    aggregate(fm[:, 0:2], fs[:, :], fin, FIN * b + 2)

                def finish2(b):
                    dve.wait_ge(fstd, 2 * b + 1)
                    step(b, 4, dve.reciprocal(fm[:, 6:7], fm[:, 2:3]))
                    step(b, 5, dve.tensor_scalar(v[:, :], t[:, :], fm[:, 0:1], fm[:, 6:7], ALU.subtract, ALU.mult))
                    step(b, 6, dve.tensor_tensor(v[:, :], v[:, :], bng[:, :], ALU.mult))
                    step(b, 7, dve.tensor_tensor(v[:, :], v[:, :], bnb[:, :], ALU.add))
                    step(b, 8, dve.scalar_tensor_tensor(v[:, :], v[:, :], 0.0, x1f[:, :], ALU.max, ALU.add))
                    step(b, 9, dve.bn_stats(fs[:, :], v[:, :]))
                    aggregate(fm[:, 4:6], fs[:, :], fin, FIN * b + 9)

                def finish3(b):
                    dve.wait_ge(fstd, 2 * b + 2)
                    step(b, 11, dve.reciprocal(fm[:, 7:8], fm[:, 3:4]))
                    wait(dve, out_stored, 16 * b)
                    dve.tensor_scalar(res[:, :], v[:, :], fm[:, 4:5], fm[:, 7:8], ALU.subtract, ALU.mult)\
                       .then_inc(fin, 1)

                def has(b):
                    return not isinstance(b, int) or 0 <= b < BLOCKS

                def iteration(i):
                    if has(i - 3):
                        finish1(i - 3)
                    if has(i - 1):
                        stats(0, i - 1, 0)
                        stats(0, i - 1, 1)
                        aggregate(mv[0][:, 0:2], bs[0][:, :, :], ln[0], LN * (i - 1) + 2)
                        norm_scalars(0, i - 1)
                    if has(i - 3):
                        finish2(i - 3)
                    if has(i):
                        for c in near_sum_steps(i):
                            near_oh(i, c)
                    if has(i - 2):
                        stats(1, i - 2, 0)
                    if has(i - 3):
                        finish3(i - 3)
                    if has(i - 1):
                        split(0, i - 1)
                    if has(i - 2):
                        stats(1, i - 2, 1)
                        aggregate(mv[1][:, 0:2], bs[1][:, :, :], ln[1], LN * (i - 2) + 2)
                        norm_scalars(1, i - 2)
                        split(1, i - 2)
                    if has(i):
                        take_h(i, SUMS * (i + 1))
                        h_low(i)

                with dve.If(near == 1):
                    for i in range(3):
                        iteration(i)
                    with dve.Fori(3, BLOCKS - 1) as i:
                        iteration(i)
                    for i in range(BLOCKS - 1, BLOCKS + 3):
                        iteration(i)
                with dve.Else():
                    dve.tensor_scalar(dst_f[:, :, :], dst_f[:, :, :], float(N), None, ALU.add).then_inc(rebased, 1)
                    dve.wait_ge(rebased, 1)
                    with dve.Fori(0, BLOCKS) as b:
                        with dve.Fori(0, BLOCKS) as n:
                            q = b * BLOCKS + n
                            for k, (j0, m) in enumerate(PAIRS):
                                wait(dve, sum_done, NP * q + k + 1)
                                for j in range(j0, j0 + m):
                                    ins = dve.tensor_scalar(oh2[:, j, :], lane[:, P:2 * P], dst2[:, tile_cols(n, j)],
                                                            None, ALU.is_equal)
                                ins.then_inc(oh2_ready, 1)
                        dve.tensor_scalar(dst_f[:, :, :], dst_f[:, :, :], float(-P), None, ALU.add)\
                           .then_inc(rebased, 1)
                        dve.wait_ge(rebased, b + 2)
                        take_h(b, NP * BLOCKS * (b + 1) + NP)
                        h_low(b)
                        for layer in range(2):
                            stats(layer, b, 0)
                            stats(layer, b, 1)
                            aggregate(mv[layer][:, 0:2], bs[layer][:, :, :], ln[layer], LN * b + 2)
                            norm_scalars(layer, b)
                            split(layer, b)
                        finish1(b)
                        finish2(b)
                        finish3(b)


def build_arrays(inputs):
    import numpy as np
    a = {k: np.asarray(v) for k, v in inputs.items()}

    def col(v):
        return np.ascontiguousarray(v.reshape(BLOCKS * TILES, P).T)

    def spread(v):
        return np.ascontiguousarray(np.broadcast_to(v.reshape(1, -1), (P, v.size)))

    def chunks(v):
        return np.ascontiguousarray(v.reshape(KH, 128).T)

    return {
        "x": a["x"],
        "xT": np.ascontiguousarray(a["x"].T.reshape(KD, 128, N).transpose(1, 0, 2)),
        "src": col(a["src"]), "dst": col(a["dst"]), "weight": col(a["edge_weight"]),
        "attrT": np.ascontiguousarray(a["edge_attr_64"].T),
        "w1T": np.ascontiguousarray(a["L0_gnn_W1"].T), "w2T": np.ascontiguousarray(a["L0_gnn_W2"].T),
        "bias01": spread(a["L0_gnn_b1"]), "bias02": spread(a["L0_gnn_b2"]),
        "eps_in": spread(a["L1_gnn_eps"]),
        "ee_w1": a["L1_gnn_ee_w1"], "ee_b1row": a["L1_gnn_ee_b1"].reshape(1, D), "ee_b1": spread(a["L1_gnn_ee_b1"]),
        "ee_w2": a["L1_gnn_ee_w2"], "ee_b2": spread(a["L1_gnn_ee_b2"]),
        "m_w1": a["L1_gnn_w1"], "m_b1": a["L1_gnn_b1"].reshape(1, H),
        "m_g1": chunks(a["L1_gnn_g1"]), "m_be1": chunks(a["L1_gnn_be1"]),
        "m_w2": a["L1_gnn_w2"], "m_b2": a["L1_gnn_b2"].reshape(1, H),
        "m_g2": chunks(a["L1_gnn_g2"]), "m_be2": chunks(a["L1_gnn_be2"]),
        "m_w3": a["L1_gnn_w3"], "m_b3": a["L1_gnn_b3"].reshape(1, D),
        "bn_g": spread(a["L1_gnn_bn_g"]), "bn_b": spread(a["L1_gnn_bn_b"]),
        "ident_in": np.eye(P, dtype=np.float32),
    }


def kernel(**inputs):
    import concourse.bacc as _bacc
    from concourse.bass_utils import run_bass_kernel_spmd as _run

    nc = _bacc.Bacc("TRN2", target_bir_lowering=False, num_devices=1)
    arrays, args = {}, []
    for name, a in build_arrays(inputs).items():
        arrays[f"in_{name}"] = a
        args.append(nc.dram_tensor(f"in_{name}", a.shape, mybir.dt.from_np(a.dtype), kind="ExternalInput").ap())
    args.append(nc.dram_tensor("out", (N, D), F32, kind="ExternalOutput").ap())
    gnn_program(nc, *args)
    return _run(nc, [arrays], core_ids=[0]).results[0]["out"]
```

```python
from contextlib import ExitStack

import concourse.bass as bass
from concourse import mybir

F32 = mybir.dt.float32
F32R = mybir.dt.float32r
I32 = mybir.dt.int32
ALU = mybir.AluOpType
ACT = mybir.ActivationFunctionType
AX_X = mybir.AxisListType.X

N, E, D, ED, H = 3125, 53125, 256, 64, 1024
P = 125
BLOCKS = N // P
TILES = E // P // BLOCKS
EDGES = [1, 4]
PAIRS = [(0, 2), (2, 2), (4, 2), (6, 2), (8, 2), (10, 2), (12, 2), (14, 2), (16, 1)]
NP = len(PAIRS)
LEAD = 3
CHUNKS = [(0, 6), (6, 6), (12, 5)]
KD = D // 128
KH = H // 128
LN_EPS = 1e-5
NORM_EPS = 1e-12
SLOPE = 0.2
SUMS = 10

def wait(eng, sem, value):
    if isinstance(value, int) and value <= 0:
        return
    eng.wait_ge(sem, value)


class Near:

    def __init__(self, edge):
        self.edge = edge
        self.steps = [(-1, TILES - edge, edge), (0, 0, 4)] + [(0, j, m) for j, m in PAIRS[2:]] + [(1, 0, edge)]
        self.slot = [0]
        for _, _, m in self.steps:
            self.slot.append(self.slot[-1] + m)

    def slot_free(self, q, k):
        if isinstance(q, int) and q == 0:
            return 0
        if k < 2:
            return SUMS * (q - 1) + 2
        if PAIRS[k][0] + PAIRS[k][1] <= TILES - self.edge:
            return SUMS * (q - 1) + k + 1
        return SUMS * q + 1

    @staticmethod
    def t2_before_t1(b):
        return b - 1

    @staticmethod
    def t1_before_t2(b):
        return min(b + 2, BLOCKS) if isinstance(b, int) else b + 2


OH_SLOTS = TILES + 2 * EDGES[-1]
OH_GROUPS = [(0, 0), (1, 1), (2, 3), (4, 5), (6, 8), (9, 9)]


class General:

    @staticmethod
    def slot_free(q, k):
        return NP * q + k + 1

    @staticmethod
    def t2_before_t1(b):
        return b

    @staticmethod
    def t1_before_t2(b):
        return b + 1


def choose(eng, lvl, near_program, general_program):
    with eng.If(lvl > len(EDGES) - 1):
        near_program(Near(EDGES[0]))
    with eng.Else():
        with eng.If(lvl > 0):
            near_program(Near(EDGES[1]))
        with eng.Else():
            general_program()


def equal(dve, out_, lanes, which, m):
    return dve.tensor_tensor(out_, lanes.unsqueeze(1).to_broadcast([P, m, P]),
                             which.unsqueeze(2).to_broadcast([P, m, P]), ALU.is_equal)


def near_sum_steps(b):
    first = 1 if isinstance(b, int) and b == 0 else 0
    last = SUMS - 1 if isinstance(b, int) and b == BLOCKS - 1 else SUMS
    return [c for c in range(first, last)]


def exists(b):
    return not isinstance(b, int) or 0 <= b < BLOCKS


def near_inc(b, c):
    if isinstance(b, int) and b == 0 and c == 1:
        return 2
    if isinstance(b, int) and b == BLOCKS - 1 and c == SUMS - 2:
        return 2
    return 1


def gnn_program(nc, x, xT, src, dst, weight, attrT, w1T, w2T, bias01, bias02, eps_in, ee_w1, ee_b1row, ee_b1,
                ee_w2, ee_b2, m_w1, m_b1, m_g1, m_be1, m_w2, m_b2, m_g2, m_be2, m_w3, m_b3, bn_g, bn_b,
                ident_in, out):
    x1_dram = nc.dram_tensor("x1_dram", (N, D), F32).ap()
    hbase_dram = nc.dram_tensor("hbase_dram", (N, D), F32).ap()
    table_dram = nc.dram_tensor("table_dram", (N, 2 * D), F32).ap()

    with ExitStack() as keep:
        def sb(name, shape, dt, ctx=keep):
            return ctx.enter_context(nc.sbuf_tensor(name, shape, dt))

        def psum(name, shape, ctx):
            return ctx.enter_context(nc.psum_tensor(name, shape, F32))

        def sem(name, ctx=keep):
            return ctx.enter_context(nc.semaphore(name))

        dst_f = sb("dst_f", [P, BLOCKS, TILES], F32)
        rel = sb("rel", [P, BLOCKS, TILES], F32)
        lane = sb("lane", [P, 3 * P], F32)
        level = sb("level", [1, 1], I32)
        src_all = sb("src_all", [P, BLOCKS * TILES], I32)
        ident = sb("ident", [P, P], F32)

        eps_t = sb("eps_t", [P, 1], F32)
        ln_eps = sb("ln_eps", [P, 1], F32)

        with ExitStack() as ca:
            def sa(name, shape, dt):
                return sb(name, shape, dt, ca)

            def ma(name):
                return sem(name, ca)

            dst_i = sa("dst_i", [P, BLOCKS, TILES], I32)
            w_sb = sa("w_sb", [P, BLOCKS * TILES], F32)
            idx = [sa(f"idx{c}", [P, m], I32) for c, (_, m) in enumerate(CHUNKS)]
            attr = sa("attr", [ED + 1, TILES * P], F32)
            raw = sa("raw", [P, TILES, D], F32)
            msg = sa("msg", [P, TILES, 2, 2 * D], F32R)
            oh = sa("oh", [P, OH_SLOTS, P], F32R)
            bad = sa("bad", [P, len(EDGES), BLOCKS, TILES], F32)
            bad_sum = sa("bad_sum", [P, len(EDGES)], F32)
            holds = sa("holds", [1, len(EDGES)], F32)
            ones_c = sa("ones_c", [P, 1], F32)
            zero_oh = sa("zero_oh", [P, P], F32)
            w1T_sb = sa("w1T_sb", [128, KD, D], F32)
            w2T_sb = sa("w2T_sb", [128, KD, D], F32)
            we1 = sa("we1", [ED + 1, D], F32)
            we2 = sa("we2", [128, KD, D], F32)
            b01 = sa("b01", [P, D], F32)
            b02 = sa("b02", [P, D], F32)
            b12 = sa("b12", [P, D], F32)
            eb1 = sa("eb1", [P, D], F32)
            r0 = sa("r0", [P, D], F32)
            eb2 = sa("eb2", [P, D], F32)
            eps_raw = sa("eps_raw", [P, 1], F32)
            warm = sa("warm", [P, 1], F32)
            xs = sa("xs", [P, D], F32)
            xr = sa("xr", [P, D], F32)
            xTb = sa("xTb", [128, KD, P], F32)
            s_r = sa("s_r", [P, 2 * D], F32)
            sT = sa("sT", [128, 4 * P], F32)
            o = sa("o", [P, D], F32)
            o2 = sa("o2", [P, D], F32)
            sq = sa("sq", [P, D], F32)
            st = sa("st", [P, 8], F32)
            bn6 = sa("bn6", [P, 6], F32)
            y = sa("y", [P, D], F32)
            x1 = sa("x1", [P, D], F32)
            tb = sa("tb", [P, D], F32)
            u = sa("u", [P, D], F32)
            table = sa("table", [P, 2, D], F32R)
            hb = sa("hb", [P, D], F32)

            ps_sum = psum("ps_sum", [P, 512], ca)
            ps_e = [psum(f"ps_e{n}", [P, 512], ca) for n in range(3)]
            ps_t = psum("ps_t", [128, 512], ca)
            ps_d = psum("ps_d", [P, 512], ca)
            ps_w = psum("ps_w", [P, 512], ca)

            consts = ma("consts")
            edges_in = ma("edges_in")
            src_in = ma("src_in")
            idx_ready = [ma(f"idx_ready{c}") for c in range(3)]
            attr_in = [ma(f"attr_in{c}") for c in range(3)]
            gathered = [ma(f"gathered{j}") for j in range(TILES)]
            xs_in, xr_in, xT_in = ma("xs_in"), ma("xr_in"), ma("xT_in")

            pool_ready = ma("pool_ready")
            prep = ma("prep")
            bad_ready, bad_total, level_ready = ma("bad_ready"), ma("bad_total"), ma("level_ready")
            rel_ready = ma("rel_ready")
            edge_net = ma("edge_net")
            high = ma("high")
            message = ma("message")
            oh_ready = ma("oh_ready")
            summed = ma("summed")

            s_ready = ma("s_ready")
            s_turned = ma("s_turned")
            sT_ready = ma("sT_ready")
            dense = ma("dense")
            edge_dense = ma("edge_dense")
            dd = ma("dd")
            da = ma("da")
            stored = ma("stored")

            DD = 13
            DA = 4
            X_READ, HB_MADE = 5, 12

            N_CONST = 16 * 15

            def tile_cols(n, j, m=1):
                return bass.ds(n * TILES + j, m)

            def rows(ap, b):
                return ap[bass.ds(b * P, P), :]

            block = ca.enter_context(nc.Block())

            @block.sync
            def _(sp):
                sp.dma_start(dst_i[:, :, :].rearrange("p b j -> p (b j)"), dst).then_inc(edges_in, 16)
                sp.dma_start(src_all[:, :], src).then_inc(src_in, 16)
                sp.dma_start(w_sb[:, :], weight).then_inc(consts, 16)
                sp.dma_start(we1[0:ED, :], ee_w1).then_inc(consts, 16)
                sp.dma_start(we1[ED:ED + 1, :], ee_b1row).then_inc(consts, 16)
                sp.dma_start(ident[:, :], ident_in).then_inc(consts, 16)
                sp.dma_start(b01[:, :], bias01).then_inc(consts, 16)
                sp.dma_start(b02[:, :], bias02).then_inc(consts, 16)
                sp.dma_start(eb1[:, :], ee_b1).then_inc(consts, 16)
                sp.dma_start(eb2[:, :], ee_b2).then_inc(consts, 16)
                sp.dma_start(eps_raw[:, :], eps_in).then_inc(consts, 16)
                for k in range(KD):
                    sp.dma_start(w1T_sb[:, k, :], w1T[k * 128:(k + 1) * 128, :]).then_inc(consts, 16)
                    sp.dma_start(w2T_sb[:, k, :], w2T[k * 128:(k + 1) * 128, :]).then_inc(consts, 16)
                    sp.dma_start(we2[:, k, :], ee_w2[k * 128:(k + 1) * 128, :]).then_inc(consts, 16)

                def load_attr(n, c):
                    j, m = CHUNKS[c]
                    sp.nop(nofuse=True)
                    sp.dma_start(attr[0:ED, j * P:(j + m) * P],
                                 attrT[:, bass.ds((n * TILES + j) * P, m * P)]).then_inc(attr_in[c], 16)

                def load_near_attr(q, c):
                    wait(sp, edge_net, NP * (q - 1) + 3 * c + 3)
                    load_attr(q, c)

                def load_xs(b):
                    wait(sp, s_ready, b)
                    sp.nop(nofuse=True)
                    sp.dma_start(xs[:, :], rows(x, b)).then_inc(xs_in, 16)

                def load_xT(b):
                    wait(sp, dense, b)
                    sp.nop(nofuse=True)
                    sp.dma_start(xTb[:, :, :], xT[:, :, bass.ds(b * P, P)]).then_inc(xT_in, 16)

                def load_xr(b):
                    wait(sp, dd, DD * (b - 1) + X_READ)
                    sp.nop(nofuse=True)
                    sp.dma_start(xr[:, :], rows(x, b)).then_inc(xr_in, 16)

                def store(b):
                    sp.wait_ge(dd, DD * (b + 1))
                    sp.nop(nofuse=True)
                    sp.dma_start(rows(x1_dram, b), x1[:, :]).then_inc(stored, 16)
                    sp.dma_start(rows(table_dram, b), table[:, :, :].rearrange("p a d -> p (a d)").bitcast(F32))\
                      .then_inc(stored, 16)
                    sp.dma_start(rows(hbase_dram, b), hb[:, :]).then_inc(stored, 16)

                sp.wait_ge(level_ready, 1)
                lvl = sp.value_load(level[0:1, 0:1])
                with sp.If(lvl > 0):
                    for c in range(3):
                        load_near_attr(0, c)
                    load_xs(0)
                    load_xT(0)
                    load_xr(0)
                    for c in range(3):
                        load_near_attr(1, c)
                    def near_block(b):
                        load_near_attr(b + 1, 0)
                        load_xs(b)
                        load_near_attr(b + 1, 1)
                        if exists(b - 2):
                            store(b - 2)
                        load_xT(b)
                        load_near_attr(b + 1, 2)
                        load_xr(b)

                    for b in range(1, 3):
                        near_block(b)
                    with sp.Fori(3, BLOCKS - 1) as b:
                        near_block(b)
                    load_xs(BLOCKS - 1)
                    store(BLOCKS - 3)
                    load_xT(BLOCKS - 1)
                    load_xr(BLOCKS - 1)
                    store(BLOCKS - 2)
                    store(BLOCKS - 1)
                with sp.Else():
                    def general_block(b):
                        load_xs(b)
                        load_xT(b)
                        load_xr(b)
                        with sp.Fori(0, BLOCKS) as n:
                            for c in range(3):
                                sp.wait_ge(message, NP * (b * BLOCKS + n) + 3 * c + 3)
                                load_attr(n, c)
                        store(b)

                    general_block(0)
                    with sp.Fori(1, BLOCKS) as b:
                        general_block(b)
                sp.wait_ge(stored, 48 * BLOCKS)

            @block.gpsimd
            def _(pool):
                pool.iota(lane[:, :], [[1, 3 * P]], base=-P, channel_multiplier=0,
                          allow_small_or_imprecise_dtypes=True).then_inc(pool_ready, 1)
                pool.wait_ge(src_in, 16)
                pool.wait_ge(level_ready, 1)
                lvl = pool.value_load(level[0:1, 0:1])

                def stage_idx(n, c):
                    j0, m = CHUNKS[c]
                    pool.tensor_copy(idx[c][:, :], src_all[:, tile_cols(n, j0, m)]).then_inc(idx_ready[c], 1)

                def stage_near_idx(q, c):
                    j0, m = CHUNKS[c]
                    for j in range(j0, j0 + m):
                        wait(pool, gathered[j], 16 * q)
                    stage_idx(q, c)

                def gather_chunk(q, c, start=0):
                    j0, m = CHUNKS[c]
                    pool.wait_ge(idx_ready[c], q + 1)
                    pool.nop(nofuse=True)
                    for j in range(j0, j0 + m):
                        if j % 2 == 0:
                            wait(pool, message, start + NP * (q - 1) + j // 2 + 1)
                            pool.nop(nofuse=True)
                        pool.indirect_dma_start(
                            out=raw[:, j, :], out_offset=None, in_=x,
                            in_offset=bass.IndirectOffsetOnAxis(ap=idx[c][:, j - j0:j - j0 + 1], axis=0),
                        ).then_inc(gathered[j], 16)

                def near_span(q):
                    last = isinstance(q, int) and q == BLOCKS - 1
                    gather_chunk(q, 0)
                    stage_near_idx(q, 2)
                    gather_chunk(q, 1)
                    if not last:
                        stage_near_idx(q + 1, 0)
                    gather_chunk(q, 2)
                    if not last:
                        stage_near_idx(q + 1, 1)

                with pool.If(lvl > 0):
                    stage_near_idx(0, 0)
                    stage_near_idx(0, 1)
                    near_span(0)
                    with pool.Fori(1, BLOCKS - 1) as q:
                        near_span(q)
                    near_span(BLOCKS - 1)
                with pool.Else():
                    def general_block(b):
                        with pool.Fori(0, BLOCKS) as n:
                            q = b * BLOCKS + n
                            for c in range(3):
                                pool.wait_ge(message, NP * q + 3 * c + 3)
                                stage_idx(n, c)
                                gather_chunk(q, c, NP)

                    general_block(0)
                    with pool.Fori(1, BLOCKS) as b:
                        general_block(b)

            @block.tensor
            def _(pe):
                pe.wait_ge(bad_ready, 1)
                pe.matmul(ps_d[0:1, 0:len(EDGES)], ones_c[:, :], bad_sum[:, :], start=True, stop=True)\
                  .then_inc(bad_total, 1)
                pe.wait_ge(level_ready, 1)
                lvl = pe.value_load(level[0:1, 0:1])
                pe.wait_ge(consts, N_CONST)

                def edge_layer(q, k, start=0):
                    j0, m = PAIRS[k]
                    pe.wait_ge(attr_in[k // 3], 16 * (q + 1))
                    wait(pe, message, start + NP * q + k - 2)
                    for j in range(j0, j0 + m):
                        mm = pe.matmul(ps_e[k % 3][:, (j - j0) * D:(j - j0 + 1) * D],
                                       attr[:, j * P:(j + 1) * P], we1[:, :], start=True, stop=True)
                    mm.then_inc(edge_net, 1)

                def add_tile(j, slot, start, stop):
                    pe.matmul(ps_sum[:, :], oh[:, slot, :], msg[:, j, 0, :], start=start, stop=False,
                              skip_group_check=True)
                    return pe.matmul(ps_sum[:, :], oh[:, slot, :], msg[:, j, 1, :], start=False, stop=stop,
                                     skip_group_check=True)

                def near_step(path, b, c):
                    _, j0, m = path.steps[c]
                    first, last = near_sum_steps(b)[0], near_sum_steps(b)[-1]
                    if c == first:
                        wait(pe, s_ready, b)
                    pe.wait_ge(oh_ready, SUMS * b + c + 1)
                    if 2 <= c <= NP - 1:
                        pe.wait_ge(message, NP * b + c + 1)
                    elif c == 1 and first == 1:
                        pe.wait_ge(message, 2)
                    elif c == SUMS - 1:
                        pe.wait_ge(message, NP * (b + 1) + (path.edge + 1) // 2)
                    for j in range(j0, j0 + m):
                        mm = add_tile(j, path.slot[c] + j - j0, c == first and j == j0,
                                      c == last and j == j0 + m - 1)
                    mm.then_inc(summed, near_inc(b, c))

                def turn(b):
                    pe.wait_ge(s_ready, b + 1)
                    wait(pe, sT_ready, b)
                    for n in range(4):
                        mm = pe.transpose(ps_t[:, n * P:(n + 1) * P], s_r[:, n * 128:(n + 1) * 128], ident[:, :])
                    mm.then_inc(s_turned, 1)

                def products(b, part):
                    k = part % KD
                    if part < KD:
                        if k == 0:
                            pe.wait_ge(xT_in, 16 * (b + 1))
                            wait(pe, dd, DD * (b - 1) + 1)
                        pe.matmul(ps_d[:, 0:D], xTb[:, k, :], w1T_sb[:, k, :], start=(k == 0), stop=False)
                    elif part < 2 * KD:
                        if k == 0:
                            pe.wait_ge(sT_ready, b + 1)
                        mm = pe.matmul(ps_d[:, 0:D], sT[:, k * P:(k + 1) * P], w2T_sb[:, k, :], start=False,
                                       stop=(k == KD - 1))
                        if k == KD - 1:
                            mm.then_inc(dense, 1)
                    else:
                        if k == 0:
                            wait(pe, dd, DD * (b - 1) + HB_MADE)
                        mm = pe.matmul(ps_w[:, 0:D], sT[:, (KD + k) * P:(KD + k + 1) * P], we2[:, k, :],
                                       start=(k == 0), stop=(k == KD - 1))
                        if k == KD - 1:
                            mm.then_inc(edge_dense, 1)

                def near_block(path, b):
                    for s in range(NP):
                        k = s + LEAD
                        if k < NP:
                            edge_layer(b, k)
                        elif exists(b + 1):
                            edge_layer(b + 1, k - NP)
                        if s in near_sum_steps(b):
                            near_step(path, b, s)
                        if exists(b - 1) and s == 0:
                            turn(b - 1)
                        if exists(b - 1) and 1 <= s <= 6:
                            products(b - 1, s - 1)
                    if SUMS - 1 in near_sum_steps(b):
                        near_step(path, b, SUMS - 1)

                def near_program(path):
                    for k in range(LEAD):
                        edge_layer(0, k)
                    for b in range(3):
                        near_block(path, b)
                    with pe.Fori(3, BLOCKS - 1) as b:
                        near_block(path, b)
                    near_block(path, BLOCKS - 1)
                    turn(BLOCKS - 1)
                    for part in range(3 * KD):
                        products(BLOCKS - 1, part)

                def general_program():
                    pe.wait_ge(prep, 3)
                    pe.matmul(ps_sum[:, 0:D], zero_oh[:, :], eb1[:, :], start=True, stop=True,
                              skip_group_check=True).then_inc(summed, NP)

                    def general_block(b):
                        wait(pe, s_ready, b)
                        pe.matmul(ps_sum[:, 0:D], zero_oh[:, :], eb1[:, :], start=True, stop=False,
                                  skip_group_check=True)
                        pe.matmul(ps_sum[:, D:2 * D], zero_oh[:, :], eb1[:, :], start=False, stop=False,
                                  skip_group_check=True)
                        with pe.Fori(0, BLOCKS) as n:
                            q = b * BLOCKS + n
                            for k, (j0, m) in enumerate(PAIRS):
                                edge_layer(q, k, NP)
                                pe.wait_ge(oh_ready, NP * q + k + 1)
                                pe.wait_ge(message, NP * (q + 1) + k + 1)
                                for j in range(j0, j0 + m):
                                    mm = add_tile(j, j, False, False)
                                mm.then_inc(summed, 1)
                        turn(b)
                        for part in range(3 * KD):
                            products(b, part)

                    general_block(0)
                    with pe.Fori(1, BLOCKS) as b:
                        general_block(b)

                choose(pe, lvl, near_program, general_program)

            @block.scalar
            def _(act):
                act.wait_ge(prep, 2)
                act.activation(warm[:, :], ln_eps[:, :], ACT.Sqrt)
                act.wait_ge(consts, N_CONST)
                act.wait_ge(level_ready, 1)
                lvl = act.value_load(level[0:1, 0:1])

                def highs(path, q, n, k):
                    j0, m = PAIRS[k]
                    wait(act, summed, path.slot_free(q, k))
                    for j in range(j0, j0 + m):
                        act.wait_ge(gathered[j], 16 * (q + 1))
                        act.activation(msg[:, j, 0, 0:D], raw[:, j, :], ACT.Copy,
                                       scale=w_sb[:, tile_cols(n, j)])
                    act.wait_ge(edge_net, NP * q + k + 1)
                    act.activation(msg[:, j0:j0 + m, 0, D:2 * D],
                                   ps_e[k % 3][:, 0:m * D].rearrange("p (j d) -> p j d", d=D),
                                   ACT.Relu).then_inc(high, 1)

                def turned(b):
                    act.wait_ge(s_turned, b + 1)
                    wait(act, edge_dense, b)
                    act.activation(sT[:, :], ps_t[:, 0:4 * P], ACT.Copy).then_inc(sT_ready, 1)

                def norm(b):
                    act.wait_ge(dd, DD * b + 2)
                    act.activation(sq[:, :], o2[:, :], ACT.Square, accum_out=st[:, 0:1]).then_inc(da, 1)
                    act.wait_ge(da, DA * b + 1)
                    act.activation(st[:, 1:2], st[:, 0:1], ACT.Sqrt).then_inc(da, 1)

                def deviation(b):
                    act.wait_ge(dd, DD * b + 7)
                    act.activation(st[:, 5:6], st[:, 4:5], ACT.Sqrt, bias=ln_eps[:, :]).then_inc(da, 1)

                def table_high(b):
                    act.wait_ge(dd, DD * b + 10)
                    act.activation(table[:, 0, :], tb[:, :], ACT.Copy).then_inc(da, 1)

                def near_block(path, b):
                    for s in range(NP):
                        k = s + LEAD
                        if k < NP:
                            highs(path, b, b, k)
                        elif exists(b + 1):
                            highs(path, b + 1, b + 1, k - NP)
                        if exists(b - 2) and s == 0:
                            deviation(b - 2)
                        if exists(b - 1) and s == 0:
                            turned(b - 1)
                        if exists(b - 2) and s == 2:
                            table_high(b - 2)
                        if exists(b - 1) and s == 6:
                            norm(b - 1)

                def near_program(path):
                    for k in range(LEAD):
                        highs(path, 0, 0, k)
                    for b in range(3):
                        near_block(path, b)
                    with act.Fori(3, BLOCKS - 1) as b:
                        near_block(path, b)
                    near_block(path, BLOCKS - 1)
                    deviation(BLOCKS - 2)
                    table_high(BLOCKS - 2)
                    turned(BLOCKS - 1)
                    norm(BLOCKS - 1)
                    deviation(BLOCKS - 1)
                    table_high(BLOCKS - 1)

                def general_program():
                    def general_block(b):
                        with act.Fori(0, BLOCKS) as n:
                            for k in range(NP):
                                highs(General, b * BLOCKS + n, n, k)
                        turned(b)
                        norm(b)
                        deviation(b)
                        table_high(b)

                    general_block(0)
                    with act.Fori(1, BLOCKS) as b:
                        general_block(b)

                choose(act, lvl, near_program, general_program)

            @block.vector
            def _(dve):
                dve.memset(ones_c[:, :], 1.0).then_inc(prep, 1)
                dve.memset(ln_eps[:, :], LN_EPS).then_inc(prep, 1)
                dve.memset(zero_oh[:, :], 0.0).then_inc(prep, 1)
                dve.memset(attr[ED:ED + 1, :], 1.0).then_inc(prep, 1)
                dve.wait_ge(edges_in, 16)
                dve.tensor_copy(dst_f[:, :, :], dst_i[:, :, :]).then_inc(prep, 1)
                dve.wait_ge(prep, 5)
                for b in range(BLOCKS):
                    dve.tensor_scalar(rel[:, b, :], dst_f[:, b, :], float(-P * b), None, ALU.add).then_inc(prep, 1)
                dve.wait_ge(prep, 5 + BLOCKS)
                for n, edge in enumerate(EDGES):
                    lim = TILES - edge
                    dve.tensor_scalar(bad[:, n, :, 0:edge], rel[:, :, 0:edge], float(-P), None, ALU.is_lt)
                    dve.tensor_scalar(bad[:, n, :, edge:TILES], rel[:, :, edge:TILES], 0.0, None, ALU.is_lt)\
                       .then_inc(prep, 1)
                    dve.wait_ge(prep, 6 + BLOCKS + 2 * n)
                    dve.scalar_tensor_tensor(bad[:, n, :, 0:lim], rel[:, :, 0:lim], float(P), bad[:, n, :, 0:lim],
                                             ALU.is_ge, ALU.add)
                    dve.scalar_tensor_tensor(bad[:, n, :, lim:TILES], rel[:, :, lim:TILES], float(2 * P),
                                             bad[:, n, :, lim:TILES], ALU.is_ge, ALU.add).then_inc(prep, 1)
                    dve.wait_ge(prep, 7 + BLOCKS + 2 * n)
                dve.reduce_sum(bad_sum[:, :], bad[:, :, :, :].rearrange("p n b j -> p n (b j)"), AX_X)\
                   .then_inc(bad_ready, 1)
                n_prep = 5 + BLOCKS + 2 * len(EDGES)
                dve.wait_ge(consts, N_CONST)
                dve.tensor_scalar(r0[:, :], eb1[:, :], 0.0, None, ALU.max).then_inc(prep, 1)
                dve.wait_ge(bad_total, 1)
                dve.tensor_scalar(holds[:, :], ps_d[0:1, 0:len(EDGES)], 0.0, None, ALU.is_equal).then_inc(prep, 1)
                dve.wait_ge(prep, n_prep + 2)
                dve.tensor_tensor(level[:, :], holds[:, 0:1], holds[:, 1:2], ALU.add).then_inc(level_ready, 1)
                dve.tensor_tensor(b12[:, :], b01[:, :], b02[:, :], ALU.add).then_inc(prep, 1)
                dve.tensor_scalar(eps_t[:, :], eps_raw[:, :], 1.0, None, ALU.add).then_inc(prep, 1)
                dve.wait_ge(prep, n_prep + 4)
                dve.wait_ge(pool_ready, 1)
                dve.wait_ge(level_ready, 1)
                lvl = dve.value_load(level[0:1, 0:1])

                def near_oh(path, b, group):
                    steps = [c for c in range(OH_GROUPS[group][0], OH_GROUPS[group][1] + 1) if c in near_sum_steps(b)]
                    if not steps:
                        return
                    wait(dve, summed, SUMS * (b - 1) + steps[-1] + 1)
                    span, j0, _ = path.steps[steps[0]]
                    m = sum(path.steps[c][2] for c in steps)
                    equal(dve, oh[:, path.slot[steps[0]]:path.slot[steps[0]] + m, :],
                          lane[:, (1 - span) * P:(2 - span) * P], rel2[:, tile_cols(b + span, j0, m)], m)\
                        .then_inc(oh_ready, sum(near_inc(b, c) for c in steps))

                rel2 = rel[:, :, :].rearrange("p b j -> p (b j)")
                dst2 = dst_f[:, :, :].rearrange("p b j -> p (b j)")

                def low_neighbour(n, j):
                    dve.scalar_tensor_tensor(msg[:, j, 1, 0:D], raw[:, j, :], w_sb[:, tile_cols(n, j)],
                                             msg[:, j, 0, 0:D].bitcast(F32), ALU.mult, ALU.subtract)

                def low_edge(k):
                    j0, m = PAIRS[k]
                    dve.scalar_tensor_tensor(msg[:, j0:j0 + m, 1, D:2 * D],
                                             ps_e[k % 3][:, 0:m * D].rearrange("p (j d) -> p j d", d=D), 0.0,
                                             msg[:, j0:j0 + m, 0, D:2 * D].bitcast(F32), ALU.max, ALU.subtract)\
                       .then_inc(message, 1)

                def take_s(b, steps):
                    dve.wait_ge(summed, steps)
                    dve.wait_ge(xs_in, 16 * (b + 1))
                    wait(dve, s_turned, b)
                    dve.scalar_tensor_tensor(s_r[:, 0:D], xs[:, :], 1.0, ps_sum[:, 0:D], ALU.add, ALU.mult)
                    dve.tensor_tensor(s_r[:, D:2 * D], ps_sum[:, D:2 * D], r0[:, :], ALU.add).then_inc(s_ready, 1)

                def tail(b, n):
                    at = DD * b
                    if n == 1:
                        dve.wait_ge(dense, b + 1)
                        ins = dve.tensor_tensor(o[:, :], ps_d[:, 0:D], b12[:, :], ALU.add)
                    elif n == 2:
                        dve.wait_ge(dd, at + 1)
                        wait(dve, da, DA * b)
                        ins = dve.scalar_tensor_tensor(o2[:, :], o[:, :], SLOPE, o[:, :], ALU.mult, ALU.max)
                    elif n == 3:
                        dve.wait_ge(da, DA * b + 2)
                        ins = dve.tensor_scalar(st[:, 2:3], st[:, 1:2], NORM_EPS, None, ALU.max)
                    elif n == 4:
                        dve.wait_ge(dd, at + 3)
                        ins = dve.reciprocal(st[:, 3:4], st[:, 2:3])
                    elif n == X_READ:
                        dve.wait_ge(dd, at + 4)
                        dve.wait_ge(xr_in, 16 * (b + 1))
                        ins = dve.scalar_tensor_tensor(y[:, :], o2[:, :], st[:, 3:4], xr[:, :], ALU.mult, ALU.add)
                    elif n == 6:
                        dve.wait_ge(dd, at + 5)
                        ins = dve.bn_stats(bn6[:, :], y[:, :])
                    elif n == 7:
                        dve.wait_ge(dd, at + 6)
                        dve.nop(nofuse=True)
                        ins = dve.bn_aggr(st[:, 3:5], bn6[:, :])
                    elif n == 8:
                        dve.wait_ge(da, DA * b + 3)
                        ins = dve.reciprocal(st[:, 6:7], st[:, 5:6])
                    elif n == 9:
                        dve.wait_ge(dd, at + 8)
                        wait(dve, stored, 48 * b)
                        ins = dve.tensor_scalar(x1[:, :], y[:, :], st[:, 3:4], st[:, 6:7], ALU.subtract, ALU.mult)
                    elif n == 10:
                        dve.wait_ge(dd, at + 9)
                        ins = dve.tensor_tensor(tb[:, :], x1[:, :], eb2[:, :], ALU.add)
                    elif n == 11:
                        dve.wait_ge(dd, at + 10)
                        ins = dve.scalar_tensor_tensor(u[:, :], x1[:, :], eps_t[:, :], tb[:, :], ALU.mult, ALU.add)
                    elif n == HB_MADE:
                        dve.wait_ge(dd, at + 11)
                        dve.wait_ge(edge_dense, b + 1)
                        ins = dve.tensor_tensor(hb[:, :], ps_w[:, 0:D], u[:, :], ALU.add)
                    else:
                        dve.wait_ge(da, DA * b + 4)
                        ins = dve.tensor_tensor(table[:, 1, :], tb[:, :], table[:, 0, :].bitcast(F32), ALU.subtract)
                    ins.then_inc(dd, 1)

                TAIL_1 = {(5, 1): 1, (5, 2): 2, (6, 2): 3, (7, 0): 4, (7, 1): 5, (8, 0): 6, (8, 1): 7}
                TAIL_2 = {(0, 2): 8, (1, 0): 9, (1, 2): 10, (2, 1): 11, (3, 0): 12, (3, 2): 13}
                OH_AT = {0: 2, 2: 3, 4: 4, 5: 5}

                def near_block(path, b):
                    def fill(s, place):
                        if exists(b - 1) and (s, place) in TAIL_1:
                            tail(b - 1, TAIL_1[s, place])
                        if exists(b - 2) and (s, place) in TAIL_2:
                            tail(b - 2, TAIL_2[s, place])

                    if exists(b - 1):
                        take_s(b - 1, SUMS * b)
                    for s in range(NP):
                        if s in OH_AT:
                            near_oh(path, b, OH_AT[s])
                        q, k = (b, s + LEAD) if s + LEAD < NP else (b + 1, s + LEAD - NP)
                        j0, m = PAIRS[k]
                        if exists(q):
                            dve.wait_ge(high, NP * q + k + 1)
                            low_neighbour(q, j0)
                        fill(s, 0)
                        if exists(q) and m == 2:
                            low_neighbour(q, j0 + 1)
                        fill(s, 1)
                        if exists(q):
                            low_edge(k)
                        fill(s, 2)
                        if s in (6, 7) and exists(b + 1):
                            near_oh(path, b + 1, s - 6)

                def near_program(path):
                    for k in range(LEAD):
                        dve.wait_ge(high, k + 1)
                        for j in range(PAIRS[k][0], PAIRS[k][0] + PAIRS[k][1]):
                            low_neighbour(0, j)
                        low_edge(k)
                    near_oh(path, 0, 1)
                    for b in range(3):
                        near_block(path, b)
                    with dve.Fori(3, BLOCKS - 1) as b:
                        near_block(path, b)
                    near_block(path, BLOCKS - 1)
                    for n in range(8, DD + 1):
                        tail(BLOCKS - 2, n)
                    take_s(BLOCKS - 1, SUMS * BLOCKS)
                    for n in range(1, DD + 1):
                        tail(BLOCKS - 1, n)

                def general_program():
                    dve.memset(bad[0:1, 0:1, 0:1, 0:1], 0.0).then_inc(message, NP)

                    def general_block(b):
                        with dve.Fori(0, BLOCKS) as n:
                            q = b * BLOCKS + n
                            for k, (j0, m) in enumerate(PAIRS):
                                dve.wait_ge(summed, NP * q + k + 1)
                                equal(dve, oh[:, j0:j0 + m, :], lane[:, P:2 * P], dst2[:, tile_cols(n, j0, m)], m)\
                                    .then_inc(oh_ready, 1)
                                dve.wait_ge(high, NP * q + k + 1)
                                for j in range(j0, j0 + m):
                                    low_neighbour(n, j)
                                low_edge(k)
                        dve.wait_ge(oh_ready, NP * BLOCKS * (b + 1))
                        dve.tensor_scalar(dst_f[:, :, :], dst_f[:, :, :], float(-P), None, ALU.add)\
                           .then_inc(rel_ready, 1)
                        dve.wait_ge(rel_ready, b + 1)
                        take_s(b, NP * BLOCKS * (b + 1) + NP)
                        for n in range(1, DD + 1):
                            tail(b, n)

                    general_block(0)
                    with dve.Fori(1, BLOCKS) as b:
                        general_block(b)

                choose(dve, lvl, near_program, general_program)

        with ExitStack() as cb:
            def s2(name, shape, dt):
                return sb(name, shape, dt, cb)

            def m2(name):
                return sem(name, cb)

            w1m = s2("w1m", [128, 2, KD, H], F32R)
            w2m = s2("w2m", [128, 2, KH, H], F32R)
            w3m = s2("w3m", [128, 2, KH, D], F32R)
            STAGE = 3
            stage = [s2(f"stage{n}", [128, H], F32) for n in range(STAGE)]
            b1m = s2("b1m", [128, H], F32R)
            b2m = s2("b2m", [128, H], F32R)
            b3m = s2("b3m", [128, D], F32R)
            ones_f = s2("ones_f", [128, P], F32)
            ones_r = s2("ones_r", [128, P], F32R)
            g1, be1 = s2("g1", [128, KH], F32), s2("be1", [128, KH], F32)
            g2, be2 = s2("g2", [128, KH], F32), s2("be2", [128, KH], F32)
            bng, bnb = s2("bng", [P, D], F32), s2("bnb", [P, D], F32)
            idx2 = [s2(f"idx2_{c}", [P, m], I32) for c, (_, m) in enumerate(CHUNKS)]
            grow = s2("grow", [P, TILES, 2 * D], F32R)
            oh2 = s2("oh2", [P, OH_SLOTS, P], F32R)
            zero2 = s2("zero2", [P, P], F32)
            zrow = s2("zrow", [P, D], F32)
            hbx = s2("hbx", [P, D], F32)
            x1f = s2("x1f", [P, D], F32)
            h = s2("h", [P, D], F32)
            hT = s2("hT", [128, 2, KD * P], F32R)
            zn = s2("zn", [P, H], F32)
            aF = s2("aF", [128, KH, P], F32)
            a1 = s2("a1", [128, 2, KH, P], F32R)
            a2 = s2("a2", [128, 2, KH, P], F32R)
            bs = [s2(f"bs{n}", [P, 2, 6], F32) for n in range(2)]
            mv = [s2(f"mv{n}", [P, 8], F32) for n in range(2)]
            fs = s2("fs", [P, 6], F32)
            fm = s2("fm", [P, 8], F32)
            t = s2("t", [P, D], F32)
            v = s2("v", [P, D], F32)
            res = s2("res", [P, D], F32)

            ps_s = psum("ps_s", [P, 512], cb)
            ps_z = [psum(f"ps_z{n}", [P, 2, 512], cb) for n in range(2)]
            ps_tr = psum("ps_tr", [128, 2, 512], cb)
            ps_y = psum("ps_y", [P, 512], cb)

            consts2 = m2("consts2")
            w_in = [m2(f"w_in{n}") for n in range(STAGE)]
            w_high, w_ready = m2("w_high"), m2("w_ready")
            prep2, prep_ones = m2("prep2"), m2("prep_ones")
            rebased = m2("rebased")
            split_high = [m2(f"split_high{n}") for n in range(2)]
            idx2_ready = [m2(f"idx2_ready{c}") for c in range(3)]
            got = [m2(f"got{j}") for j in range(TILES)]
            hb_in, x1_in = m2("hb_in"), m2("x1_in")
            oh2_ready = m2("oh2_ready")
            sum_done = m2("sum_done")
            h_ready = m2("h_ready")
            h_turned = m2("h_turned")
            hT_high, hT_ready = m2("hT_high"), m2("hT_ready")
            z_done = [m2(f"z_done{n}") for n in range(2)]
            ln = [m2(f"ln{n}") for n in range(2)]
            std = [m2(f"std{n}") for n in range(2)]
            zn_ready = [m2(f"zn_ready{n}") for n in range(2)]
            turned2 = [m2(f"turned2_{n}") for n in range(2)]
            relu_out = [m2(f"relu_out{n}") for n in range(2)]
            a_ready = [m2(f"a_ready{n}") for n in range(2)]
            y_done = m2("y_done")
            fin = m2("fin")
            fstd = m2("fstd")
            out_stored = m2("out_stored")
            LN = 5
            FIN = 12

            pieces = [(m_w1[k * 128:(k + 1) * 128, :], w1m[:, :, k, :]) for k in range(KD)]
            pieces += [(m_w2[k * 128:(k + 1) * 128, :], w2m[:, :, k, :]) for k in range(KH)]
            pieces += [(m_w3[k * 512:(k + 1) * 512, :].rearrange("(k p) d -> p k d", p=128), w3m[:, :, 4 * k:4 * k + 4, :])
                       for k in range(KH // 4)]
            biases = [(m_b1, b1m, H), (m_b2, b2m, H), (m_b3, b3m, D)]
            N_SPLIT = len(pieces) + len(biases)

            def pick(dest, part):
                return dest[:, part]

            def as_piece(tile, dest):
                return tile if len(dest.shape) == 3 else tile.rearrange("p (k d) -> p k d", d=D)

            block2 = cb.enter_context(nc.Block())

            @block2.sync
            def _(sp):
                lvl = sp.value_load(level[0:1, 0:1])

                def load_hb(b):
                    wait(sp, h_ready, b)
                    sp.nop(nofuse=True)
                    sp.dma_start(hbx[:, :], rows(hbase_dram, b)).then_inc(hb_in, 16)

                def load_x1(b):
                    wait(sp, fin, FIN * b)
                    sp.nop(nofuse=True)
                    sp.dma_start(x1f[:, :], rows(x1_dram, b)).then_inc(x1_in, 16)

                def store(b):
                    sp.wait_ge(fin, FIN * (b + 1))
                    sp.nop(nofuse=True)
                    sp.dma_start(rows(out, b), res[:, :]).then_inc(out_stored, 16)

                def load_weights():
                    for tile, source in ((g1, m_g1), (be1, m_be1), (g2, m_g2), (be2, m_be2), (bng, bn_g), (bnb, bn_b)):
                        sp.dma_start(tile[:, :], source).then_inc(consts2, 16)
                    for n, (source, dest) in enumerate(pieces):
                        wait(sp, w_ready, n - STAGE + 1)
                        sp.dma_start(as_piece(stage[n % STAGE][:, :], dest), source).then_inc(w_in[n % STAGE], 16)
                    for n, (source, dest, width) in enumerate(biases, len(pieces)):
                        wait(sp, w_ready, n - STAGE + 1)
                        for row in (0, 32):
                            sp.dma_start(stage[n % STAGE][row:row + 1, 0:width], source).then_inc(w_in[n % STAGE], 16)

                def iteration(i):
                    if exists(i):
                        load_hb(i)
                    if exists(i - 3):
                        load_x1(i - 3)
                    if exists(i - 4):
                        store(i - 4)

                load_weights()
                with sp.If(lvl > 0):
                    for i in range(4):
                        iteration(i)
                    with sp.Fori(4, BLOCKS) as i:
                        iteration(i)
                    for i in range(BLOCKS, BLOCKS + 4):
                        iteration(i)
                with sp.Else():
                    def general_block(b):
                        load_hb(b)
                        load_x1(b)
                        store(b)

                    general_block(0)
                    with sp.Fori(1, BLOCKS) as b:
                        general_block(b)
                sp.wait_ge(out_stored, 16 * BLOCKS)

            @block2.gpsimd
            def _(pool):
                lvl = pool.value_load(level[0:1, 0:1])

                def stage_idx(n, c):
                    j0, m = CHUNKS[c]
                    pool.tensor_copy(idx2[c][:, :], src_all[:, tile_cols(n, j0, m)]).then_inc(idx2_ready[c], 1)

                def stage_near_idx(q, c):
                    j0, m = CHUNKS[c]
                    for j in range(j0, j0 + m):
                        wait(pool, got[j], 16 * q)
                    stage_idx(q, c)

                def gather_chunk(path, q, c):
                    j0, m = CHUNKS[c]
                    pool.wait_ge(idx2_ready[c], q + 1)
                    pool.nop(nofuse=True)
                    for j in range(j0, j0 + m):
                        if j % 2 == 0:
                            wait(pool, sum_done, path.slot_free(q, j // 2))
                            pool.nop(nofuse=True)
                        pool.indirect_dma_start(
                            out=grow[:, j, :].bitcast(F32), out_offset=None, in_=table_dram,
                            in_offset=bass.IndirectOffsetOnAxis(ap=idx2[c][:, j - j0:j - j0 + 1], axis=0),
                        ).then_inc(got[j], 16)

                def near_span(path, q):
                    last = isinstance(q, int) and q == BLOCKS - 1
                    gather_chunk(path, q, 0)
                    stage_near_idx(q, 2)
                    gather_chunk(path, q, 1)
                    if not last:
                        stage_near_idx(q + 1, 0)
                    gather_chunk(path, q, 2)
                    if not last:
                        stage_near_idx(q + 1, 1)

                def near_program(path):
                    stage_near_idx(0, 0)
                    stage_near_idx(0, 1)
                    near_span(path, 0)
                    with pool.Fori(1, BLOCKS - 1) as q:
                        near_span(path, q)
                    near_span(path, BLOCKS - 1)

                def general_program():
                    def general_block(b):
                        with pool.Fori(0, BLOCKS) as n:
                            q = b * BLOCKS + n
                            for c in range(3):
                                pool.wait_ge(sum_done, General.slot_free(q, (CHUNKS[c][0] + CHUNKS[c][1] - 1) // 2))
                                stage_idx(n, c)
                                gather_chunk(General, q, c)

                    general_block(0)
                    with pool.Fori(1, BLOCKS) as b:
                        general_block(b)

                choose(pool, lvl, near_program, general_program)

            @block2.tensor
            def _(pe):
                lvl = pe.value_load(level[0:1, 0:1])
                pe.wait_ge(prep2, 3)

                def add_tile(j, slot, start, stop):
                    pe.matmul(ps_s[:, 0:D], oh2[:, slot, :], grow[:, j, 0:D], start=start, stop=False,
                              skip_group_check=True)
                    return pe.matmul(ps_s[:, 0:D], oh2[:, slot, :], grow[:, j, D:2 * D], start=False, stop=stop,
                                     skip_group_check=True)

                def near_step(path, b, c):
                    span, j0, m = path.steps[c]
                    first, last = near_sum_steps(b)[0], near_sum_steps(b)[-1]
                    if c == first:
                        wait(pe, h_ready, b)
                    pe.wait_ge(oh2_ready, SUMS * b + c + 1)
                    for j in range(j0, j0 + m):
                        pe.wait_ge(got[j], 16 * (b + span + 1))
                        mm = add_tile(j, path.slot[c] + j - j0, c == first and j == j0,
                                      c == last and j == j0 + m - 1)
                    mm.then_inc(sum_done, near_inc(b, c))

                def turn_h(path, b):
                    pe.wait_ge(h_ready, b + 1)
                    wait(pe, relu_out[1], 2 * path.t2_before_t1(b))
                    for k in range(KD):
                        mm = pe.transpose(ps_tr[:, 0, k * P:(k + 1) * P], h[:, k * 128:(k + 1) * 128], ident[:, :])
                    mm.then_inc(h_turned, 1)

                def three(acc, left, right, start, stop):
                    for n, (a, b) in enumerate(((0, 0), (0, 1), (1, 0))):
                        mm = pe.matmul(acc, left(a), right(b), start=start and n == 0, stop=stop and n == 2,
                                       skip_group_check=True)
                    return mm

                def layer1(b):
                    pe.wait_ge(hT_ready, b + 1)
                    wait(pe, zn_ready[0], 2 * b)
                    for n in range(2):
                        cols = slice(n * 512, (n + 1) * 512)
                        pe.matmul(ps_z[0][:, n, :], ones_r[:, :], b1m[:, cols], start=True, stop=False,
                                  skip_group_check=True)
                        for k in range(KD):
                            mm = three(ps_z[0][:, n, :], lambda a: hT[:, a, k * P:(k + 1) * P],
                                       lambda a: w1m[:, a, k, cols], False, k == KD - 1)
                        mm.then_inc(z_done[0], 1)

                def layer2(b, n):
                    if n == 0:
                        pe.wait_ge(a_ready[0], 2 * (b + 1))
                        wait(pe, zn_ready[1], 2 * b)
                    cols = slice(n * 512, (n + 1) * 512)
                    pe.matmul(ps_z[1][:, n, :], ones_r[:, :], b2m[:, cols], start=True, stop=False,
                              skip_group_check=True)
                    for k in range(KH):
                        mm = three(ps_z[1][:, n, :], lambda a: a1[:, a, k, :], lambda a: w2m[:, a, k, cols],
                                   False, k == KH - 1)
                    mm.then_inc(z_done[1], 1)

                def layer3(b, part):
                    if part == 0:
                        wait(pe, fin, FIN * b)
                        pe.wait_ge(a_ready[1], 2 * b + 1)
                        pe.matmul(ps_y[:, 0:D], ones_r[:, :], b3m[:, :], start=True, stop=False,
                                  skip_group_check=True)
                    else:
                        pe.wait_ge(a_ready[1], 2 * b + 2)
                    for k in range(4 * part, 4 * part + 4):
                        mm = three(ps_y[:, 0:D], lambda a: a2[:, a, k, :], lambda a: w3m[:, a, k, :],
                                   False, k == KH - 1)
                    if part == 1:
                        mm.then_inc(y_done, 1)

                def turn_z(path, layer, b):
                    if layer == 0:
                        pe.wait_ge(hT_ready, b + 1)
                    else:
                        pe.wait_ge(relu_out[0], 2 * path.t1_before_t2(b))
                    for half in range(2):
                        pe.wait_ge(zn_ready[layer], 2 * b + half + 1)
                        for c in range(4):
                            k = 4 * half + c
                            mm = pe.transpose(ps_tr[:, half, c * P:(c + 1) * P], zn[:, k * 128:(k + 1) * 128],
                                              ident[:, :])
                        mm.then_inc(turned2[layer], 1)

                def iteration(path, i):
                    if exists(i - 1):
                        layer1(i - 1)
                    if exists(i - 2):
                        layer2(i - 2, 0)
                    if exists(i - 1):
                        turn_z(path, 0, i - 1)
                    if exists(i - 2):
                        layer2(i - 2, 1)
                    if exists(i):
                        steps = near_sum_steps(i)
                        for c in steps:
                            if c < 5:
                                near_step(path, i, c)
                    if exists(i - 2):
                        turn_z(path, 1, i - 2)
                    if exists(i):
                        for c in steps:
                            if c >= 5:
                                near_step(path, i, c)
                    if exists(i - 2):
                        layer3(i - 2, 0)
                    if exists(i):
                        turn_h(path, i)
                    if exists(i - 2):
                        layer3(i - 2, 1)

                def near_program(path):
                    iteration(path, 0)
                    pe.wait_ge(w_ready, N_SPLIT)
                    for i in range(1, 3):
                        iteration(path, i)
                    with pe.Fori(3, BLOCKS - 1) as i:
                        iteration(path, i)
                    for i in range(BLOCKS - 1, BLOCKS + 2):
                        iteration(path, i)

                def general_program():
                    pe.wait_ge(w_ready, N_SPLIT)
                    pe.matmul(ps_s[:, 0:D], zero2[:, :], zrow[:, :], start=True, stop=True,
                              skip_group_check=True).then_inc(sum_done, NP)
                    def general_block(b):
                        wait(pe, h_ready, b)
                        pe.matmul(ps_s[:, 0:D], zero2[:, :], zrow[:, :], start=True, stop=False,
                                  skip_group_check=True)
                        with pe.Fori(0, BLOCKS) as n:
                            q = b * BLOCKS + n
                            for k, (j0, m) in enumerate(PAIRS):
                                pe.wait_ge(oh2_ready, NP * q + k + 1)
                                for j in range(j0, j0 + m):
                                    pe.wait_ge(got[j], 16 * (q + 1))
                                    mm = add_tile(j, j, False, False)
                                mm.then_inc(sum_done, 1)
                        turn_h(General, b)
                        layer1(b)
                        turn_z(General, 0, b)
                        layer2(b, 0)
                        layer2(b, 1)
                        turn_z(General, 1, b)
                        layer3(b, 0)
                        layer3(b, 1)

                    general_block(0)
                    with pe.Fori(1, BLOCKS) as b:
                        general_block(b)

                choose(pe, lvl, near_program, general_program)

            @block2.scalar
            def _(act):
                lvl = act.value_load(level[0:1, 0:1])
                for n, (source, dest) in enumerate(pieces):
                    act.wait_ge(w_in[n % STAGE], 16 * (n // STAGE + 1))
                    act.activation(pick(dest, 0), as_piece(stage[n % STAGE][:, :], dest), ACT.Copy)\
                       .then_inc(w_high, 1)
                act.wait_ge(prep2, 5)
                for n, (source, dest, width) in enumerate(biases, len(pieces)):
                    act.wait_ge(w_in[n % STAGE], 16 * (n // STAGE + 2))
                    act.activation(dest[0:1, :], stage[n % STAGE][0:1, 0:width], ACT.Copy)
                    act.activation(dest[32:33, :], stage[n % STAGE][32:33, 0:width], ACT.Copy).then_inc(w_high, 1)
                act.wait_ge(consts2, 96)

                def h_high(b):
                    act.wait_ge(h_turned, b + 1)
                    wait(act, z_done[0], 2 * b)
                    act.activation(hT[:, 0, :], ps_tr[:, 0, 0:KD * P], ACT.Copy).then_inc(hT_high, 1)

                def deviation(layer, b):
                    act.wait_ge(ln[layer], LN * b + 3)
                    act.activation(mv[layer][:, 2:3], mv[layer][:, 1:2], ACT.Sqrt, bias=ln_eps[:, :])\
                       .then_inc(std[layer], 1)

                def normalize(path, layer, b):
                    act.wait_ge(ln[layer], LN * (b + 1))
                    if layer == 0:
                        wait(act, turned2[1], 2 * path.t2_before_t1(b))
                    else:
                        act.wait_ge(turned2[0], 2 * path.t1_before_t2(b))
                    for n in range(2):
                        act.activation(zn[:, n * 512:(n + 1) * 512], ps_z[layer][:, n, :], ACT.Identity,
                                       bias=mv[layer][:, 4:5], scale=mv[layer][:, 3:4]).then_inc(zn_ready[layer], 1)

                def relu(path, layer, b):
                    gg, bb = ((g1, be1), (g2, be2))[layer]
                    if layer == 0:
                        wait(act, a_ready[1], 2 * path.t2_before_t1(b))
                    else:
                        act.wait_ge(a_ready[0], 2 * path.t1_before_t2(b))
                    for half in range(2):
                        act.wait_ge(turned2[layer], 2 * b + half + 1)
                        for c in range(4):
                            k = 4 * half + c
                            ins = act.activation(aF[:, k, :], ps_tr[:, half, c * P:(c + 1) * P], ACT.Relu,
                                                 bias=bb[:, k:k + 1], scale=gg[:, k:k + 1])
                        ins.then_inc(relu_out[layer], 1)

                def finish_std(b, n):
                    act.wait_ge(fin, FIN * b + (3, 10)[n])
                    act.activation(fm[:, 2 + n:3 + n], fm[:, 1:2] if n == 0 else fm[:, 5:6], ACT.Sqrt,
                                   bias=ln_eps[:, :]).then_inc(fstd, 1)

                def iteration(path, i):
                    if exists(i - 3):
                        finish_std(i - 3, 0)
                    if exists(i - 1):
                        deviation(0, i - 1)
                        normalize(path, 0, i - 1)
                    if exists(i - 3):
                        finish_std(i - 3, 1)
                    if exists(i - 1):
                        relu(path, 0, i - 1)
                    if exists(i - 2):
                        deviation(1, i - 2)
                        normalize(path, 1, i - 2)
                        relu(path, 1, i - 2)
                    if exists(i):
                        h_high(i)

                def near_program(path):
                    for i in range(3):
                        iteration(path, i)
                    with act.Fori(3, BLOCKS) as i:
                        iteration(path, i)
                    for i in range(BLOCKS, BLOCKS + 3):
                        iteration(path, i)

                def general_program():
                    def general_block(b):
                        h_high(b)
                        for layer in range(2):
                            deviation(layer, b)
                            normalize(General, layer, b)
                            relu(General, layer, b)
                        finish_std(b, 0)
                        finish_std(b, 1)

                    general_block(0)
                    with act.Fori(1, BLOCKS) as b:
                        general_block(b)

                choose(act, lvl, near_program, general_program)

            @block2.vector
            def _(dve):
                dve.memset(zero2[:, :], 0.0).then_inc(prep2, 1)
                dve.memset(zrow[:, :], 0.0).then_inc(prep2, 1)
                dve.memset(ones_f[:, :], 1.0).then_inc(prep_ones, 1)
                dve.wait_ge(prep_ones, 1)
                dve.tensor_copy(ones_r[:, :], ones_f[:, :]).then_inc(prep2, 1)
                dve.memset(b1m[:, :].bitcast(F32), 0.0)
                dve.memset(b2m[:, :].bitcast(F32), 0.0).then_inc(prep2, 1)
                dve.memset(b3m[:, :].bitcast(F32), 0.0).then_inc(prep2, 1)
                lvl = dve.value_load(level[0:1, 0:1])
                for n, (source, dest) in enumerate(pieces):
                    dve.wait_ge(w_high, n + 1)
                    dve.tensor_tensor(pick(dest, 1), as_piece(stage[n % STAGE][:, :], dest),
                                      pick(dest, 0).bitcast(F32), ALU.subtract).then_inc(w_ready, 1)
                for n, (source, dest, width) in enumerate(biases, len(pieces)):
                    dve.wait_ge(w_high, n + 1)
                    dve.tensor_tensor(dest[32:33, :], stage[n % STAGE][32:33, 0:width],
                                      dest[32:33, :].bitcast(F32), ALU.subtract).then_inc(w_ready, 1)
                dve.wait_ge(consts2, 96)
                rel2 = rel[:, :, :].rearrange("p b j -> p (b j)")
                dst2 = dst_f[:, :, :].rearrange("p b j -> p (b j)")

                def near_oh(path, b, group):
                    steps = [c for c in range(OH_GROUPS[group][0], OH_GROUPS[group][1] + 1) if c in near_sum_steps(b)]
                    if not steps:
                        return
                    wait(dve, sum_done, SUMS * (b - 1) + steps[-1] + 1)
                    span, j0, _ = path.steps[steps[0]]
                    m = sum(path.steps[c][2] for c in steps)
                    equal(dve, oh2[:, path.slot[steps[0]]:path.slot[steps[0]] + m, :],
                          lane[:, (1 - span) * P:(2 - span) * P], rel2[:, tile_cols(b + span, j0, m)], m)\
                        .then_inc(oh2_ready, sum(near_inc(b, c) for c in steps))

                def take_h(b, steps):
                    dve.wait_ge(sum_done, steps)
                    dve.wait_ge(hb_in, 16 * (b + 1))
                    wait(dve, h_turned, b)
                    dve.tensor_tensor(h[:, :], ps_s[:, 0:D], hbx[:, :], ALU.add).then_inc(h_ready, 1)

                def h_low(b):
                    dve.wait_ge(hT_high, b + 1)
                    dve.tensor_tensor(hT[:, 1, :], ps_tr[:, 0, 0:KD * P], hT[:, 0, :].bitcast(F32), ALU.subtract)\
                       .then_inc(hT_ready, 1)

                def stats(layer, b, n):
                    dve.wait_ge(z_done[layer], 2 * b + n + 1)
                    dve.bn_stats(bs[layer][:, n, :], ps_z[layer][:, n, :]).then_inc(ln[layer], 1)

                def aggregate(out_, in_, s, value):
                    dve.wait_ge(s, value)
                    dve.nop(nofuse=True)
                    dve.bn_aggr(out_, in_).then_inc(s, 1)

                def norm_scalars(layer, b):
                    m = mv[layer]
                    dve.wait_ge(std[layer], b + 1)
                    dve.reciprocal(m[:, 3:4], m[:, 2:3]).then_inc(ln[layer], 1)
                    dve.wait_ge(ln[layer], LN * b + 4)
                    dve.scalar_tensor_tensor(m[:, 4:5], m[:, 0:1], -1.0, m[:, 3:4], ALU.mult, ALU.mult)\
                       .then_inc(ln[layer], 1)

                def split(layer, b):
                    a = (a1, a2)[layer]
                    if layer == 0:
                        wait(dve, z_done[1], 2 * b)
                    else:
                        wait(dve, y_done, b)
                    for half in range(2):
                        ks = slice(4 * half, 4 * half + 4)
                        dve.wait_ge(relu_out[layer], 2 * b + half + 1)
                        dve.tensor_copy(a[:, 0, ks, :], aF[:, ks, :]).then_inc(split_high[layer], 1)
                        dve.wait_ge(split_high[layer], 2 * b + half + 1)
                        dve.tensor_tensor(a[:, 1, ks, :], aF[:, ks, :], a[:, 0, ks, :].bitcast(F32), ALU.subtract)\
                           .then_inc(a_ready[layer], 1)

                def step(b, n, ins):
                    ins.then_inc(fin, 1)
                    dve.wait_ge(fin, FIN * b + n)

                def finish1(b):
                    dve.wait_ge(y_done, b + 1)
                    dve.wait_ge(x1_in, 16 * (b + 1))
                    step(b, 1, dve.tensor_tensor(t[:, :], ps_y[:, 0:D], x1f[:, :], ALU.add))
                    step(b, 2, dve.bn_stats(fs[:, :], t[:, :]))
                    aggregate(fm[:, 0:2], fs[:, :], fin, FIN * b + 2)

                def finish2(b):
                    dve.wait_ge(fstd, 2 * b + 1)
                    step(b, 4, dve.reciprocal(fm[:, 6:7], fm[:, 2:3]))
                    step(b, 5, dve.tensor_scalar(v[:, :], t[:, :], fm[:, 0:1], fm[:, 6:7], ALU.subtract, ALU.mult))
                    step(b, 6, dve.tensor_tensor(v[:, :], v[:, :], bng[:, :], ALU.mult))
                    step(b, 7, dve.tensor_tensor(v[:, :], v[:, :], bnb[:, :], ALU.add))
                    step(b, 8, dve.scalar_tensor_tensor(v[:, :], v[:, :], 0.0, x1f[:, :], ALU.max, ALU.add))
                    step(b, 9, dve.bn_stats(fs[:, :], v[:, :]))
                    aggregate(fm[:, 4:6], fs[:, :], fin, FIN * b + 9)

                def finish3(b):
                    dve.wait_ge(fstd, 2 * b + 2)
                    step(b, 11, dve.reciprocal(fm[:, 7:8], fm[:, 3:4]))
                    wait(dve, out_stored, 16 * b)
                    dve.tensor_scalar(res[:, :], v[:, :], fm[:, 4:5], fm[:, 7:8], ALU.subtract, ALU.mult)\
                       .then_inc(fin, 1)

                def iteration(path, i):
                    if exists(i - 3):
                        finish1(i - 3)
                    if exists(i - 1):
                        stats(0, i - 1, 0)
                        stats(0, i - 1, 1)
                        aggregate(mv[0][:, 0:2], bs[0][:, :, :], ln[0], LN * (i - 1) + 2)
                        norm_scalars(0, i - 1)
                    if exists(i - 3):
                        finish2(i - 3)
                    if exists(i):
                        for group in range(len(OH_GROUPS)):
                            near_oh(path, i, group)
                    if exists(i - 2):
                        stats(1, i - 2, 0)
                    if exists(i - 3):
                        finish3(i - 3)
                    if exists(i - 1):
                        split(0, i - 1)
                    if exists(i - 2):
                        stats(1, i - 2, 1)
                        aggregate(mv[1][:, 0:2], bs[1][:, :, :], ln[1], LN * (i - 2) + 2)
                        norm_scalars(1, i - 2)
                        split(1, i - 2)
                    if exists(i):
                        take_h(i, SUMS * (i + 1))
                        h_low(i)

                def near_program(path):
                    for i in range(3):
                        iteration(path, i)
                    with dve.Fori(3, BLOCKS - 1) as i:
                        iteration(path, i)
                    for i in range(BLOCKS - 1, BLOCKS + 3):
                        iteration(path, i)

                def general_program():
                    dve.tensor_scalar(dst_f[:, :, :], dst_f[:, :, :], float(N), None, ALU.add).then_inc(rebased, 1)
                    dve.wait_ge(rebased, 1)
                    def general_block(b):
                        with dve.Fori(0, BLOCKS) as n:
                            q = b * BLOCKS + n
                            for k, (j0, m) in enumerate(PAIRS):
                                dve.wait_ge(sum_done, NP * q + k + 1)
                                equal(dve, oh2[:, j0:j0 + m, :], lane[:, P:2 * P], dst2[:, tile_cols(n, j0, m)], m)\
                                    .then_inc(oh2_ready, 1)
                        dve.wait_ge(oh2_ready, NP * BLOCKS * (b + 1))
                        dve.tensor_scalar(dst_f[:, :, :], dst_f[:, :, :], float(-P), None, ALU.add)\
                           .then_inc(rebased, 1)
                        dve.wait_ge(rebased, b + 2)
                        take_h(b, NP * BLOCKS * (b + 1) + NP)
                        h_low(b)
                        for layer in range(2):
                            stats(layer, b, 0)
                            stats(layer, b, 1)
                            aggregate(mv[layer][:, 0:2], bs[layer][:, :, :], ln[layer], LN * b + 2)
                            norm_scalars(layer, b)
                            split(layer, b)
                        finish1(b)
                        finish2(b)
                        finish3(b)

                    general_block(0)
                    with dve.Fori(1, BLOCKS) as b:
                        general_block(b)

                choose(dve, lvl, near_program, general_program)


def build_arrays(inputs):
    import numpy as np
    a = {k: np.asarray(v) for k, v in inputs.items()}

    def col(v):
        return np.ascontiguousarray(v.reshape(BLOCKS * TILES, P).T)

    def spread(v):
        return np.ascontiguousarray(np.broadcast_to(v.reshape(1, -1), (P, v.size)))

    def chunks(v):
        return np.ascontiguousarray(v.reshape(KH, 128).T)

    return {
        "x": a["x"],
        "xT": np.ascontiguousarray(a["x"].T.reshape(KD, 128, N).transpose(1, 0, 2)),
        "src": col(a["src"]), "dst": col(a["dst"]), "weight": col(a["edge_weight"]),
        "attrT": np.ascontiguousarray(a["edge_attr_64"].T),
        "w1T": np.ascontiguousarray(a["L0_gnn_W1"].T), "w2T": np.ascontiguousarray(a["L0_gnn_W2"].T),
        "bias01": spread(a["L0_gnn_b1"]), "bias02": spread(a["L0_gnn_b2"]),
        "eps_in": spread(a["L1_gnn_eps"]),
        "ee_w1": a["L1_gnn_ee_w1"], "ee_b1row": a["L1_gnn_ee_b1"].reshape(1, D), "ee_b1": spread(a["L1_gnn_ee_b1"]),
        "ee_w2": a["L1_gnn_ee_w2"], "ee_b2": spread(a["L1_gnn_ee_b2"]),
        "m_w1": a["L1_gnn_w1"], "m_b1": a["L1_gnn_b1"].reshape(1, H),
        "m_g1": chunks(a["L1_gnn_g1"]), "m_be1": chunks(a["L1_gnn_be1"]),
        "m_w2": a["L1_gnn_w2"], "m_b2": a["L1_gnn_b2"].reshape(1, H),
        "m_g2": chunks(a["L1_gnn_g2"]), "m_be2": chunks(a["L1_gnn_be2"]),
        "m_w3": a["L1_gnn_w3"], "m_b3": a["L1_gnn_b3"].reshape(1, D),
        "bn_g": spread(a["L1_gnn_bn_g"]), "bn_b": spread(a["L1_gnn_bn_b"]),
        "ident_in": np.eye(P, dtype=np.float32),
    }


def kernel(**inputs):
    import concourse.bacc as _bacc
    from concourse.bass_utils import run_bass_kernel_spmd as _run

    nc = _bacc.Bacc("TRN2", target_bir_lowering=False, num_devices=1)
    arrays, args = {}, []
    for name, a in build_arrays(inputs).items():
        arrays[f"in_{name}"] = a
        args.append(nc.dram_tensor(f"in_{name}", a.shape, mybir.dt.from_np(a.dtype), kind="ExternalInput").ap())
    args.append(nc.dram_tensor("out", (N, D), F32, kind="ExternalOutput").ap())
    gnn_program(nc, *args)
    return _run(nc, [arrays], core_ids=[0]).results[0]["out"]
```

```python
from contextlib import ExitStack

import concourse.bass as bass
from concourse import mybir

F32 = mybir.dt.float32
F32R = mybir.dt.float32r
I32 = mybir.dt.int32
ALU = mybir.AluOpType
ACT = mybir.ActivationFunctionType
AX_X = mybir.AxisListType.X

N, E, D, ED, H = 3125, 53125, 256, 64, 1024
P = 125
BLOCKS = N // P
TILES = E // P // BLOCKS
EDGES = [1, 4]
PAIRS = [(0, 2), (2, 2), (4, 2), (6, 2), (8, 2), (10, 2), (12, 2), (14, 2), (16, 1)]
NP = len(PAIRS)
LEAD = 3
CHUNKS = [(0, 6), (6, 6), (12, 5)]
KD = D // 128
KH = H // 128
ROWS, LOW = 33, 32
LN_EPS = 1e-5
NORM_EPS = 1e-12
SLOPE = 0.2
SUMS = 10

def wait(eng, sem, value):
    if isinstance(value, int) and value <= 0:
        return
    eng.wait_ge(sem, value)


class Near:

    skewed = True

    def __init__(self, edge):
        self.edge = edge
        self.steps = [(-1, TILES - edge, edge), (0, 0, 4)] + [(0, j, m) for j, m in PAIRS[2:]] + [(1, 0, edge)]
        self.slot = [0]
        for _, _, m in self.steps:
            self.slot.append(self.slot[-1] + m)

    def slot_free(self, q, k):
        if isinstance(q, int) and q == 0:
            return 0
        if k < 2:
            return SUMS * (q - 1) + 2
        if PAIRS[k][0] + PAIRS[k][1] <= TILES - self.edge:
            return SUMS * (q - 1) + k + 1
        return SUMS * q + 1


OH_SLOTS = TILES + 2 * EDGES[-1]
OH_GROUPS = [(0, 0), (1, 1), (2, 3), (4, 5), (6, 8), (9, 9)]


class General:

    skewed = False

    @staticmethod
    def slot_free(q, k):
        return NP * q + k + 1


def choose(eng, lvl, near_program, general_program):
    with eng.If(lvl > len(EDGES) - 1):
        near_program(Near(EDGES[0]))
    with eng.Else():
        with eng.If(lvl > 0):
            near_program(Near(EDGES[1]))
        with eng.Else():
            general_program()


def equal(dve, out_, lanes, which, m):
    return dve.tensor_tensor(out_, lanes.unsqueeze(1).to_broadcast([P, m, P]),
                             which.unsqueeze(2).to_broadcast([P, m, P]), ALU.is_equal)


def near_sum_steps(b):
    first = 1 if isinstance(b, int) and b == 0 else 0
    last = SUMS - 1 if isinstance(b, int) and b == BLOCKS - 1 else SUMS
    return [c for c in range(first, last)]


def exists(b):
    return not isinstance(b, int) or 0 <= b < BLOCKS


def near_inc(b, c):
    if isinstance(b, int) and b == 0 and c == 1:
        return 2
    if isinstance(b, int) and b == BLOCKS - 1 and c == SUMS - 2:
        return 2
    return 1


def gnn_program(nc, x, xT, src, dst, weight, attrT, w1T, w2T, bias01, bias02, eps_in, ee_w1, ee_b1row, ee_b1,
                ee_w2, ee_b2, m_w1, m_b1, m_g1, m_be1, m_w2, m_b2, m_g2, m_be2, m_w3, m_b3, bn_g, bn_b,
                ident_in, out):
    x1_dram = nc.dram_tensor("x1_dram", (N, D), F32).ap()
    hbase_dram = nc.dram_tensor("hbase_dram", (N, D), F32).ap()
    table_dram = nc.dram_tensor("table_dram", (N, 2 * D), F32).ap()

    with ExitStack() as keep:
        def sb(name, shape, dt, ctx=keep):
            return ctx.enter_context(nc.sbuf_tensor(name, shape, dt))

        def psum(name, shape, ctx):
            return ctx.enter_context(nc.psum_tensor(name, shape, F32))

        def sem(name, ctx=keep):
            return ctx.enter_context(nc.semaphore(name))

        dst_f = sb("dst_f", [P, BLOCKS, TILES], F32)
        rel = sb("rel", [P, BLOCKS, TILES], F32)
        lane = sb("lane", [P, 3 * P], F32)
        level = sb("level", [1, 1], I32)
        src_all = sb("src_all", [P, BLOCKS * TILES], I32)
        ident = sb("ident", [P, P], F32)

        w_in = sem("w_in")

        eps_t = sb("eps_t", [P, 1], F32)
        ln_eps = sb("ln_eps", [P, 1], F32)

        with ExitStack() as ca:
            def sa(name, shape, dt):
                return sb(name, shape, dt, ca)

            def ma(name):
                return sem(name, ca)

            weights_base = nc.sbuf_base
            w1_raw = sa("w1_raw", [128, KD, H], F32)
            w2_raw = sa("w2_raw", [128, KH, H], F32)
            w3_raw = sa("w3_raw", [128, KH, D], F32)
            dst_i = sa("dst_i", [P, BLOCKS, TILES], I32)
            w_sb = sa("w_sb", [P, BLOCKS * TILES], F32)
            idx = [sa(f"idx{c}", [P, m], I32) for c, (_, m) in enumerate(CHUNKS)]
            attr = sa("attr", [ED + 1, TILES * P], F32)
            raw = sa("raw", [P, TILES, D], F32)
            msg = sa("msg", [P, TILES, 2, 2 * D], F32R)
            oh = sa("oh", [P, OH_SLOTS, P], F32R)
            base = sa("base", [P, BLOCKS * TILES], F32)
            bad = sa("bad", [P, len(EDGES), BLOCKS, TILES], F32)
            bad_sum = sa("bad_sum", [P, len(EDGES)], F32)
            holds = sa("holds", [1, len(EDGES)], F32)
            ones_c = sa("ones_c", [P, 1], F32)
            zero_oh = sa("zero_oh", [P, P], F32)
            w1T_sb = sa("w1T_sb", [128, KD, D], F32)
            w2T_sb = sa("w2T_sb", [128, KD, D], F32)
            we1 = sa("we1", [ED + 1, D], F32)
            we2 = sa("we2", [128, KD, D], F32)
            b0_raw = sa("b0_raw", [ROWS, 2, D], F32)
            b0_sum = sa("b0_sum", [ROWS, D], F32)
            bias0 = sa("bias0", [ROWS, D], F32R)
            lane_ones = sa("lane_ones", [ROWS, P], F32)
            ones0 = sa("ones0", [ROWS, P], F32R)
            eb1 = sa("eb1", [P, D], F32)
            r0 = sa("r0", [P, D], F32)
            eb2 = sa("eb2", [P, D], F32)
            eps_raw = sa("eps_raw", [P, 1], F32)
            warm = sa("warm", [P, 1], F32)
            xs = sa("xs", [P, D], F32)
            xr = sa("xr", [P, D], F32)
            xTb = sa("xTb", [128, KD, P], F32)
            s_r = sa("s_r", [P, 2 * D], F32)
            sT = sa("sT", [128, 4 * P], F32)
            o = sa("o", [P, D], F32)
            ol = sa("ol", [P, D], F32)
            sq = sa("sq", [P, D], F32)
            st = sa("st", [P, 8], F32)
            bn6 = sa("bn6", [P, 6], F32)
            y = sa("y", [P, D], F32)
            x1 = sa("x1", [P, D], F32)
            tb = sa("tb", [P, D], F32)
            u = sa("u", [P, D], F32)
            table = sa("table", [P, 2, D], F32R)
            hb = sa("hb", [P, D], F32)

            ps_sum = [psum(f"ps_sum{n}", [P, 512], ca) for n in range(2)]
            ps_e = [psum(f"ps_e{n}", [P, 512], ca) for n in range(3)]
            ps_t = psum("ps_t", [128, 512], ca)
            ps_d = psum("ps_d", [P, 512], ca)
            ps_w = psum("ps_w", [P, 512], ca)

            consts = ma("consts")
            edges_in = ma("edges_in")
            src_in, weight_in, we1_in = ma("src_in"), ma("weight_in"), ma("we1_in")
            idx_ready = [ma(f"idx_ready{c}") for c in range(3)]
            attr_in = [ma(f"attr_in{c}") for c in range(3)]
            gathered = [ma(f"gathered{j}") for j in range(TILES)]
            xs_in, xr_in, xT_in = ma("xs_in"), ma("xr_in"), ma("xT_in")

            pool_ready = ma("pool_ready")
            prep = ma("prep")
            bad_ready, bad_total, level_ready = ma("bad_ready"), ma("bad_total"), ma("level_ready")
            rel_ready = ma("rel_ready")
            bias0_ready = ma("bias0_ready")
            edge_net = ma("edge_net")
            high = ma("high")
            message = ma("message")
            oh_ready = ma("oh_ready")
            summed = ma("summed")

            s_ready = ma("s_ready")
            s_turned = ma("s_turned")
            sT_ready = ma("sT_ready")
            dense = ma("dense")
            edge_dense = ma("edge_dense")
            dd = ma("dd")
            da = ma("da")
            stored = ma("stored")

            DD = 12
            DA = 5
            X_READ, HB_MADE = 4, 11

            N_CONST = 16 * 14

            def tile_cols(n, j, m=1):
                return bass.ds(n * TILES + j, m)

            def one(k):
                return bass.ds(k, 1)

            def piece(ap, k, m):
                return ap[bass.ds(k * m, m), :].rearrange("(k p) n -> p k n", p=128)

            def rows(ap, b):
                return ap[bass.ds(b * P, P), :]

            block = ca.enter_context(nc.Block())

            @block.sync
            def _(sp):
                def load_attr(n, c):
                    j, m = CHUNKS[c]
                    sp.nop(nofuse=True)
                    sp.dma_start(attr[0:ED, j * P:(j + m) * P],
                                 attrT[:, bass.ds((n * TILES + j) * P, m * P)]).then_inc(attr_in[c], 16)

                sp.dma_start(dst_i[:, :, :].rearrange("p b j -> p (b j)"), dst).then_inc(edges_in, 16)
                sp.dma_start(src_all[:, :], src).then_inc(src_in, 16)
                sp.dma_start(w_sb[:, :], weight).then_inc(weight_in, 16)
                sp.dma_start(we1[0:ED, :], ee_w1).then_inc(we1_in, 16)
                sp.dma_start(we1[ED:ED + 1, :], ee_b1row).then_inc(we1_in, 16)
                load_attr(0, 0)
                sp.dma_start(ident[:, :], ident_in).then_inc(consts, 16)
                for row in (0, LOW):
                    sp.dma_start(b0_raw[row:row + 1, 0, :], bias01).then_inc(consts, 16)
                    sp.dma_start(b0_raw[row:row + 1, 1, :], bias02).then_inc(consts, 16)
                sp.dma_start(eb1[:, :], ee_b1).then_inc(consts, 16)
                sp.dma_start(eb2[:, :], ee_b2).then_inc(consts, 16)
                sp.dma_start(eps_raw[:, :], eps_in).then_inc(consts, 16)
                for k in range(KD):
                    sp.dma_start(w1T_sb[:, k, :], w1T[k * 128:(k + 1) * 128, :]).then_inc(consts, 16)
                    sp.dma_start(w2T_sb[:, k, :], w2T[k * 128:(k + 1) * 128, :]).then_inc(consts, 16)
                    sp.dma_start(we2[:, k, :], ee_w2[k * 128:(k + 1) * 128, :]).then_inc(consts, 16)

                def load_w1(k):
                    sp.dma_start(w1_raw[:, one(k), :], piece(m_w1, k, 128)).then_inc(w_in, 16)

                def load_w2(k):
                    sp.dma_start(w2_raw[:, one(k), :], piece(m_w2, k, 128)).then_inc(w_in, 16)

                def load_w3(k):
                    sp.dma_start(w3_raw[:, bass.ds(k * KH // 2, KH // 2), :], piece(m_w3, k, H // 2))\
                      .then_inc(w_in, 16)

                def load_near_attr(q, c):
                    wait(sp, edge_net, NP * (q - 1) + 3 * c + 3)
                    load_attr(q, c)

                def load_xs(b):
                    wait(sp, s_ready, b)
                    sp.nop(nofuse=True)
                    sp.dma_start(xs[:, :], rows(x, b)).then_inc(xs_in, 16)

                def load_xT(b):
                    wait(sp, dense, b)
                    sp.nop(nofuse=True)
                    sp.dma_start(xTb[:, :, :], xT[:, :, bass.ds(b * P, P)]).then_inc(xT_in, 16)

                def load_xr(b):
                    wait(sp, dd, DD * (b - 1) + X_READ)
                    sp.nop(nofuse=True)
                    sp.dma_start(xr[:, :], rows(x, b)).then_inc(xr_in, 16)

                def store(b):
                    sp.wait_ge(dd, DD * (b + 1))
                    sp.nop(nofuse=True)
                    sp.dma_start(rows(x1_dram, b), x1[:, :]).then_inc(stored, 16)
                    sp.dma_start(rows(table_dram, b), table[:, :, :].rearrange("p a d -> p (a d)").bitcast(F32))\
                      .then_inc(stored, 16)
                    sp.dma_start(rows(hbase_dram, b), hb[:, :]).then_inc(stored, 16)

                for c in range(1, 3):
                    load_attr(0, c)
                sp.wait_ge(level_ready, 1)
                lvl = sp.value_load(level[0:1, 0:1])
                with sp.If(lvl > 0):
                    load_xs(0)
                    load_xT(0)
                    for c in range(3):
                        load_near_attr(1, c)

                    def near_block(b):
                        load_near_attr(b + 1, 0)
                        load_xs(b)
                        load_near_attr(b + 1, 1)
                        load_xr(b - 1)
                        load_near_attr(b + 1, 2)
                        load_xT(b)
                        if exists(b - 2):
                            store(b - 2)

                    for b in range(1, 3):
                        near_block(b)
                    with sp.Fori(3, 3 + KH) as b:
                        near_block(b)
                        load_w2(b - 3)
                    with sp.Fori(3 + KH, 3 + KH + KD) as b:
                        near_block(b)
                        load_w1(b - 3 - KH)
                    with sp.Fori(3 + KH + KD, 5 + KH + KD) as b:
                        near_block(b)
                        load_w3(b - 3 - KH - KD)
                    with sp.Fori(5 + KH + KD, BLOCKS - 1) as b:
                        near_block(b)
                    load_xs(BLOCKS - 1)
                    load_xr(BLOCKS - 2)
                    load_xT(BLOCKS - 1)
                    store(BLOCKS - 3)
                    load_xr(BLOCKS - 1)
                    store(BLOCKS - 2)
                    store(BLOCKS - 1)
                with sp.Else():
                    for c in range(3):
                        sp.wait_ge(attr_in[c], 16)
                    for k in range(KH):
                        load_w2(k)
                    for k in range(KD):
                        load_w1(k)
                    for k in range(2):
                        load_w3(k)

                    def general_block(b):
                        load_xs(b)
                        load_xT(b)
                        load_xr(b)
                        with sp.Fori(0, BLOCKS) as n:
                            for c in range(3):
                                sp.wait_ge(message, NP * (b * BLOCKS + n) + 3 * c + 3)
                                load_attr(n, c)
                        store(b)

                    general_block(0)
                    with sp.Fori(1, BLOCKS) as b:
                        general_block(b)
                sp.wait_ge(stored, 48 * BLOCKS)

            @block.gpsimd
            def _(pool):
                pool.iota(lane[:, :], [[1, 3 * P]], base=-P, channel_multiplier=0,
                          allow_small_or_imprecise_dtypes=True).then_inc(pool_ready, 1)
                pool.iota(base[:, :], [[P, BLOCKS], [0, TILES]], base=0, channel_multiplier=0,
                          allow_small_or_imprecise_dtypes=True).then_inc(pool_ready, 1)
                pool.wait_ge(pool_ready, 2)
                pool.memset(attr[ED:ED + 1, :], 1.0).then_inc(pool_ready, 1)
                pool.wait_ge(pool_ready, 3)
                pool.wait_ge(src_in, 16)

                def stage_idx(n, c):
                    j0, m = CHUNKS[c]
                    pool.tensor_copy(idx[c][:, :], src_all[:, tile_cols(n, j0, m)]).then_inc(idx_ready[c], 1)

                def stage_near_idx(q, c):
                    j0, m = CHUNKS[c]
                    for j in range(j0, j0 + m):
                        wait(pool, gathered[j], 16 * q)
                    stage_idx(q, c)

                def gather_chunk(q, c, start=0):
                    j0, m = CHUNKS[c]
                    pool.wait_ge(idx_ready[c], q + 1 + (1 if start else 0))
                    pool.nop(nofuse=True)
                    for j in range(j0, j0 + m):
                        if j % 2 == 0:
                            wait(pool, message, start + NP * (q - 1) + j // 2 + 1)
                            pool.nop(nofuse=True)
                        pool.indirect_dma_start(
                            out=raw[:, j, :], out_offset=None, in_=x,
                            in_offset=bass.IndirectOffsetOnAxis(ap=idx[c][:, j - j0:j - j0 + 1], axis=0),
                        ).then_inc(gathered[j], 16)

                for c in range(3):
                    stage_idx(0, c)
                for c in range(3):
                    gather_chunk(0, c)
                pool.wait_ge(level_ready, 1)
                lvl = pool.value_load(level[0:1, 0:1])

                def near_span(q):
                    last = isinstance(q, int) and q == BLOCKS - 1
                    gather_chunk(q, 0)
                    stage_near_idx(q, 2)
                    gather_chunk(q, 1)
                    if not last:
                        stage_near_idx(q + 1, 0)
                    gather_chunk(q, 2)
                    if not last:
                        stage_near_idx(q + 1, 1)

                with pool.If(lvl > 0):
                    stage_near_idx(1, 0)
                    stage_near_idx(1, 1)
                    with pool.Fori(1, BLOCKS - 1) as q:
                        near_span(q)
                    near_span(BLOCKS - 1)
                with pool.Else():
                    for j in range(TILES):
                        pool.wait_ge(gathered[j], 16)

                    def general_block(b):
                        with pool.Fori(0, BLOCKS) as n:
                            q = b * BLOCKS + n
                            for c in range(3):
                                pool.wait_ge(message, NP * q + 3 * c + 3)
                                stage_idx(n, c)
                                gather_chunk(q, c, NP)

                    general_block(0)
                    with pool.Fori(1, BLOCKS) as b:
                        general_block(b)

            @block.tensor
            def _(pe):
                pe.wait_ge(pool_ready, 3)
                pe.wait_ge(bad_ready, 1)
                pe.matmul(ps_d[0:1, 0:len(EDGES)], ones_c[:, :], bad_sum[:, :], start=True, stop=True)\
                  .then_inc(bad_total, 1)
                pe.wait_ge(level_ready, 1)
                lvl = pe.value_load(level[0:1, 0:1])
                pe.wait_ge(we1_in, 32)

                def edge_layer(q, k, start=0):
                    j0, m = PAIRS[k]
                    pe.wait_ge(attr_in[k // 3], 16 * (q + 1 + (1 if start else 0)))
                    wait(pe, message, start + NP * q + k - 2)
                    for j in range(j0, j0 + m):
                        mm = pe.matmul(ps_e[k % 3][:, (j - j0) * D:(j - j0 + 1) * D],
                                       attr[:, j * P:(j + 1) * P], we1[:, :], start=True, stop=True)
                    mm.then_inc(edge_net, 1)

                def add_tile(bank, j, slot, start, stop):
                    pe.matmul(ps_sum[bank][:, :], oh[:, slot, :], msg[:, j, 0, :], start=start, stop=False,
                              skip_group_check=True)
                    return pe.matmul(ps_sum[bank][:, :], oh[:, slot, :], msg[:, j, 1, :], start=False, stop=stop,
                                     skip_group_check=True)

                def near_step(path, b, c, bank):
                    _, j0, m = path.steps[c]
                    first, last = near_sum_steps(b)[0], near_sum_steps(b)[-1]
                    if c == first:
                        wait(pe, s_ready, b - 1)
                    pe.wait_ge(oh_ready, SUMS * b + c + 1)
                    if 2 <= c <= NP - 1:
                        pe.wait_ge(message, NP * b + c + 1)
                    elif c == 1 and first == 1:
                        pe.wait_ge(message, 2)
                    elif c == SUMS - 1:
                        pe.wait_ge(message, NP * (b + 1) + (path.edge + 1) // 2)
                    for j in range(j0, j0 + m):
                        mm = add_tile(bank, j, path.slot[c] + j - j0, c == first and j == j0,
                                      c == last and j == j0 + m - 1)
                    mm.then_inc(summed, near_inc(b, c))

                def turn(b):
                    pe.wait_ge(s_ready, b + 1)
                    wait(pe, sT_ready, b)
                    for n in range(4):
                        mm = pe.transpose(ps_t[:, n * P:(n + 1) * P], s_r[:, n * 128:(n + 1) * 128], ident[:, :])
                    mm.then_inc(s_turned, 1)

                def products(b, part):
                    k = part % KD
                    if part < KD:
                        if isinstance(b, int) and b == 0 and k == 0:
                            pe.wait_ge(consts, N_CONST)
                            pe.wait_ge(bias0_ready, 1)
                        if k == 0:
                            wait(pe, dd, DD * (b - 1) + 1)
                            pe.matmul(ps_d[:, 0:D], ones0[:, :], bias0[:, :], start=True, stop=False)
                            pe.wait_ge(xT_in, 16 * (b + 1))
                        pe.matmul(ps_d[:, 0:D], xTb[:, k, :], w1T_sb[:, k, :], start=False, stop=False)
                    elif part < 2 * KD:
                        if k == 0:
                            pe.wait_ge(sT_ready, b + 1)
                        mm = pe.matmul(ps_d[:, 0:D], sT[:, k * P:(k + 1) * P], w2T_sb[:, k, :], start=False,
                                       stop=(k == KD - 1))
                        if k == KD - 1:
                            mm.then_inc(dense, 1)
                    else:
                        if k == 0:
                            wait(pe, dd, DD * (b - 1) + HB_MADE)
                        mm = pe.matmul(ps_w[:, 0:D], sT[:, (KD + k) * P:(KD + k + 1) * P], we2[:, k, :],
                                       start=(k == 0), stop=(k == KD - 1))
                        if k == KD - 1:
                            mm.then_inc(edge_dense, 1)

                def near_block(path, b, bank):
                    for s in range(NP):
                        k = s + LEAD
                        if k < NP:
                            edge_layer(b, k)
                        elif exists(b + 1):
                            edge_layer(b + 1, k - NP)
                        if s in near_sum_steps(b):
                            near_step(path, b, s, bank)
                        if exists(b - 2) and s == 0:
                            products(b - 2, 2 * KD)
                            products(b - 2, 2 * KD + 1)
                        if exists(b - 1) and 3 <= s <= 6:
                            products(b - 1, s - 3)
                        if exists(b - 1) and s == 3:
                            turn(b - 1)
                    if SUMS - 1 in near_sum_steps(b):
                        near_step(path, b, SUMS - 1, bank)

                def near_program(path):
                    for k in range(LEAD):
                        edge_layer(0, k)
                    for b in range(4):
                        near_block(path, b, b % 2)
                    with pe.Fori(4, BLOCKS - 2, 2) as b:
                        near_block(path, b, 0)
                        near_block(path, b + 1, 1)
                    near_block(path, BLOCKS - 1, (BLOCKS - 1) % 2)
                    for part in range(2 * KD, 3 * KD):
                        products(BLOCKS - 2, part)
                    turn(BLOCKS - 1)
                    for part in range(3 * KD):
                        products(BLOCKS - 1, part)

                def general_program():
                    pe.wait_ge(consts, N_CONST)
                    pe.wait_ge(prep, 3)
                    pe.matmul(ps_sum[0][:, 0:D], zero_oh[:, :], eb1[:, :], start=True, stop=True,
                              skip_group_check=True).then_inc(summed, NP)

                    def general_block(b):
                        wait(pe, s_ready, b)
                        pe.matmul(ps_sum[0][:, 0:D], zero_oh[:, :], eb1[:, :], start=True, stop=False,
                                  skip_group_check=True)
                        pe.matmul(ps_sum[0][:, D:2 * D], zero_oh[:, :], eb1[:, :], start=False, stop=False,
                                  skip_group_check=True)
                        with pe.Fori(0, BLOCKS) as n:
                            q = b * BLOCKS + n
                            for k, (j0, m) in enumerate(PAIRS):
                                edge_layer(q, k, NP)
                                pe.wait_ge(oh_ready, NP * q + k + 1)
                                pe.wait_ge(message, NP * (q + 1) + k + 1)
                                for j in range(j0, j0 + m):
                                    mm = add_tile(0, j, j, False, False)
                                mm.then_inc(summed, 1)
                        turn(b)
                        for part in range(3 * KD):
                            products(b, part)

                    general_block(0)
                    with pe.Fori(1, BLOCKS) as b:
                        general_block(b)

                choose(pe, lvl, near_program, general_program)

            @block.scalar
            def _(act):
                act.wait_ge(prep, 2)
                act.activation(warm[:, :], ln_eps[:, :], ACT.Sqrt)
                act.wait_ge(weight_in, 16)
                act.wait_ge(level_ready, 1)
                lvl = act.value_load(level[0:1, 0:1])

                def highs(path, q, n, k):
                    j0, m = PAIRS[k]
                    wait(act, summed, path.slot_free(q, k))
                    for j in range(j0, j0 + m):
                        act.wait_ge(gathered[j], 16 * (q + (2 if path is General else 1)))
                        act.activation(msg[:, j, 0, 0:D], raw[:, j, :], ACT.Copy,
                                       scale=w_sb[:, tile_cols(n, j)])
                    act.wait_ge(edge_net, NP * q + k + 1)
                    act.activation(msg[:, j0:j0 + m, 0, D:2 * D],
                                   ps_e[k % 3][:, 0:m * D].rearrange("p (j d) -> p j d", d=D),
                                   ACT.Relu).then_inc(high, 1)

                def turned(b):
                    act.wait_ge(s_turned, b + 1)
                    wait(act, edge_dense, b)
                    act.activation(sT[:, :], ps_t[:, 0:4 * P], ACT.Copy).then_inc(sT_ready, 1)

                def leak(b):
                    act.wait_ge(dense, b + 1)
                    wait(act, dd, DD * (b - 1) + 1)
                    act.activation(ol[:, :], ps_d[:, 0:D], ACT.Copy, scale=SLOPE).then_inc(da, 1)

                def norm(b):
                    act.wait_ge(dd, DD * b + 1)
                    act.activation(sq[:, :], o[:, :], ACT.Square, accum_out=st[:, 0:1]).then_inc(da, 1)
                    act.wait_ge(da, DA * b + 2)
                    act.activation(st[:, 1:2], st[:, 0:1], ACT.Sqrt).then_inc(da, 1)

                def deviation(b):
                    act.wait_ge(dd, DD * b + 6)
                    act.activation(st[:, 5:6], st[:, 4:5], ACT.Sqrt, bias=ln_eps[:, :]).then_inc(da, 1)

                def table_high(b):
                    act.wait_ge(dd, DD * b + 9)
                    act.activation(table[:, 0, :], tb[:, :], ACT.Copy).then_inc(da, 1)

                def near_block(path, b):
                    for s in range(NP):
                        k = s + LEAD
                        if k < NP:
                            highs(path, b, b, k)
                        elif exists(b + 1):
                            highs(path, b + 1, b + 1, k - NP)
                        if exists(b - 2) and s == 0:
                            norm(b - 2)
                        if exists(b - 1) and s == 3:
                            turned(b - 1)
                        if exists(b - 2) and s == 4:
                            deviation(b - 2)
                        if exists(b - 2) and s == 6:
                            table_high(b - 2)
                        if exists(b - 1) and s == 7:
                            leak(b - 1)

                def near_program(path):
                    for k in range(LEAD):
                        highs(path, 0, 0, k)
                    for b in range(3):
                        near_block(path, b)
                    with act.Fori(3, BLOCKS - 1) as b:
                        near_block(path, b)
                    near_block(path, BLOCKS - 1)
                    turned(BLOCKS - 1)
                    norm(BLOCKS - 2)
                    deviation(BLOCKS - 2)
                    table_high(BLOCKS - 2)
                    leak(BLOCKS - 1)
                    norm(BLOCKS - 1)
                    deviation(BLOCKS - 1)
                    table_high(BLOCKS - 1)

                def general_program():
                    def general_block(b):
                        with act.Fori(0, BLOCKS) as n:
                            for k in range(NP):
                                highs(General, b * BLOCKS + n, n, k)
                        turned(b)
                        leak(b)
                        norm(b)
                        deviation(b)
                        table_high(b)

                    general_block(0)
                    with act.Fori(1, BLOCKS) as b:
                        general_block(b)

                choose(act, lvl, near_program, general_program)

            @block.vector
            def _(dve):
                dve.memset(ones_c[:, :], 1.0).then_inc(prep, 1)
                dve.memset(ln_eps[:, :], LN_EPS).then_inc(prep, 1)
                dve.memset(zero_oh[:, :], 0.0).then_inc(prep, 1)
                dve.wait_ge(edges_in, 16)
                dve.tensor_copy(dst_f[:, :, :], dst_i[:, :, :]).then_inc(prep, 1)
                dve.wait_ge(prep, 4)
                dve.wait_ge(pool_ready, 2)
                dve.tensor_tensor(rel[:, :, :].rearrange("p b j -> p (b j)"),
                                  dst_f[:, :, :].rearrange("p b j -> p (b j)"), base[:, :], ALU.subtract)\
                   .then_inc(prep, 1)
                dve.wait_ge(prep, 5)
                for n, edge in enumerate(EDGES):
                    lim = TILES - edge
                    dve.tensor_scalar(bad[:, n, :, 0:edge], rel[:, :, 0:edge], float(-P), None, ALU.is_lt)
                    dve.tensor_scalar(bad[:, n, :, edge:TILES], rel[:, :, edge:TILES], 0.0, None, ALU.is_lt)\
                       .then_inc(prep, 1)
                    dve.wait_ge(prep, 6 + 2 * n)
                    dve.scalar_tensor_tensor(bad[:, n, :, 0:lim], rel[:, :, 0:lim], float(P), bad[:, n, :, 0:lim],
                                             ALU.is_ge, ALU.add)
                    dve.scalar_tensor_tensor(bad[:, n, :, lim:TILES], rel[:, :, lim:TILES], float(2 * P),
                                             bad[:, n, :, lim:TILES], ALU.is_ge, ALU.add).then_inc(prep, 1)
                    dve.wait_ge(prep, 7 + 2 * n)
                dve.reduce_sum(bad_sum[:, :], bad[:, :, :, :].rearrange("p n b j -> p n (b j)"), AX_X)\
                   .then_inc(bad_ready, 1)
                n_prep = 5 + 2 * len(EDGES)
                dve.wait_ge(bad_total, 1)
                dve.tensor_scalar(holds[:, :], ps_d[0:1, 0:len(EDGES)], 0.0, None, ALU.is_equal).then_inc(prep, 1)
                dve.wait_ge(prep, n_prep + 1)
                dve.tensor_tensor(level[:, :], holds[:, 0:1], holds[:, 1:2], ALU.add).then_inc(level_ready, 1)
                dve.wait_ge(pool_ready, 3)
                dve.wait_ge(level_ready, 1)
                dve.wait_ge(weight_in, 16)
                lvl = dve.value_load(level[0:1, 0:1])

                def constants():
                    dve.wait_ge(consts, N_CONST)
                    dve.tensor_scalar(r0[:, :], eb1[:, :], 0.0, None, ALU.max).then_inc(prep, 1)
                    dve.memset(bias0[:, :].bitcast(F32), 0.0).then_inc(prep, 1)
                    dve.memset(lane_ones[:, :], 1.0).then_inc(prep, 1)
                    for row in (0, LOW):
                        dve.tensor_tensor(b0_sum[row:row + 1, :], b0_raw[row:row + 1, 0, :], b0_raw[row:row + 1, 1, :],
                                          ALU.add).then_inc(prep, 1)
                    dve.wait_ge(prep, n_prep + 6)
                    dve.tensor_copy(ones0[:, :], lane_ones[:, :]).then_inc(prep, 1)
                    for row in (0, LOW):
                        dve.tensor_copy(bias0[row:row + 1, :], b0_sum[row:row + 1, :]).then_inc(prep, 1)
                    dve.wait_ge(prep, n_prep + 9)
                    dve.tensor_tensor(bias0[LOW:ROWS, :], b0_sum[LOW:ROWS, :], bias0[LOW:ROWS, :].bitcast(F32),
                                      ALU.subtract).then_inc(bias0_ready, 1)
                    dve.tensor_scalar(eps_t[:, :], eps_raw[:, :], 1.0, None, ALU.add).then_inc(prep, 1)
                    dve.wait_ge(prep, n_prep + 10)

                def near_oh(path, b, group):
                    steps = [c for c in range(OH_GROUPS[group][0], OH_GROUPS[group][1] + 1) if c in near_sum_steps(b)]
                    if not steps:
                        return
                    wait(dve, summed, SUMS * (b - 1) + steps[-1] + 1)
                    span, j0, _ = path.steps[steps[0]]
                    m = sum(path.steps[c][2] for c in steps)
                    equal(dve, oh[:, path.slot[steps[0]]:path.slot[steps[0]] + m, :],
                          lane[:, (1 - span) * P:(2 - span) * P], rel2[:, tile_cols(b + span, j0, m)], m)\
                        .then_inc(oh_ready, sum(near_inc(b, c) for c in steps))

                rel2 = rel[:, :, :].rearrange("p b j -> p (b j)")
                dst2 = dst_f[:, :, :].rearrange("p b j -> p (b j)")

                def low_neighbour(n, j):
                    dve.scalar_tensor_tensor(msg[:, j, 1, 0:D], raw[:, j, :], w_sb[:, tile_cols(n, j)],
                                             msg[:, j, 0, 0:D].bitcast(F32), ALU.mult, ALU.subtract)

                def low_edge(k):
                    j0, m = PAIRS[k]
                    dve.scalar_tensor_tensor(msg[:, j0:j0 + m, 1, D:2 * D],
                                             ps_e[k % 3][:, 0:m * D].rearrange("p (j d) -> p j d", d=D), 0.0,
                                             msg[:, j0:j0 + m, 0, D:2 * D].bitcast(F32), ALU.max, ALU.subtract)\
                       .then_inc(message, 1)

                def take_s(b, steps, bank):
                    dve.wait_ge(summed, steps)
                    dve.wait_ge(xs_in, 16 * (b + 1))
                    wait(dve, s_turned, b)
                    dve.scalar_tensor_tensor(s_r[:, 0:D], xs[:, :], 1.0, ps_sum[bank][:, 0:D], ALU.add, ALU.mult)
                    dve.tensor_tensor(s_r[:, D:2 * D], ps_sum[bank][:, D:2 * D], r0[:, :], ALU.add).then_inc(s_ready, 1)

                def tail(b, n):
                    at = DD * b
                    if n == 1:
                        dve.wait_ge(dense, b + 1)
                        dve.wait_ge(da, DA * b + 1)
                        ins = dve.tensor_tensor(o[:, :], ps_d[:, 0:D], ol[:, :], ALU.max)
                    elif n == 2:
                        dve.wait_ge(da, DA * b + 3)
                        ins = dve.tensor_scalar(st[:, 2:3], st[:, 1:2], NORM_EPS, None, ALU.max)
                    elif n == 3:
                        dve.wait_ge(dd, at + 2)
                        ins = dve.reciprocal(st[:, 3:4], st[:, 2:3])
                    elif n == X_READ:
                        dve.wait_ge(dd, at + 3)
                        dve.wait_ge(xr_in, 16 * (b + 1))
                        ins = dve.scalar_tensor_tensor(y[:, :], o[:, :], st[:, 3:4], xr[:, :], ALU.mult, ALU.add)
                    elif n == 5:
                        dve.wait_ge(dd, at + 4)
                        ins = dve.bn_stats(bn6[:, :], y[:, :])
                    elif n == 6:
                        dve.wait_ge(dd, at + 5)
                        dve.nop(nofuse=True)
                        ins = dve.bn_aggr(st[:, 3:5], bn6[:, :])
                    elif n == 7:
                        dve.wait_ge(da, DA * b + 4)
                        ins = dve.reciprocal(st[:, 6:7], st[:, 5:6])
                    elif n == 8:
                        dve.wait_ge(dd, at + 7)
                        wait(dve, stored, 48 * b)
                        ins = dve.tensor_scalar(x1[:, :], y[:, :], st[:, 3:4], st[:, 6:7], ALU.subtract, ALU.mult)
                    elif n == 9:
                        dve.wait_ge(dd, at + 8)
                        ins = dve.tensor_tensor(tb[:, :], x1[:, :], eb2[:, :], ALU.add)
                    elif n == 10:
                        dve.wait_ge(dd, at + 9)
                        ins = dve.scalar_tensor_tensor(u[:, :], x1[:, :], eps_t[:, :], tb[:, :], ALU.mult, ALU.add)
                    elif n == HB_MADE:
                        dve.wait_ge(dd, at + 10)
                        dve.wait_ge(edge_dense, b + 1)
                        ins = dve.tensor_tensor(hb[:, :], ps_w[:, 0:D], u[:, :], ALU.add)
                    else:
                        dve.wait_ge(da, DA * (b + 1))
                        ins = dve.tensor_tensor(table[:, 1, :], tb[:, :], table[:, 0, :].bitcast(F32), ALU.subtract)
                    ins.then_inc(dd, 1)

                TAIL_1 = {(8, 0): 1}
                TAIL_2 = {(1, 1): 2, (1, 2): 3, (3, 0): 4, (3, 1): 5, (3, 2): 6, (4, 2): 7, (5, 0): 8, (5, 2): 9,
                          (6, 0): 10, (6, 1): 11, (7, 1): 12}
                OH_THIS = {2: 3, 4: 4, 5: 5}
                OH_NEXT = {6: 0, 7: 1, 8: 2}

                def near_block(path, b, bank):
                    def fill(s, place):
                        if exists(b - 1) and (s, place) in TAIL_1:
                            tail(b - 1, TAIL_1[s, place])
                        if exists(b - 2) and (s, place) in TAIL_2:
                            tail(b - 2, TAIL_2[s, place])

                    for s in range(NP):
                        if s in OH_THIS:
                            near_oh(path, b, OH_THIS[s])
                        q, k = (b, s + LEAD) if s + LEAD < NP else (b + 1, s + LEAD - NP)
                        j0, m = PAIRS[k]
                        if exists(q):
                            dve.wait_ge(high, NP * q + k + 1)
                            low_neighbour(q, j0)
                        fill(s, 0)
                        if exists(q) and m == 2:
                            low_neighbour(q, j0 + 1)
                        fill(s, 1)
                        if exists(q):
                            low_edge(k)
                        fill(s, 2)
                        if s == 1 and exists(b - 1):
                            take_s(b - 1, SUMS * b, 1 - bank)
                        if s in OH_NEXT and exists(b + 1):
                            near_oh(path, b + 1, OH_NEXT[s])

                def near_program(path):
                    for k in range(LEAD):
                        dve.wait_ge(high, k + 1)
                        for j in range(PAIRS[k][0], PAIRS[k][0] + PAIRS[k][1]):
                            low_neighbour(0, j)
                        low_edge(k)
                    near_oh(path, 0, 1)
                    near_oh(path, 0, 2)
                    near_block(path, 0, 0)
                    constants()
                    for b in range(1, 4):
                        near_block(path, b, b % 2)
                    with dve.Fori(4, BLOCKS - 2, 2) as b:
                        near_block(path, b, 0)
                        near_block(path, b + 1, 1)
                    last = BLOCKS - 1
                    near_block(path, last, last % 2)
                    take_s(last, SUMS * BLOCKS, last % 2)
                    for n in range(2, DD + 1):
                        tail(last - 1, n)
                    for n in range(1, DD + 1):
                        tail(last, n)

                def general_program():
                    constants()
                    dve.memset(bad[0:1, 0:1, 0:1, 0:1], 0.0).then_inc(message, NP)

                    def general_block(b):
                        with dve.Fori(0, BLOCKS) as n:
                            q = b * BLOCKS + n
                            for k, (j0, m) in enumerate(PAIRS):
                                dve.wait_ge(summed, NP * q + k + 1)
                                equal(dve, oh[:, j0:j0 + m, :], lane[:, P:2 * P], dst2[:, tile_cols(n, j0, m)], m)\
                                    .then_inc(oh_ready, 1)
                                dve.wait_ge(high, NP * q + k + 1)
                                for j in range(j0, j0 + m):
                                    low_neighbour(n, j)
                                low_edge(k)
                        dve.wait_ge(oh_ready, NP * BLOCKS * (b + 1))
                        dve.tensor_scalar(dst_f[:, :, :], dst_f[:, :, :], float(-P), None, ALU.add)\
                           .then_inc(rel_ready, 1)
                        dve.wait_ge(rel_ready, b + 1)
                        take_s(b, NP * BLOCKS * (b + 1) + NP, 0)
                        for n in range(1, DD + 1):
                            tail(b, n)

                    general_block(0)
                    with dve.Fori(1, BLOCKS) as b:
                        general_block(b)

                choose(dve, lvl, near_program, general_program)

        with ExitStack() as cb:
            def s2(name, shape, dt):
                return sb(name, shape, dt, cb)

            def m2(name):
                return sem(name, cb)

            assert nc.sbuf_base == weights_base
            w1_low = s2("w1_low", [128, KD, H], F32R)
            w2_low = s2("w2_low", [128, KH, H], F32R)
            w3_low = s2("w3_low", [128, KH, D], F32R)
            w1_high = s2("w1_high", [128, KD, H], F32R)
            w2_high = s2("w2_high", [128, KH, H], F32R)
            w3_high = s2("w3_high", [128, KH, D], F32R)
            bias = s2("bias", [ROWS, 2 * H + D], F32R)
            bias_raw = s2("bias_raw", [ROWS, 2 * H + D], F32)
            ones_f = s2("ones_f", [ROWS, P], F32)
            ones_r = s2("ones_r", [ROWS, P], F32R)
            g1, be1 = s2("g1", [128, KH], F32), s2("be1", [128, KH], F32)
            g2, be2 = s2("g2", [128, KH], F32), s2("be2", [128, KH], F32)
            bng, bnb = s2("bng", [P, D], F32), s2("bnb", [P, D], F32)
            idx2 = [s2(f"idx2_{c}", [P, m], I32) for c, (_, m) in enumerate(CHUNKS)]
            grow = s2("grow", [P, TILES, 2 * D], F32R)
            oh2 = s2("oh2", [P, OH_SLOTS, P], F32R)
            zero2 = s2("zero2", [P, P], F32)
            zrow = s2("zrow", [P, D], F32)
            hbx = s2("hbx", [P, D], F32)
            x1f = s2("x1f", [P, D], F32)
            h = s2("h", [P, D], F32)
            hT = s2("hT", [128, 2, KD * P], F32R)
            zn = s2("zn", [P, H], F32)
            aF = s2("aF", [128, KH, P], F32)
            a1 = s2("a1", [128, 2, KH, P], F32R)
            a2 = s2("a2", [128, 2, KH, P], F32R)
            bs = [s2(f"bs{n}", [P, 2, 6], F32) for n in range(2)]
            mv = [s2(f"mv{n}", [P, 8], F32) for n in range(2)]
            fs = s2("fs", [P, 6], F32)
            fm = s2("fm", [P, 8], F32)
            t = s2("t", [P, D], F32)
            v = s2("v", [P, D], F32)
            res = s2("res", [P, D], F32)

            ps_s = psum("ps_s", [P, 512], cb)
            ps_z = [psum(f"ps_z{n}", [P, 2, 512], cb) for n in range(2)]
            ps_tr = psum("ps_tr", [128, 2, 512], cb)
            ps_y = psum("ps_y", [P, 512], cb)

            consts2 = m2("consts2")
            bias_in = m2("bias_in")
            w_high, w_ready = m2("w_high"), m2("w_ready")
            prep2, prep_ones = m2("prep2"), m2("prep_ones")
            rebased = m2("rebased")
            split_high = [m2(f"split_high{n}") for n in range(2)]
            idx2_ready = [m2(f"idx2_ready{c}") for c in range(3)]
            got = [m2(f"got{j}") for j in range(TILES)]
            hb_in, x1_in = m2("hb_in"), m2("x1_in")
            oh2_ready = m2("oh2_ready")
            sum_done = m2("sum_done")
            h_ready = m2("h_ready")
            h_turned = m2("h_turned")
            hT_high, hT_ready = m2("hT_high"), m2("hT_ready")
            z_done = [m2(f"z_done{n}") for n in range(2)]
            ln = [m2(f"ln{n}") for n in range(2)]
            std = [m2(f"std{n}") for n in range(2)]
            zn_ready = [[m2(f"zn_ready{n}_{half}") for half in range(2)] for n in range(2)]
            turned2 = [m2(f"turned2_{n}") for n in range(2)]
            relu_out = [m2(f"relu_out{n}") for n in range(2)]
            a_ready = [m2(f"a_ready{n}") for n in range(2)]
            y_done = m2("y_done")
            fin = m2("fin")
            fstd = m2("fstd")
            out_stored = m2("out_stored")
            SPLIT_SUM = 2
            LN = 5
            FIN = 12
            X1_READ = 8

            pieces = [(w1_raw[:, k, :], w1_high[:, k, :], w1_low[:, k, :]) for k in range(KD)]
            pieces += [(w2_raw[:, k, :], w2_high[:, k, :], w2_low[:, k, :]) for k in range(KH)]
            pieces += [tuple(w[:, k:k + KH // 2, :] for w in (w3_raw, w3_high, w3_low)) for k in (0, KH // 2)]
            N_SPLIT = len(pieces) + 1

            block2 = cb.enter_context(nc.Block())

            @block2.sync
            def _(sp):
                lvl = sp.value_load(level[0:1, 0:1])

                def load_hb(b):
                    wait(sp, h_ready, b)
                    sp.nop(nofuse=True)
                    sp.dma_start(hbx[:, :], rows(hbase_dram, b)).then_inc(hb_in, 16)

                def load_x1(b):
                    wait(sp, fin, FIN * (b - 1) + X1_READ)
                    sp.nop(nofuse=True)
                    sp.dma_start(x1f[:, :], rows(x1_dram, b)).then_inc(x1_in, 16)

                def store(b):
                    sp.wait_ge(fin, FIN * (b + 1))
                    sp.nop(nofuse=True)
                    sp.dma_start(rows(out, b), res[:, :]).then_inc(out_stored, 16)

                for row in (0, LOW):
                    for source, at, width in ((m_b1, 0, H), (m_b2, H, H), (m_b3, 2 * H, D)):
                        sp.dma_start(bias_raw[row:row + 1, at:at + width], source).then_inc(bias_in, 16)
                for tile, source in ((g1, m_g1), (be1, m_be1), (g2, m_g2), (be2, m_be2), (bng, bn_g), (bnb, bn_b)):
                    sp.dma_start(tile[:, :], source).then_inc(consts2, 16)

                def iteration(i):
                    if exists(i + 1):
                        load_hb(i + 1)
                    if exists(i - 1):
                        load_x1(i - 1)
                    if exists(i - 2):
                        store(i - 2)

                with sp.If(lvl > 0):
                    for i in range(-1, 3):
                        iteration(i)
                    with sp.Fori(3, BLOCKS - 1) as i:
                        iteration(i)
                    for i in range(BLOCKS - 1, BLOCKS + 2):
                        iteration(i)
                with sp.Else():
                    def general_block(b):
                        load_hb(b)
                        load_x1(b)
                        store(b)

                    general_block(0)
                    with sp.Fori(1, BLOCKS) as b:
                        general_block(b)
                sp.wait_ge(out_stored, 16 * BLOCKS)

            @block2.gpsimd
            def _(pool):
                lvl = pool.value_load(level[0:1, 0:1])

                def stage_idx(n, c):
                    j0, m = CHUNKS[c]
                    pool.tensor_copy(idx2[c][:, :], src_all[:, tile_cols(n, j0, m)]).then_inc(idx2_ready[c], 1)

                def stage_near_idx(q, c):
                    j0, m = CHUNKS[c]
                    for j in range(j0, j0 + m):
                        wait(pool, got[j], 16 * q)
                    stage_idx(q, c)

                def gather_chunk(path, q, c):
                    j0, m = CHUNKS[c]
                    pool.wait_ge(idx2_ready[c], q + 1)
                    pool.nop(nofuse=True)
                    for j in range(j0, j0 + m):
                        if j % 2 == 0:
                            wait(pool, sum_done, path.slot_free(q, j // 2))
                            pool.nop(nofuse=True)
                        pool.indirect_dma_start(
                            out=grow[:, j, :].bitcast(F32), out_offset=None, in_=table_dram,
                            in_offset=bass.IndirectOffsetOnAxis(ap=idx2[c][:, j - j0:j - j0 + 1], axis=0),
                        ).then_inc(got[j], 16)

                def near_span(path, q):
                    last = isinstance(q, int) and q == BLOCKS - 1
                    gather_chunk(path, q, 0)
                    stage_near_idx(q, 2)
                    gather_chunk(path, q, 1)
                    if not last:
                        stage_near_idx(q + 1, 0)
                    gather_chunk(path, q, 2)
                    if not last:
                        stage_near_idx(q + 1, 1)

                def near_program(path):
                    stage_near_idx(0, 0)
                    stage_near_idx(0, 1)
                    near_span(path, 0)
                    with pool.Fori(1, BLOCKS - 1) as q:
                        near_span(path, q)
                    near_span(path, BLOCKS - 1)

                def general_program():
                    def general_block(b):
                        with pool.Fori(0, BLOCKS) as n:
                            q = b * BLOCKS + n
                            for c in range(3):
                                pool.wait_ge(sum_done, General.slot_free(q, (CHUNKS[c][0] + CHUNKS[c][1] - 1) // 2))
                                stage_idx(n, c)
                                gather_chunk(General, q, c)

                    general_block(0)
                    with pool.Fori(1, BLOCKS) as b:
                        general_block(b)

                choose(pool, lvl, near_program, general_program)

            @block2.tensor
            def _(pe):
                lvl = pe.value_load(level[0:1, 0:1])
                pe.wait_ge(prep2, 3)

                def add_tile(j, slot, start, stop):
                    pe.matmul(ps_s[:, 0:D], oh2[:, slot, :], grow[:, j, 0:D], start=start, stop=False,
                              skip_group_check=True)
                    return pe.matmul(ps_s[:, 0:D], oh2[:, slot, :], grow[:, j, D:2 * D], start=False, stop=stop,
                                     skip_group_check=True)

                def near_step(path, b, c):
                    span, j0, m = path.steps[c]
                    first, last = near_sum_steps(b)[0], near_sum_steps(b)[-1]
                    if c == first:
                        wait(pe, h_ready, b)
                    pe.wait_ge(oh2_ready, SUMS * b + c + 1)
                    for j in range(j0, j0 + m):
                        pe.wait_ge(got[j], 16 * (b + span + 1))
                        mm = add_tile(j, path.slot[c] + j - j0, c == first and j == j0,
                                      c == last and j == j0 + m - 1)
                    mm.then_inc(sum_done, near_inc(b, c))

                def turn_h(path, b):
                    pe.wait_ge(h_ready, b + 1)
                    wait(pe, relu_out[0 if path.skewed else 1], 2 * b)
                    for k in range(KD):
                        mm = pe.transpose(ps_tr[:, 0, k * P:(k + 1) * P], h[:, k * 128:(k + 1) * 128], ident[:, :])
                    mm.then_inc(h_turned, 1)

                def three(acc, left, right, stop):
                    for a, b in ((0, 0), (0, 1), (1, 0)):
                        mm = pe.matmul(acc, left[a], right[b], start=False, stop=stop and a == 1,
                                       skip_group_check=True)
                    return mm

                def open_bank(acc, at, width):
                    pe.matmul(acc, ones_r[:, :], bias[:, at:at + width], start=True, stop=False,
                              skip_group_check=True)

                def layer1(b, n):
                    if n == 0:
                        pe.wait_ge(hT_ready, b + 1)
                    wait(pe, zn_ready[0][n], b)
                    cols = slice(n * 512, (n + 1) * 512)
                    open_bank(ps_z[0][:, n, :], n * 512, 512)
                    for k in range(KD):
                        mm = three(ps_z[0][:, n, :], [hT[:, a, k * P:(k + 1) * P] for a in range(2)],
                                   [w[:, k, cols] for w in (w1_high, w1_low)], k == KD - 1)
                    mm.then_inc(z_done[0], 1)

                def layer2(b, n):
                    wait(pe, zn_ready[1][n], b)
                    cols = slice(n * 512, (n + 1) * 512)
                    open_bank(ps_z[1][:, n, :], H + n * 512, 512)
                    for k in range(KH):
                        if n == 0 and k % 4 == 0:
                            pe.wait_ge(a_ready[0], 2 * b + k // 4 + 1)
                        mm = three(ps_z[1][:, n, :], [a1[:, a, k, :] for a in range(2)],
                                   [w[:, k, cols] for w in (w2_high, w2_low)], k == KH - 1)
                    mm.then_inc(z_done[1], 1)

                def layer3(b, half):
                    if half == 0:
                        wait(pe, fin, FIN * (b - 1) + 1)
                        open_bank(ps_y[:, 0:D], 2 * H, D)
                    pe.wait_ge(a_ready[1], 2 * b + half + 1)
                    for k in range(half * KH // 2, (half + 1) * KH // 2):
                        mm = three(ps_y[:, 0:D], [a2[:, a, k, :] for a in range(2)],
                                   [w[:, k, :] for w in (w3_high, w3_low)], k == KH - 1)
                    if half == 1:
                        mm.then_inc(y_done, 1)

                def turn_z(path, layer, b, half):
                    if layer == 0:
                        pe.wait_ge(hT_ready, b + 1)
                        wait(pe, relu_out[1], 2 * (b - 1) + half + 1)
                    else:
                        pe.wait_ge(relu_out[0], 2 * b + half + 1)
                        if path.skewed and exists(b + 1):
                            pe.wait_ge(hT_ready, b + 2)
                    pe.wait_ge(zn_ready[layer][half], b + 1)
                    for c in range(4):
                        k = 4 * half + c
                        mm = pe.transpose(ps_tr[:, half, c * P:(c + 1) * P], zn[:, k * 128:(k + 1) * 128],
                                          ident[:, :])
                    mm.then_inc(turned2[layer], 1)

                def starts(i):
                    return isinstance(i, int) and i == 0

                def iteration(path, i):
                    steps = near_sum_steps(i + 1) if exists(i + 1) else []
                    if exists(i - 1):
                        layer2(i - 1, 0)
                    if exists(i):
                        turn_h(path, i)
                    if exists(i - 1):
                        layer2(i - 1, 1)
                    for c in steps:
                        if c < SPLIT_SUM and not starts(i):
                            near_step(path, i + 1, c)
                    if exists(i):
                        layer1(i, 0)
                    if exists(i - 1):
                        turn_z(path, 1, i - 1, 0)
                        turn_z(path, 1, i - 1, 1)
                    if exists(i):
                        layer1(i, 1)
                    for c in steps:
                        if c >= SPLIT_SUM and not starts(i):
                            near_step(path, i + 1, c)
                    if exists(i):
                        turn_z(path, 0, i, 0)
                        turn_z(path, 0, i, 1)
                    if starts(i):
                        for c in steps:
                            near_step(path, i + 1, c)
                    if exists(i - 1):
                        layer3(i - 1, 0)
                        layer3(i - 1, 1)

                def near_program(path):
                    iteration(path, -1)
                    pe.wait_ge(w_ready, N_SPLIT)
                    for i in range(3):
                        iteration(path, i)
                    with pe.Fori(3, BLOCKS - 2) as i:
                        iteration(path, i)
                    for i in range(BLOCKS - 2, BLOCKS + 1):
                        iteration(path, i)

                def general_program():
                    pe.wait_ge(w_ready, N_SPLIT)
                    pe.matmul(ps_s[:, 0:D], zero2[:, :], zrow[:, :], start=True, stop=True,
                              skip_group_check=True).then_inc(sum_done, NP)
                    def general_block(b):
                        wait(pe, h_ready, b)
                        pe.matmul(ps_s[:, 0:D], zero2[:, :], zrow[:, :], start=True, stop=False,
                                  skip_group_check=True)
                        with pe.Fori(0, BLOCKS) as n:
                            q = b * BLOCKS + n
                            for k, (j0, m) in enumerate(PAIRS):
                                pe.wait_ge(oh2_ready, NP * q + k + 1)
                                for j in range(j0, j0 + m):
                                    pe.wait_ge(got[j], 16 * (q + 1))
                                    mm = add_tile(j, j, False, False)
                                mm.then_inc(sum_done, 1)
                        turn_h(General, b)
                        layer1(b, 0)
                        layer1(b, 1)
                        turn_z(General, 0, b, 0)
                        turn_z(General, 0, b, 1)
                        layer2(b, 0)
                        layer2(b, 1)
                        turn_z(General, 1, b, 0)
                        turn_z(General, 1, b, 1)
                        layer3(b, 0)
                        layer3(b, 1)

                    general_block(0)
                    with pe.Fori(1, BLOCKS) as b:
                        general_block(b)

                choose(pe, lvl, near_program, general_program)

            @block2.scalar
            def _(act):
                lvl = act.value_load(level[0:1, 0:1])
                act.wait_ge(w_in, 16 * (KD + KH + 2))
                for whole, high_part, _ in pieces:
                    act.activation(high_part, whole, ACT.Copy).then_inc(w_high, 1)
                act.wait_ge(prep2, 4)
                act.wait_ge(bias_in, 96)
                act.activation(bias[0:1, :], bias_raw[0:1, :], ACT.Copy)
                act.activation(bias[LOW:LOW + 1, :], bias_raw[LOW:LOW + 1, :], ACT.Copy).then_inc(w_high, 1)
                act.wait_ge(consts2, 96)

                def h_high(b):
                    act.wait_ge(h_turned, b + 1)
                    wait(act, z_done[0], 2 * b)
                    act.activation(hT[:, 0, :], ps_tr[:, 0, 0:KD * P], ACT.Copy).then_inc(hT_high, 1)

                def deviation(layer, b):
                    act.wait_ge(ln[layer], LN * b + 3)
                    act.activation(mv[layer][:, 2:3], mv[layer][:, 1:2], ACT.Sqrt, bias=ln_eps[:, :])\
                       .then_inc(std[layer], 1)

                def normalize(layer, b):
                    act.wait_ge(ln[layer], LN * (b + 1))
                    if layer == 0:
                        wait(act, turned2[1], 2 * b)
                    else:
                        act.wait_ge(turned2[0], 2 * (b + 1))
                    act.activation(zn[:, 0:512], ps_z[layer][:, 0, :], ACT.Identity,
                                   bias=mv[layer][:, 4:5], scale=mv[layer][:, 3:4]).then_inc(zn_ready[layer][0], 1)

                def relu(layer, b, half):
                    gg, bb = ((g1, be1), (g2, be2))[layer]
                    if half == 0:
                        if layer == 0:
                            wait(act, a_ready[1], 2 * b)
                        else:
                            act.wait_ge(a_ready[0], 2 * (b + 1))
                    act.wait_ge(turned2[layer], 2 * b + half + 1)
                    for c in range(4):
                        k = 4 * half + c
                        ins = act.activation(aF[:, k, :], ps_tr[:, half, c * P:(c + 1) * P], ACT.Relu,
                                             bias=bb[:, k:k + 1], scale=gg[:, k:k + 1])
                    ins.then_inc(relu_out[layer], 1)

                def finish_std(b, n):
                    act.wait_ge(fin, FIN * b + (3, 10)[n])
                    act.activation(fm[:, 2 + n:3 + n], fm[:, 1:2] if n == 0 else fm[:, 5:6], ACT.Sqrt,
                                   bias=ln_eps[:, :]).then_inc(fstd, 1)

                def iteration(i):
                    if exists(i - 2):
                        finish_std(i - 2, 0)
                        finish_std(i - 2, 1)
                    if exists(i):
                        h_high(i)
                    if exists(i - 1):
                        deviation(1, i - 1)
                        normalize(1, i - 1)
                        relu(1, i - 1, 0)
                        relu(1, i - 1, 1)
                    if exists(i):
                        deviation(0, i)
                        normalize(0, i)
                        relu(0, i, 0)
                        relu(0, i, 1)

                def near_program(path):
                    for i in range(3):
                        iteration(i)
                    with act.Fori(3, BLOCKS - 2) as i:
                        iteration(i)
                    for i in range(BLOCKS - 2, BLOCKS + 2):
                        iteration(i)

                def general_program():
                    def general_block(b):
                        h_high(b)
                        for layer in range(2):
                            deviation(layer, b)
                            normalize(layer, b)
                            relu(layer, b, 0)
                            relu(layer, b, 1)
                        finish_std(b, 0)
                        finish_std(b, 1)

                    general_block(0)
                    with act.Fori(1, BLOCKS) as b:
                        general_block(b)

                choose(act, lvl, near_program, general_program)

            @block2.vector
            def _(dve):
                dve.memset(zero2[:, :], 0.0).then_inc(prep2, 1)
                dve.memset(zrow[:, :], 0.0).then_inc(prep2, 1)
                dve.memset(ones_f[:, :], 1.0).then_inc(prep_ones, 1)
                dve.wait_ge(prep_ones, 1)
                dve.tensor_copy(ones_r[:, :], ones_f[:, :]).then_inc(prep2, 1)
                dve.memset(bias[:, :].bitcast(F32), 0.0).then_inc(prep2, 1)
                lvl = dve.value_load(level[0:1, 0:1])
                def split_weights():
                    for n, (whole, high_part, low_part) in enumerate(pieces):
                        dve.wait_ge(w_high, n + 1)
                        dve.tensor_tensor(low_part, whole, high_part.bitcast(F32), ALU.subtract).then_inc(w_ready, 1)
                    dve.wait_ge(w_high, N_SPLIT)
                    dve.tensor_tensor(bias[LOW:ROWS, :], bias_raw[LOW:ROWS, :], bias[LOW:ROWS, :].bitcast(F32),
                                      ALU.subtract).then_inc(w_ready, 1)
                    dve.wait_ge(consts2, 96)

                rel2 = rel[:, :, :].rearrange("p b j -> p (b j)")
                dst2 = dst_f[:, :, :].rearrange("p b j -> p (b j)")

                def near_oh(path, b, group):
                    steps = [c for c in range(OH_GROUPS[group][0], OH_GROUPS[group][1] + 1) if c in near_sum_steps(b)]
                    if not steps:
                        return
                    wait(dve, sum_done, SUMS * (b - 1) + steps[-1] + 1)
                    span, j0, _ = path.steps[steps[0]]
                    m = sum(path.steps[c][2] for c in steps)
                    equal(dve, oh2[:, path.slot[steps[0]]:path.slot[steps[0]] + m, :],
                          lane[:, (1 - span) * P:(2 - span) * P], rel2[:, tile_cols(b + span, j0, m)], m)\
                        .then_inc(oh2_ready, sum(near_inc(b, c) for c in steps))

                def take_h(b, steps):
                    dve.wait_ge(sum_done, steps)
                    dve.wait_ge(hb_in, 16 * (b + 1))
                    wait(dve, h_turned, b)
                    dve.tensor_tensor(h[:, :], ps_s[:, 0:D], hbx[:, :], ALU.add).then_inc(h_ready, 1)

                def h_low(b):
                    dve.wait_ge(hT_high, b + 1)
                    dve.tensor_tensor(hT[:, 1, :], ps_tr[:, 0, 0:KD * P], hT[:, 0, :].bitcast(F32), ALU.subtract)\
                       .then_inc(hT_ready, 1)

                def stats(layer, b, n):
                    dve.wait_ge(z_done[layer], 2 * b + n + 1)
                    dve.bn_stats(bs[layer][:, n, :], ps_z[layer][:, n, :]).then_inc(ln[layer], 1)

                def aggregate(out_, in_, s, value):
                    dve.wait_ge(s, value)
                    dve.nop(nofuse=True)
                    dve.bn_aggr(out_, in_).then_inc(s, 1)

                def norm_scalars(layer, b):
                    m = mv[layer]
                    dve.wait_ge(std[layer], b + 1)
                    dve.reciprocal(m[:, 3:4], m[:, 2:3]).then_inc(ln[layer], 1)
                    dve.wait_ge(ln[layer], LN * b + 4)
                    dve.scalar_tensor_tensor(m[:, 4:5], m[:, 0:1], -1.0, m[:, 3:4], ALU.mult, ALU.mult)\
                       .then_inc(ln[layer], 1)

                def normalize(layer, b):
                    if layer == 0:
                        wait(dve, turned2[1], 2 * b)
                    else:
                        dve.wait_ge(turned2[0], 2 * (b + 1))
                    m = mv[layer]
                    dve.tensor_scalar(zn[:, 512:H], ps_z[layer][:, 1, :], m[:, 0:1], m[:, 3:4], ALU.subtract,
                                      ALU.mult).then_inc(zn_ready[layer][1], 1)

                def split(layer, b, half):
                    a = (a1, a2)[layer]
                    if layer == 0:
                        wait(dve, z_done[1], 2 * b)
                    else:
                        wait(dve, y_done, b)
                    ks = slice(4 * half, 4 * half + 4)
                    dve.wait_ge(relu_out[layer], 2 * b + half + 1)
                    dve.tensor_copy(a[:, 0, ks, :], aF[:, ks, :]).then_inc(split_high[layer], 1)
                    dve.wait_ge(split_high[layer], 2 * b + half + 1)
                    dve.tensor_tensor(a[:, 1, ks, :], aF[:, ks, :], a[:, 0, ks, :].bitcast(F32), ALU.subtract)\
                       .then_inc(a_ready[layer], 1)

                def step(b, n, ins):
                    ins.then_inc(fin, 1)
                    dve.wait_ge(fin, FIN * b + n)

                def finish1(b):
                    dve.wait_ge(y_done, b + 1)
                    dve.wait_ge(x1_in, 16 * (b + 1))
                    step(b, 1, dve.tensor_tensor(t[:, :], ps_y[:, 0:D], x1f[:, :], ALU.add))
                    step(b, 2, dve.bn_stats(fs[:, :], t[:, :]))
                    aggregate(fm[:, 0:2], fs[:, :], fin, FIN * b + 2)

                def finish2(b):
                    dve.wait_ge(fstd, 2 * b + 1)
                    step(b, 4, dve.reciprocal(fm[:, 6:7], fm[:, 2:3]))
                    step(b, 5, dve.tensor_scalar(v[:, :], t[:, :], fm[:, 0:1], fm[:, 6:7], ALU.subtract, ALU.mult))
                    step(b, 6, dve.tensor_tensor(v[:, :], v[:, :], bng[:, :], ALU.mult))
                    step(b, 7, dve.tensor_tensor(v[:, :], v[:, :], bnb[:, :], ALU.add))
                    step(b, 8, dve.scalar_tensor_tensor(v[:, :], v[:, :], 0.0, x1f[:, :], ALU.max, ALU.add))
                    step(b, 9, dve.bn_stats(fs[:, :], v[:, :]))
                    aggregate(fm[:, 4:6], fs[:, :], fin, FIN * b + 9)

                def finish3(b):
                    dve.wait_ge(fstd, 2 * b + 2)
                    step(b, 11, dve.reciprocal(fm[:, 7:8], fm[:, 3:4]))
                    wait(dve, out_stored, 16 * b)
                    dve.tensor_scalar(res[:, :], v[:, :], fm[:, 4:5], fm[:, 7:8], ALU.subtract, ALU.mult)\
                       .then_inc(fin, 1)

                def starts(i):
                    return isinstance(i, int) and i == 0

                def iteration(path, i):
                    if exists(i - 2):
                        finish1(i - 2)
                    if starts(i):
                        h_low(i)
                    if exists(i + 1) and exists(i):
                        for group in range(len(OH_GROUPS)):
                            near_oh(path, i + 1, group)
                    if exists(i - 2):
                        finish2(i - 2)
                    if exists(i) and not starts(i):
                        h_low(i)
                    if exists(i - 1):
                        stats(1, i - 1, 0)
                    if exists(i - 2):
                        finish3(i - 2)
                    if exists(i - 1):
                        stats(1, i - 1, 1)
                        aggregate(mv[1][:, 0:2], bs[1][:, :, :], ln[1], LN * (i - 1) + 2)
                        norm_scalars(1, i - 1)
                        normalize(1, i - 1)
                    if exists(i):
                        stats(0, i, 0)
                    if exists(i - 1):
                        split(1, i - 1, 0)
                    if exists(i):
                        stats(0, i, 1)
                        aggregate(mv[0][:, 0:2], bs[0][:, :, :], ln[0], LN * i + 2)
                        norm_scalars(0, i)
                        normalize(0, i)
                    if exists(i - 1):
                        split(1, i - 1, 1)
                    if exists(i + 1) and not starts(i):
                        take_h(i + 1, SUMS * (i + 2))
                    if exists(i):
                        split(0, i, 0)
                        split(0, i, 1)
                    if starts(i):
                        take_h(i + 1, SUMS * (i + 2))

                def near_program(path):
                    for group in range(len(OH_GROUPS)):
                        near_oh(path, 0, group)
                    split_weights()
                    for i in range(-1, 3):
                        iteration(path, i)
                    with dve.Fori(3, BLOCKS - 2) as i:
                        iteration(path, i)
                    for i in range(BLOCKS - 2, BLOCKS + 2):
                        iteration(path, i)

                def general_program():
                    split_weights()
                    dve.tensor_scalar(dst_f[:, :, :], dst_f[:, :, :], float(N), None, ALU.add).then_inc(rebased, 1)
                    dve.wait_ge(rebased, 1)
                    def general_block(b):
                        with dve.Fori(0, BLOCKS) as n:
                            q = b * BLOCKS + n
                            for k, (j0, m) in enumerate(PAIRS):
                                dve.wait_ge(sum_done, NP * q + k + 1)
                                equal(dve, oh2[:, j0:j0 + m, :], lane[:, P:2 * P], dst2[:, tile_cols(n, j0, m)], m)\
                                    .then_inc(oh2_ready, 1)
                        dve.wait_ge(oh2_ready, NP * BLOCKS * (b + 1))
                        dve.tensor_scalar(dst_f[:, :, :], dst_f[:, :, :], float(-P), None, ALU.add)\
                           .then_inc(rebased, 1)
                        dve.wait_ge(rebased, b + 2)
                        take_h(b, NP * BLOCKS * (b + 1) + NP)
                        h_low(b)
                        for layer in range(2):
                            stats(layer, b, 0)
                            stats(layer, b, 1)
                            aggregate(mv[layer][:, 0:2], bs[layer][:, :, :], ln[layer], LN * b + 2)
                            norm_scalars(layer, b)
                            normalize(layer, b)
                            split(layer, b, 0)
                            split(layer, b, 1)
                        finish1(b)
                        finish2(b)
                        finish3(b)

                    general_block(0)
                    with dve.Fori(1, BLOCKS) as b:
                        general_block(b)

                choose(dve, lvl, near_program, general_program)


def build_arrays(inputs):
    import numpy as np
    a = {k: np.asarray(v) for k, v in inputs.items()}

    def col(v):
        return np.ascontiguousarray(v.reshape(BLOCKS * TILES, P).T)

    def spread(v):
        return np.ascontiguousarray(np.broadcast_to(v.reshape(1, -1), (P, v.size)))

    def chunks(v):
        return np.ascontiguousarray(v.reshape(KH, 128).T)

    return {
        "x": a["x"],
        "xT": np.ascontiguousarray(a["x"].T.reshape(KD, 128, N).transpose(1, 0, 2)),
        "src": col(a["src"]), "dst": col(a["dst"]), "weight": col(a["edge_weight"]),
        "attrT": np.ascontiguousarray(a["edge_attr_64"].T),
        "w1T": np.ascontiguousarray(a["L0_gnn_W1"].T), "w2T": np.ascontiguousarray(a["L0_gnn_W2"].T),
        "bias01": a["L0_gnn_b1"].reshape(1, D), "bias02": a["L0_gnn_b2"].reshape(1, D),
        "eps_in": spread(a["L1_gnn_eps"]),
        "ee_w1": a["L1_gnn_ee_w1"], "ee_b1row": a["L1_gnn_ee_b1"].reshape(1, D), "ee_b1": spread(a["L1_gnn_ee_b1"]),
        "ee_w2": a["L1_gnn_ee_w2"], "ee_b2": spread(a["L1_gnn_ee_b2"]),
        "m_w1": a["L1_gnn_w1"], "m_b1": a["L1_gnn_b1"].reshape(1, H),
        "m_g1": chunks(a["L1_gnn_g1"]), "m_be1": chunks(a["L1_gnn_be1"]),
        "m_w2": a["L1_gnn_w2"], "m_b2": a["L1_gnn_b2"].reshape(1, H),
        "m_g2": chunks(a["L1_gnn_g2"]), "m_be2": chunks(a["L1_gnn_be2"]),
        "m_w3": a["L1_gnn_w3"], "m_b3": a["L1_gnn_b3"].reshape(1, D),
        "bn_g": spread(a["L1_gnn_bn_g"]), "bn_b": spread(a["L1_gnn_bn_b"]),
        "ident_in": np.eye(P, dtype=np.float32),
    }


def kernel(**inputs):
    import concourse.bacc as _bacc
    from concourse.bass_utils import run_bass_kernel_spmd as _run

    nc = _bacc.Bacc("TRN2", target_bir_lowering=False, num_devices=1)
    arrays, args = {}, []
    for name, a in build_arrays(inputs).items():
        arrays[f"in_{name}"] = a
        args.append(nc.dram_tensor(f"in_{name}", a.shape, mybir.dt.from_np(a.dtype), kind="ExternalInput").ap())
    args.append(nc.dram_tensor("out", (N, D), F32, kind="ExternalOutput").ap())
    gnn_program(nc, *args)
    return _run(nc, [arrays], core_ids=[0]).results[0]["out"]
```
